# Optimizing a Trainium2 kernel written in Bass

```python
import numpy as np
import jax
import jax.numpy as jnp

def _softmax(x, axis=-1):
    return jax.nn.softmax(x, axis=axis)

def _gelu(x):
    return jax.nn.gelu(x, approximate=True)

def _silu(x):
    return jax.nn.silu(x)

def _sigmoid(x):
    return jax.nn.sigmoid(x)

def _layernorm(x, axis=-1, eps=1e-05):
    m = jnp.mean(x, axis=axis, keepdims=True)
    v = jnp.var(x, axis=axis, keepdims=True)
    return (x - m) / jnp.sqrt(v + eps)

def _scatter_add(tgt, idx, src, axis=0):
    return tgt.at[idx].add(src)

def _segment_sum(src, seg, n):
    return jax.ops.segment_sum(src, seg, n)
kernel_name = 'mk_flamingo_gated_d4_seqx_r8_4993b7'

def setup_inputs(seed: int=0):
    np.random.seed(seed)
    _w = jnp.asarray

    def _rec_inputs():
        import jax
        import jax.numpy as jnp
        _rk = jax.random.key(seed)
        x = -0.000125 + 0.9999 * jax.random.normal(jax.random.fold_in(_rk, 1), (8, 128, 256), jnp.float32)
        _lenS = 128 - jax.random.randint(jax.random.fold_in(_rk, 7), (8,), 0, max(1, 128 // 4) + 1, jnp.int32)
        _lenS2 = 128 - jax.random.randint(jax.random.fold_in(_rk, 8), (8,), 0, max(1, 128 // 4) + 1, jnp.int32)
        _ctx_2048P = jax.random.normal(jax.random.fold_in(_rk, 11), (8, 16, 256), jnp.float32)
        _ctx_2048c = jax.random.dirichlet(jax.random.fold_in(_rk, 511), 0.3 * jnp.ones((16,), jnp.float32), (8, 128))
        _ctx_2048t = jnp.einsum('bsk,bkd->bsd', _ctx_2048c, _ctx_2048P)
        _ctx_2048t = _ctx_2048t * jax.lax.rsqrt(jnp.mean(jnp.square(_ctx_2048t)) + 1e-12) * 0.953939
        ctx_2048 = -1.52775e-05 + 0.999936 * (_ctx_2048t + 0.3 * jax.random.normal(jax.random.fold_in(_rk, 611), (8, 128, 256), jnp.float32))
        _validS = jnp.arange(128)[None, :] < _lenS[:, None]
        _validS2 = jnp.arange(128)[None, :] < _lenS2[:, None]
        _causal = jnp.tril(jnp.ones((128, 128), dtype=bool))
        mask_BxS2_bk0 = jnp.logical_not(jnp.broadcast_to(_validS2[:, :], (8, 128)))
        _g = jax.random.normal(jax.random.fold_in(_rk, 9001), (2, 4), jnp.float32)
        _g = jnp.sign(_g) * jnp.maximum(jnp.abs(_g), 1.0) + (_g == 0) * 1.0
        g_xattn = _g[0]
        g_ffn = _g[1]
        return (x, ctx_2048, mask_BxS2_bk0, g_xattn, g_ffn)
    x, ctx_2048, mask_BxS2_bk0, g_xattn, g_ffn = _rec_inputs()

    def _L0_xattn_setup():
        import jax, jax.numpy as jnp
        import numpy as np
        EPS = 1e-06
        NUM_HEADS = 16

        def _feature_map(x):
            return jnp.where(x > 0, x + 1.0, jnp.exp(x))
        key = jax.random.key(seed)
        ks = jax.random.split(key, 7)
        B, L, S, D = (4, 512, 512, 256)
        sc = 1.0 / np.sqrt(D)
        return {'query': jax.random.normal(ks[0], (B, L, D), jnp.float32), 'kv': jax.random.normal(ks[1], (B, S, D), jnp.float32), 'Wq': jax.random.normal(ks[2], (D, D), jnp.float32) * sc, 'Wg': jax.random.normal(ks[3], (D, D), jnp.float32) * sc, 'bg': jnp.ones((D,), jnp.float32), 'Wkv': jax.random.normal(ks[4], (2 * D, D), jnp.float32) * sc, 'Wo': jax.random.normal(ks[5], (D, D), jnp.float32) * sc}
    _L0_xattn_all = _L0_xattn_setup()
    _L0_xattn_in = {k: v for k, v in _L0_xattn_all.items() if k in ('Wq', 'Wg', 'bg', 'Wkv', 'Wo')}
    del _L0_xattn_all

    def _L0_ffn_setup():
        import jax, jax.numpy as jnp
        import numpy as np
        D = 256
        E = 8
        R = 16
        K = 2
        INIT_BONUS = 3.0
        ANNEAL_STEPS = 625
        CURRENT_STEP = 1
        key = jax.random.key(seed)
        ks = jax.random.split(key, 7)
        s_in = 1.0 / np.sqrt(D)
        s_r = 1.0 / np.sqrt(R)
        return {'x': jax.random.normal(ks[0], (2, 512, D), dtype=jnp.float32), 'Wr': jax.random.normal(ks[1], (D, E), dtype=jnp.float32) * s_in, 'br': jax.random.normal(ks[2], (E,), dtype=jnp.float32) * 0.01, 'Wd': jax.random.normal(ks[3], (E, D, R), dtype=jnp.float32) * s_in, 'bd': jnp.zeros((E, R), dtype=jnp.float32), 'Wu': jax.random.normal(ks[4], (E, R, D), dtype=jnp.float32) * s_r, 'bu': jnp.zeros((E, D), dtype=jnp.float32)}
    _L0_ffn_all = _L0_ffn_setup()
    _L0_ffn_in = {k: v for k, v in _L0_ffn_all.items() if k in ('Wr', 'br', 'Wd', 'bd', 'Wu', 'bu')}
    del _L0_ffn_all

    def _L1_xattn_setup():
        import jax, jax.numpy as jnp
        import numpy as np
        N_HEAD = 8
        key = jax.random.key(seed)
        k1, k2, k3 = jax.random.split(key, 3)
        B, D, L = (4, 128, 256)
        q = jax.random.normal(k1, (B, D, L), dtype=jnp.float32)
        k = jax.random.normal(k2, (B, D, L), dtype=jnp.float32)
        v = jax.random.normal(k3, (B, D, L), dtype=jnp.float32)
        gamma = jnp.ones((), dtype=jnp.float32)
        return {'q': q, 'k': k, 'v': v, 'gamma': gamma}
    _L1_xattn_all = _L1_xattn_setup()
    _L1_xattn_in = {k: v for k, v in _L1_xattn_all.items() if k in ('gamma',)}
    del _L1_xattn_all

    def _L1_ffn_setup():
        import jax, jax.numpy as jnp
        import numpy as np
        D_MODEL, D_FF, NS, NR, KR = (256, 176, 2, 16, 4)
        B, S = (4, 256)

        def _moe_forward(u, shared_w1, shared_b1, shared_w2, shared_b2, routed_w1, routed_b1, routed_w2, routed_b2, centroids, bias):
            b, s, d = u.shape
            flat = u.reshape(-1, d)
            T = flat.shape[0]
            h = jax.nn.relu(jnp.einsum('td,ndf->ntf', flat, shared_w1) + shared_b1[:, None, :])
            shared_out = jnp.einsum('ntf,nfd->td', h, shared_w2) + shared_b2.sum(0)
            out = flat + shared_out
            scores = jax.nn.sigmoid(flat @ centroids.T) + bias
            vals, idx = jax.lax.top_k(scores, KR)
            gating = jnp.zeros_like(scores).at[jnp.arange(T)[:, None], idx].set(vals)
            gating = gating / jnp.clip(gating.sum(-1, keepdims=True), 1e-08)

            def step(acc, ew):
                w1, b1, w2, b2, g = ew
                hj = jax.nn.relu(flat @ w1 + b1)
                yj = hj @ w2 + b2
                return (acc + yj * g[:, None], None)
            rout0 = jnp.zeros_like(flat)
            rout, _ = jax.lax.scan(step, rout0, (routed_w1, routed_b1, routed_w2, routed_b2, gating.T))
            return (out + rout).reshape(b, s, d)
        key = jax.random.key(seed)
        ks = jax.random.split(key, 10)
        s1 = 1.0 / np.sqrt(D_MODEL)
        s2 = 1.0 / np.sqrt(D_FF)
        return {'u': jax.random.normal(ks[0], (B, S, D_MODEL), dtype=jnp.float32), 'shared_w1': jax.random.normal(ks[1], (NS, D_MODEL, D_FF), dtype=jnp.float32) * s1, 'shared_b1': jnp.zeros((NS, D_FF), dtype=jnp.float32), 'shared_w2': jax.random.normal(ks[2], (NS, D_FF, D_MODEL), dtype=jnp.float32) * s2, 'shared_b2': jnp.zeros((NS, D_MODEL), dtype=jnp.float32), 'routed_w1': jax.random.normal(ks[3], (NR, D_MODEL, D_FF), dtype=jnp.float32) * s1, 'routed_b1': jnp.zeros((NR, D_FF), dtype=jnp.float32), 'routed_w2': jax.random.normal(ks[4], (NR, D_FF, D_MODEL), dtype=jnp.float32) * s2, 'routed_b2': jnp.zeros((NR, D_MODEL), dtype=jnp.float32), 'centroids': jax.random.normal(ks[5], (NR, D_MODEL), dtype=jnp.float32) * s1, 'bias': jnp.zeros((NR,), dtype=jnp.float32)}
    _L1_ffn_all = _L1_ffn_setup()
    _L1_ffn_in = {k: v for k, v in _L1_ffn_all.items() if k in ('shared_w1', 'shared_b1', 'shared_w2', 'shared_b2', 'routed_w1', 'routed_b1', 'routed_w2', 'routed_b2', 'centroids', 'bias')}
    del _L1_ffn_all

    def _L2_xattn_setup():
        import jax, jax.numpy as jnp
        import numpy as np
        key = jax.random.key(seed)
        k1, k2, k3 = jax.random.split(key, 3)
        B, S, D, M = (8, 256, 256, 128)
        hidden_states = jax.random.normal(k1, (B, S, D), dtype=jnp.float32)
        memory_tokens = jax.random.normal(k2, (B, M, D), dtype=jnp.float32)
        memory_mask = jax.random.randint(k3, (B, M), 0, 2).astype(jnp.bool_)
        return {'hidden_states': hidden_states, 'memory_tokens': memory_tokens, 'memory_mask': memory_mask}
    _L2_xattn_all = _L2_xattn_setup()
    _L2_xattn_in = {k: v for k, v in _L2_xattn_all.items() if k in ()}
    del _L2_xattn_all

    def _L2_ffn_setup():
        import jax, jax.numpy as jnp
        import numpy as np
        HIDDEN = 256
        INTER = 704
        B, S = (2, 256)

        def _ternary(key, shape):
            return jax.random.randint(key, shape, -1, 2).astype(jnp.float32)
        key = jax.random.key(seed)
        ks = jax.random.split(key, 7)
        x = jax.random.normal(ks[0], (B, S, HIDDEN), dtype=jnp.float32)
        gate_w = _ternary(ks[1], (INTER, HIDDEN))
        up_w = _ternary(ks[2], (INTER, HIDDEN))
        down_w = _ternary(ks[3], (HIDDEN, INTER))
        gate_s = jax.random.uniform(ks[4], (INTER,), minval=0.01, maxval=0.1, dtype=jnp.float32)
        up_s = jax.random.uniform(ks[5], (INTER,), minval=0.01, maxval=0.1, dtype=jnp.float32)
        down_s = jax.random.uniform(ks[6], (HIDDEN,), minval=0.01, maxval=0.1, dtype=jnp.float32)
        return {'x': x, 'gate_w': gate_w, 'up_w': up_w, 'down_w': down_w, 'gate_s': gate_s, 'up_s': up_s, 'down_s': down_s}
    _L2_ffn_all = _L2_ffn_setup()
    _L2_ffn_in = {k: v for k, v in _L2_ffn_all.items() if k in ('gate_w', 'up_w', 'down_w', 'gate_s', 'up_s', 'down_s')}
    del _L2_ffn_all

    def _L3_xattn_setup():
        import jax, jax.numpy as jnp
        import numpy as np
        B_DIM, T_DIM, C_DIM = (16, 128, 256)

        def _wkv(w, u, k, v):
            Bn, Tn, Cn = k.shape
            NEG_INF = jnp.float32(-1e+38)

            def step(carry, kv_t):
                p, q, o = carry
                kt, vt = kv_t
                no = jnp.maximum(o, u + kt)
                A = jnp.exp(o - no)
                E = jnp.exp(u + kt - no)
                y = (A * p + E * vt) / (A * q + E)
                no2 = jnp.maximum(w + o, kt)
                A2 = jnp.exp(w + o - no2)
                E2 = jnp.exp(kt - no2)
                return ((A2 * p + E2 * vt, A2 * q + E2, no2), y)
            init = (jnp.zeros((Bn, Cn), k.dtype), jnp.zeros((Bn, Cn), k.dtype), jnp.full((Bn, Cn), NEG_INF, k.dtype))
            kT = jnp.moveaxis(k, 1, 0)
            vT = jnp.moveaxis(v, 1, 0)
            _, yT = jax.lax.scan(step, init, (kT, vT))
            return jnp.moveaxis(yT, 0, 1)
        key = jax.random.key(seed)
        k1, k2, k3, k4 = jax.random.split(key, 4)
        w = -jnp.exp(jax.random.normal(k1, (C_DIM,), jnp.float32))
        u = jax.random.normal(k2, (C_DIM,), jnp.float32)
        k = jax.random.normal(k3, (B_DIM, T_DIM, C_DIM), jnp.float32)
        v = jax.random.normal(k4, (B_DIM, T_DIM, C_DIM), jnp.float32)
        return {'B': B_DIM, 'T': T_DIM, 'C': C_DIM, 'w': w, 'u': u, 'k': k, 'v': v}
    _L3_xattn_all = _L3_xattn_setup()
    _L3_xattn_in = {k: v for k, v in _L3_xattn_all.items() if k in ('w', 'u')}
    del _L3_xattn_all

    def _L3_ffn_setup():
        import jax, jax.numpy as jnp
        import numpy as np
        B, S, D = (4, 512, 256)
        E, R, K = (8, 16, 2)
        key = jax.random.key(seed)
        k1, k2, k3, k4 = jax.random.split(key, 4)
        x = jax.random.normal(k1, (B, S, D), dtype=jnp.float32)
        router_w = jax.random.normal(k2, (E, D), dtype=jnp.float32) * 0.02
        experts_down = jax.random.normal(k3, (E, D, R), dtype=jnp.float32) * 0.01
        experts_up = jax.random.normal(k4, (E, R, D), dtype=jnp.float32) * 0.01
        return {'x': x, 'router_w': router_w, 'experts_down': experts_down, 'experts_up': experts_up}
    _L3_ffn_all = _L3_ffn_setup()
    _L3_ffn_in = {k: v for k, v in _L3_ffn_all.items() if k in ('router_w', 'experts_down', 'experts_up')}
    del _L3_ffn_all
    return {'x': x, 'ctx_2048': ctx_2048, 'mask_BxS2_bk0': mask_BxS2_bk0, 'g_xattn': g_xattn, 'g_ffn': g_ffn, 'L0_xattn_Wq': _L0_xattn_in['Wq'], 'L0_xattn_Wg': _L0_xattn_in['Wg'], 'L0_xattn_bg': _L0_xattn_in['bg'], 'L0_xattn_Wkv': _L0_xattn_in['Wkv'], 'L0_xattn_Wo': _L0_xattn_in['Wo'], 'L0_ffn_Wr': _L0_ffn_in['Wr'], 'L0_ffn_br': _L0_ffn_in['br'], 'L0_ffn_Wd': _L0_ffn_in['Wd'], 'L0_ffn_bd': _L0_ffn_in['bd'], 'L0_ffn_Wu': _L0_ffn_in['Wu'], 'L0_ffn_bu': _L0_ffn_in['bu'], 'L1_xattn_gamma': _L1_xattn_in['gamma'], 'L1_ffn_shared_w1': _L1_ffn_in['shared_w1'], 'L1_ffn_shared_b1': _L1_ffn_in['shared_b1'], 'L1_ffn_shared_w2': _L1_ffn_in['shared_w2'], 'L1_ffn_shared_b2': _L1_ffn_in['shared_b2'], 'L1_ffn_routed_w1': _L1_ffn_in['routed_w1'], 'L1_ffn_routed_b1': _L1_ffn_in['routed_b1'], 'L1_ffn_routed_w2': _L1_ffn_in['routed_w2'], 'L1_ffn_routed_b2': _L1_ffn_in['routed_b2'], 'L1_ffn_centroids': _L1_ffn_in['centroids'], 'L1_ffn_bias': _L1_ffn_in['bias'], 'L2_ffn_gate_w': _L2_ffn_in['gate_w'], 'L2_ffn_up_w': _L2_ffn_in['up_w'], 'L2_ffn_down_w': _L2_ffn_in['down_w'], 'L2_ffn_gate_s': _L2_ffn_in['gate_s'], 'L2_ffn_up_s': _L2_ffn_in['up_s'], 'L2_ffn_down_s': _L2_ffn_in['down_s'], 'L3_xattn_w': _L3_xattn_in['w'], 'L3_xattn_u': _L3_xattn_in['u'], 'L3_ffn_router_w': _L3_ffn_in['router_w'], 'L3_ffn_experts_down': _L3_ffn_in['experts_down'], 'L3_ffn_experts_up': _L3_ffn_in['experts_up']}

def reference(x, ctx_2048, mask_BxS2_bk0, g_xattn, g_ffn, L0_xattn_Wq, L0_xattn_Wg, L0_xattn_bg, L0_xattn_Wkv, L0_xattn_Wo, L0_ffn_Wr, L0_ffn_br, L0_ffn_Wd, L0_ffn_bd, L0_ffn_Wu, L0_ffn_bu, L1_xattn_gamma, L1_ffn_shared_w1, L1_ffn_shared_b1, L1_ffn_shared_w2, L1_ffn_shared_b2, L1_ffn_routed_w1, L1_ffn_routed_b1, L1_ffn_routed_w2, L1_ffn_routed_b2, L1_ffn_centroids, L1_ffn_bias, L2_ffn_gate_w, L2_ffn_up_w, L2_ffn_down_w, L2_ffn_gate_s, L2_ffn_up_s, L2_ffn_down_s, L3_xattn_w, L3_xattn_u, L3_ffn_router_w, L3_ffn_experts_down, L3_ffn_experts_up):
    import jax
    import jax.numpy as jnp

    def _L0_xattn_ref(query, kv, Wq, Wg, bg, Wkv, Wo):
        import jax, jax.numpy as jnp
        import numpy as np
        EPS = 1e-06
        NUM_HEADS = 16

        def _feature_map(x):
            return jnp.where(x > 0, x + 1.0, jnp.exp(x))
        B, L, D = query.shape
        S = kv.shape[1]
        H = NUM_HEADS
        hd = D // H
        q = query @ Wq.T
        gate = jax.nn.sigmoid(query @ Wg.T + bg)
        kvp = kv @ Wkv.T
        k, v = jnp.split(kvp, 2, axis=-1)
        q = _feature_map(q.reshape(B, L, H, hd).transpose(0, 2, 1, 3))
        k = _feature_map(k.reshape(B, S, H, hd).transpose(0, 2, 1, 3))
        v = v.reshape(B, S, H, hd).transpose(0, 2, 1, 3)
        kv_summary = jnp.einsum('bhsd,bhse->bhde', k, v)
        k_sum = k.sum(axis=-2)
        z = 1.0 / (jnp.einsum('bhld,bhd->bhl', q, k_sum)[..., None] + EPS)
        attn = jnp.einsum('bhld,bhde->bhle', q, kv_summary) * z
        attn = attn.transpose(0, 2, 1, 3).reshape(B, L, D)
        out = attn * gate @ Wo.T
        return out

    def _L0_ffn_ref(x, Wr, br, Wd, bd, Wu, bu):
        import jax, jax.numpy as jnp
        import numpy as np
        D = 256
        E = 8
        R = 16
        K = 2
        INIT_BONUS = 3.0
        ANNEAL_STEPS = 625
        CURRENT_STEP = 1
        logits = jnp.einsum('btd,de->bte', x, Wr) + br
        progress = min(CURRENT_STEP / ANNEAL_STEPS, 1.0)
        bonus = INIT_BONUS * (1.0 - progress)
        logits = logits + bonus
        gates = jax.nn.softmax(logits, axis=-1)
        topk_vals, topk_idx = jax.lax.top_k(gates, K)
        topk_vals = topk_vals / topk_vals.sum(axis=-1, keepdims=True)
        w = (jax.nn.one_hot(topk_idx, E, dtype=x.dtype) * topk_vals[..., None]).sum(axis=-2)
        h = jax.nn.relu(jnp.einsum('btd,edr->betr', x, Wd) + bd[None, :, None, :])
        eo = jnp.einsum('betr,erd->betd', h, Wu) + bu[None, :, None, :]
        out = jnp.einsum('bte,betd->btd', w, eo)
        return out

    def _L1_xattn_ref(q, k, v, gamma):
        import jax, jax.numpy as jnp
        import numpy as np
        N_HEAD = 8
        B, Dq, Lq = q.shape
        Dv, Lk = (v.shape[-2], v.shape[-1])
        h = N_HEAD
        dq = Dq // h
        dv = Dv // h
        qh = q.reshape(B, h, dq, Lq)
        kh = k.reshape(B, h, dq, Lk)
        vh = v.reshape(B, h, dv, Lk)
        scale = 1.0 / jnp.sqrt(jnp.asarray(dq, dtype=q.dtype))
        qk = jnp.einsum('bhdq,bhdl->bhql', qh, kh) * scale
        sm = jax.nn.softmax(qk, axis=-1)
        ret = jnp.einsum('bhql,bhdl->bhdq', sm, vh)
        ret = ret.reshape(B, Dv, Lq)
        return gamma * ret

    def _L1_ffn_ref(u, shared_w1, shared_b1, shared_w2, shared_b2, routed_w1, routed_b1, routed_w2, routed_b2, centroids, bias):
        import jax, jax.numpy as jnp
        import numpy as np
        D_MODEL, D_FF, NS, NR, KR = (256, 176, 2, 16, 4)
        B, S = (4, 256)

        def _moe_forward(u, shared_w1, shared_b1, shared_w2, shared_b2, routed_w1, routed_b1, routed_w2, routed_b2, centroids, bias):
            b, s, d = u.shape
            flat = u.reshape(-1, d)
            T = flat.shape[0]
            h = jax.nn.relu(jnp.einsum('td,ndf->ntf', flat, shared_w1) + shared_b1[:, None, :])
            shared_out = jnp.einsum('ntf,nfd->td', h, shared_w2) + shared_b2.sum(0)
            out = flat + shared_out
            scores = jax.nn.sigmoid(flat @ centroids.T) + bias
            vals, idx = jax.lax.top_k(scores, KR)
            gating = jnp.zeros_like(scores).at[jnp.arange(T)[:, None], idx].set(vals)
            gating = gating / jnp.clip(gating.sum(-1, keepdims=True), 1e-08)

            def step(acc, ew):
                w1, b1, w2, b2, g = ew
                hj = jax.nn.relu(flat @ w1 + b1)
                yj = hj @ w2 + b2
                return (acc + yj * g[:, None], None)
            rout0 = jnp.zeros_like(flat)
            rout, _ = jax.lax.scan(step, rout0, (routed_w1, routed_b1, routed_w2, routed_b2, gating.T))
            return (out + rout).reshape(b, s, d)
        return _moe_forward(u, shared_w1, shared_b1, shared_w2, shared_b2, routed_w1, routed_b1, routed_w2, routed_b2, centroids, bias)

    def _L2_xattn_ref(hidden_states, memory_tokens, memory_mask):
        import jax, jax.numpy as jnp
        import numpy as np
        B, S, D = hidden_states.shape
        scale = 1.0 / jnp.sqrt(jnp.asarray(D, hidden_states.dtype))
        scores = jnp.einsum('bsd,bmd->bsm', hidden_states, memory_tokens) * scale
        neg_inf = jnp.asarray(-1e+30, scores.dtype)
        scores = jnp.where(memory_mask[:, None, :], scores, neg_inf)
        attn = jax.nn.softmax(scores, axis=-1)
        readout = jnp.einsum('bsm,bmd->bsd', attn, memory_tokens)
        valid_b = jnp.any(memory_mask, axis=-1)
        out = jnp.where(valid_b[:, None, None], readout, jnp.zeros_like(readout))
        return out

    def _L2_ffn_ref(x, gate_w, up_w, down_w, gate_s, up_s, down_s):
        import jax, jax.numpy as jnp
        import numpy as np
        HIDDEN = 256
        INTER = 704
        B, S = (2, 256)

        def _ternary(key, shape):
            return jax.random.randint(key, shape, -1, 2).astype(jnp.float32)
        b, s, h = x.shape
        xf = x.reshape(b * s, h)
        g = jnp.einsum('th,ih->ti', xf, gate_w) * gate_s
        u = jnp.einsum('th,ih->ti', xf, up_w) * up_s
        hdn = jax.nn.silu(g) * u
        out = jnp.einsum('ti,hi->th', hdn, down_w) * down_s
        return out.reshape(b, s, -1)

    def _L3_xattn_ref(B, T, C, w, u, k, v):
        import jax, jax.numpy as jnp
        import numpy as np
        B_DIM, T_DIM, C_DIM = (16, 128, 256)

        def _wkv(w, u, k, v):
            Bn, Tn, Cn = k.shape
            NEG_INF = jnp.float32(-1e+38)

            def step(carry, kv_t):
                p, q, o = carry
                kt, vt = kv_t
                no = jnp.maximum(o, u + kt)
                A = jnp.exp(o - no)
                E = jnp.exp(u + kt - no)
                y = (A * p + E * vt) / (A * q + E)
                no2 = jnp.maximum(w + o, kt)
                A2 = jnp.exp(w + o - no2)
                E2 = jnp.exp(kt - no2)
                return ((A2 * p + E2 * vt, A2 * q + E2, no2), y)
            init = (jnp.zeros((Bn, Cn), k.dtype), jnp.zeros((Bn, Cn), k.dtype), jnp.full((Bn, Cn), NEG_INF, k.dtype))
            kT = jnp.moveaxis(k, 1, 0)
            vT = jnp.moveaxis(v, 1, 0)
            _, yT = jax.lax.scan(step, init, (kT, vT))
            return jnp.moveaxis(yT, 0, 1)
        return _wkv(w, u, k, v)

    def _L3_ffn_ref(x, router_w, experts_down, experts_up):
        import jax, jax.numpy as jnp
        import numpy as np
        B, S, D = (4, 512, 256)
        E, R, K = (8, 16, 2)
        E_ = router_w.shape[0]
        logits = jnp.einsum('bsd,ed->bse', jax.lax.stop_gradient(x), router_w)
        w, idx = jax.lax.top_k(logits, K)
        w = jax.nn.softmax(w, axis=-1)
        w_full = jnp.sum(jax.nn.one_hot(idx, E_, dtype=x.dtype) * w[..., None], axis=2)
        h = jnp.einsum('bsd,edr->bser', x, experts_down)
        out = x + jnp.einsum('bser,bse,erd->bsd', h, w_full, experts_up)
        return out
    x = x + jnp.tanh(g_xattn[0]) * _L0_xattn_ref(_layernorm(x, axis=-1), ctx_2048, L0_xattn_Wq, L0_xattn_Wg, L0_xattn_bg, L0_xattn_Wkv, L0_xattn_Wo)
    x = x + jnp.tanh(g_ffn[0]) * _L0_ffn_ref(_layernorm(x, axis=-1), L0_ffn_Wr, L0_ffn_br, L0_ffn_Wd, L0_ffn_bd, L0_ffn_Wu, L0_ffn_bu)
    x = x + jnp.tanh(g_xattn[1]) * _L1_xattn_ref(_layernorm(x, axis=-1), ctx_2048, ctx_2048, L1_xattn_gamma)
    x = x + jnp.tanh(g_ffn[1]) * _L1_ffn_ref(_layernorm(x, axis=-1), L1_ffn_shared_w1, L1_ffn_shared_b1, L1_ffn_shared_w2, L1_ffn_shared_b2, L1_ffn_routed_w1, L1_ffn_routed_b1, L1_ffn_routed_w2, L1_ffn_routed_b2, L1_ffn_centroids, L1_ffn_bias)
    x = x + jnp.tanh(g_xattn[2]) * _L2_xattn_ref(_layernorm(x, axis=-1), ctx_2048, mask_BxS2_bk0)
    x = x + jnp.tanh(g_ffn[2]) * _L2_ffn_ref(_layernorm(x, axis=-1), L2_ffn_gate_w, L2_ffn_up_w, L2_ffn_down_w, L2_ffn_gate_s, L2_ffn_up_s, L2_ffn_down_s)
    x = x + jnp.tanh(g_xattn[3]) * _L3_xattn_ref(8, 128, 256, L3_xattn_w, L3_xattn_u, _layernorm(x, axis=-1), ctx_2048)
    x = x + jnp.tanh(g_ffn[3]) * _L3_ffn_ref(_layernorm(x, axis=-1), L3_ffn_router_w, L3_ffn_experts_down, L3_ffn_experts_up)
    return x

_drawn_inputs = setup_inputs


def setup_inputs(seed=0):
    import zlib

    import numpy as np

    out = dict(_drawn_inputs(seed))
    spreads = {'L0_xattn_bg': (1.0, 0.2),
     'L0_ffn_bd': (0.0, 0.1),
     'L0_ffn_bu': (0.0, 0.1),
     'L1_ffn_shared_b1': (0.0, 0.1),
     'L1_ffn_shared_b2': (0.0, 0.1),
     'L1_ffn_routed_b1': (0.0, 0.542),
     'L1_ffn_routed_b2': (0.0, 0.372),
     'L1_ffn_bias': (0.0, 0.1)}
    factors = {'g_ffn': 34.32,
     'L3_ffn_router_w': 8.0,
     'L3_ffn_experts_down': 8.0,
     'L3_ffn_experts_up': 8.0}
    for name, (base, spread) in spreads.items():
        noise = np.random.default_rng([zlib.crc32(name.encode()), seed]).standard_normal(out[name].shape)
        drawn = base * np.exp(spread * noise) if base else spread * noise
        out[name] = jnp.asarray(drawn.astype(out[name].dtype))
    for name, factor in factors.items():
        out[name] = (out[name] * factor).astype(out[name].dtype)
    return out
```

```python
from contextlib import ExitStack

import numpy as np

import concourse.bass as bass
from concourse import mybir

ALU = mybir.AluOpType
ACT = mybir.ActivationFunctionType
F32 = mybir.dt.float32
F32R = mybir.dt.float32r
U8 = mybir.dt.uint8
AX_X = mybir.AxisListType.X

P = 128
NB = 8
D = 256
KC = D // P
G = 4
NG = NB // G
BIG = 3.0e38
LN_EPS = 1e-5

STAGES = 8


class Machine:

    def __init__(self, nc, ctx, dram):
        self.nc, self.ctx, self.dram = nc, ctx, dram

        self.X = self.sb("X", [P, NB, D])
        self.CT = self.sb("CT", [P, KC, NB, P])
        self.CN = self.sb("CN", [P, NB, D])
        self.const = self.sb("const", [P, CONST_COLS])
        self.ident = self.const[:, 0:P]
        self.blockdiag = self.const[:, P:2 * P]
        self.headcol = self.const[:, 2 * P:2 * P + 8]
        self.minus_half = self.const[:, 2 * P + 8:2 * P + 16]
        self.one_row = self.const[:, 2 * P + 16:2 * P + 17]
        self.gates_raw = self.sb("gates_raw", [P, 8])
        self.tg = self.sb("tg", [P, 8])
        self.xn = self.sb("xn", [P, G, D])
        self.xn_all = self.sb("xn_all", [P, NB, D])
        self.stats = self.sb("stats", [P, G, 6])
        self.mv = self.sb("mv", [P, G, 2])
        self.veps = self.sb("veps", [P, G])
        self.rstd = self.sb("rstd", [P, G])
        self.xt_hi = self.sb("xt_hi", [P, KC, NB, P], F32R)
        self.xt_lo = self.sb("xt_lo", [P, KC, NB, P], F32R)
        self.bank = [ctx.enter_context(nc.psum_tensor(f"bank{i}", [P, 512], F32)) for i in range(8)]

        self.arena_f = self.sb("arena_f", [P, ARENA_F])
        self.arena_r = self.sb("arena_r", [P, ARENA_R], F32R)
        self.used = {"f": 0, "r": 0}
        self.ring_raw = [self.sb(f"ring_raw{i}", [P, 6 * P]) for i in range(2)]
        self.ring_hi = [self.sb(f"ring_hi{i}", [P, 6 * P], F32R) for i in range(2)]
        self.ring_lo = [self.sb(f"ring_lo{i}", [P, 6 * P], F32R) for i in range(2)]
        self.x_done = self.sem("x_done")
        self.vector_steps = self.sem("vector_steps")
        self.steps = 0
        self.norm_mv, self.norm_veps = self.sem("norm_mv"), self.sem("norm_veps")
        self.norm_rstd, self.norm_xn = self.sem("norm_rstd"), self.sem("norm_xn")
        self.xt_raw, self.xt_hi_ready, self.xt_lo_ready = self.sem("xt_raw"), self.sem("xt_hi"), self.sem("xt_lo")
        self.transposed = 0
        self.const_in = self.sem("const_in")
        self.ctx_in = self.sem("ctx_in")
        self.tg_ready = self.sem("tg_ready")

    def step(self, instruction):
        instruction.then_inc(self.vector_steps, 1)
        self.steps += 1

    def wait_steps(self, dve):
        dve.wait_ge(self.vector_steps, self.steps)

    def sb(self, name, shape, dt=F32):
        return self.ctx.enter_context(self.nc.sbuf_tensor(name, shape, dt))

    def work(self, shape, dt=F32):
        size = int(np.prod(shape[1:]))
        arena, name = (self.arena_r, "r") if dt == F32R else (self.arena_f, "f")
        a = self.used[name]
        self.used[name] += size
        view = arena[0:shape[0], a:a + size]
        if len(shape) > 2:
            dims = " ".join(f"d{n}" for n in range(len(shape) - 1))
            view = view.rearrange(f"p ({dims}) -> p {dims}", **{f"d{n}": v for n, v in enumerate(shape[1:])})
        return view

    def sem(self, name):
        return self.ctx.enter_context(self.nc.semaphore(name))

    def x_at(self, stage, b):
        return 16 * NG + NB * stage + b


CONST_COLS = 2 * P + 20
ARENA_F = 19000
ARENA_R = 9216


def f(view):
    return view.bitcast(F32)


def split_matmul(pe, out, lhs, rhs, start, stop, **kw):
    (lh, ll), (rh, rl) = lhs, rhs
    pe.matmul(out, ll, rh, start=start, stop=False, **kw)
    pe.matmul(out, lh, rl, start=False, stop=False, **kw)
    return pe.matmul(out, lh, rh, start=False, stop=stop, **kw)


class Norm:

    def __init__(self, m, stage):
        self.m, self.stage = m, stage
        self.passed = stage * NG
        self.mv, self.veps, self.rstd, self.xn = m.norm_mv, m.norm_veps, m.norm_rstd, m.norm_xn

    def xn_at(self, n):
        return G * self.passed + n

    def vector(self, dve, g, out):
        m = self.m
        for j in range(G):
            dve.wait_ge(m.x_done, m.x_at(self.stage - 1, G * g + j + 1) if self.stage else 16 * g + 16)
            m.step(dve.bn_stats(m.stats[:, j, :], m.X[:, G * g + j, :]))
        for j in range(G):
            m.wait_steps(dve)
            dve.bn_aggr(m.mv[:, j, :], m.stats[:, j, :]).then_inc(self.mv, 1)
        dve.wait_ge(self.rstd, self.passed + g + 1)
        for j in range(G):
            b = G * g + j
            dve.tensor_scalar(out(j), m.X[:, b, :], m.mv[:, j, 0:1], m.rstd[:, j:j + 1],
                              ALU.subtract, ALU.mult).then_inc(self.xn, 1)

    def gpsimd(self, pool, g):
        m = self.m
        pool.wait_ge(self.mv, self.xn_at(G * g + G))
        pool.tensor_scalar(m.veps[:, :], m.mv[:, :, 1], LN_EPS, None, ALU.add).then_inc(self.veps, 1)
        pool.wait_ge(self.veps, self.passed + g + 1)
        pool.tensor_tensor(m.rstd[:, :], m.veps[:, :], m.minus_half[:, 0:G], ALU.pow).then_inc(self.rstd, 1)


class Transposed:

    def __init__(self, m, banks, norm, hi=None, lo=None):
        self.m, self.banks, self.norm = m, banks, norm
        self.hi = hi or (lambda g, c: m.xt_hi[:, c, 0:G, :])
        self.lo = lo or (lambda g, c: m.xt_lo[:, c, 0:G, :])
        self.passed = m.transposed
        m.transposed += NG
        self.raw, self.hi_ready, self.lo_ready = m.xt_raw, m.xt_hi_ready, m.xt_lo_ready

    def lo_at(self, groups):
        return KC * (self.passed + groups)

    def tensor(self, pe, g, xn):
        pe.wait_ge(self.norm.xn, self.norm.xn_at(G * g + G))
        for c in range(KC):
            for j in range(G):
                mm = pe.transpose(self.banks[c][:, j * P:(j + 1) * P], xn(j)[:, c * P:(c + 1) * P], self.m.ident)
        mm.then_inc(self.raw, 1)

    def bank(self, c):
        return self.banks[c][:, :].rearrange("p (j n) -> p j n", j=G)

    def scalar(self, act, g):
        act.wait_ge(self.raw, self.passed + g + 1)
        for c in range(KC):
            act.activation(self.hi(g, c), self.bank(c), ACT.Copy).then_inc(self.hi_ready, 1)

    def vector(self, dve, g):
        for c in range(KC):
            dve.wait_ge(self.hi_ready, KC * (self.passed + g) + c + 1)
            dve.tensor_tensor(self.lo(g, c), self.bank(c), f(self.hi(g, c)), ALU.subtract).then_inc(self.lo_ready, 1)


def after(engine, sem, count):
    if not (isinstance(count, int) and count <= 0):
        engine.wait_ge(sem, count)


def l0_attention(m, stage):
    HD = 16
    s = lambda name: m.sem(f"l0a_{name}")
    norm = Norm(m, stage)
    cols = {"kv": (0, 2 * D), "q": (2 * D, 3 * D), "g": (3 * D, 4 * D), "o": (4 * D, 5 * D)}
    W = m.work([P, KC, 5 * D])
    W_hi = m.work([P, KC, 5 * D], F32R)
    W_lo = m.work([P, KC, 5 * D], F32R)
    bg = m.work([P, D])
    ct_hi = m.work([P, KC, G, P], F32R)
    ct_lo = m.work([P, KC, G, P], F32R)
    k_min = m.work([P, G, D])
    k_exp = m.work([P, G, D])
    k_feat = m.work([P, G, D])
    v_one = m.work([P, G, KC, P + 1])
    q_min = m.work([P, KC, G * P])
    q_exp = m.work([P, KC, G * P])
    q_feat = m.work([P, KC, G * P])
    g_sum = m.work([P, G, D])
    g_tanh = m.work([P, G, D])
    summary = m.work([P, G, KC, P + 8])
    z_den = m.work([P, G, KC, 8])
    z = m.work([P, G, KC, 8])
    attn = m.work([P, G, D])
    gated = m.work([P, G, D])
    gt_hi = m.work([P, G, KC, P], F32R)
    gt_lo = m.work([P, G, KC, P], F32R)
    half_tg = m.work([P, 1])

    w_in, w_hi_ready, w_lo_ready, bg_in, ones_ready = s("w_in"), s("w_hi"), s("w_lo"), s("bg_in"), s("ones")
    ct_hi_ready, ct_ready = s("ct_hi"), s("ct")
    kv_proj, k_min_ready, k_exp_ready, k_ready, v_ready = s("kv_proj"), s("k_min"), s("k_exp"), s("k"), s("v")
    q_proj, q_min_ready, q_exp_ready, q_ready = s("q_proj"), s("q_min"), s("q_exp"), s("q")
    g_proj, g_sum_ready, g_tanh_ready = s("g_proj"), s("g_sum"), s("g_tanh")
    kv_sum, summary_ready, num_ready = s("kv_sum"), s("summary"), s("num")
    attn_ready, gated_ready, gt_raw, gt_hi_ready, gt_lo_ready, out_ready = s("attn"), s("gated"), s("gt_raw"), s("gt_hi"), s("gt_lo"), s("out")

    kv_bank = [m.bank[0], m.bank[1]]
    xt = Transposed(m, [m.bank[2], m.bank[3]], norm)
    q_bank = [m.bank[4], m.bank[5]]
    g_bank = lambda j: m.bank[6 + j // 2][:, (j % 2) * D:(j % 2 + 1) * D]
    sum_bank = lambda j: m.bank[j % 2][:, :].rearrange("p (c n) -> p c n", c=KC)
    num_bank = lambda j: m.bank[2 + j % 2][:, :].rearrange("p (c n) -> p c n", c=KC)
    gt_bank = lambda j: m.bank[4 + j % 2][:, 0:D].rearrange("p (c n) -> p c n", c=KC)
    out_bank = lambda j: m.bank[6 + j % 2][:, 0:D]

    def load(sp):
        w = m.dram["l0a_w"].rearrange("p (c n) -> p c n", c=KC)
        sp.dma_start(W[:, :, 0:2 * D], w[:, :, 0:2 * D]).then_inc(w_in, 16)
        sp.dma_start(W[:, :, 2 * D:5 * D], w[:, :, 2 * D:5 * D]).then_inc(w_in, 16)
        sp.dma_start(bg[:, :], m.dram["l0a_bg"].broadcast_to((P, D))).then_inc(bg_in, 16)

    def gpsimd(pool):
        pool.memset(v_one[:, :, :, P:P + 1], 1.0).then_inc(ones_ready, 1)
        for g in range(NG):
            pool.wait_ge(m.ctx_in, 32)
            pool.wait_ge(m.x_done, m.x_at(stage, G * g))
            for c in range(KC):
                pool.tensor_copy(ct_hi[:, c, :, :], m.CT[:, c, bass.ds(G * g, G), :]).then_inc(ct_hi_ready, 1)
                pool.wait_ge(ct_hi_ready, KC * g + c + 1)
                pool.tensor_tensor(ct_lo[:, c, :, :], m.CT[:, c, bass.ds(G * g, G), :], f(ct_hi[:, c, :, :]), ALU.subtract).then_inc(ct_ready, 1)
            norm.gpsimd(pool, g)

    def scalar(act):
        act.wait_ge(w_in, 32)
        act.activation(W_hi[:, :, 0:2 * D], W[:, :, 0:2 * D], ACT.Copy).then_inc(w_hi_ready, 1)
        act.activation(W_hi[:, :, 2 * D:5 * D], W[:, :, 2 * D:5 * D], ACT.Copy).then_inc(w_hi_ready, 1)
        for g in range(NG):
            act.wait_ge(m.x_done, m.x_at(stage, G * g))
            act.wait_ge(ones_ready, 1)
            for j in range(G):
                act.wait_ge(k_min_ready, G * g + j + 1)
                act.activation(k_exp[:, j, :], k_min[:, j, :], ACT.Exp).then_inc(k_exp_ready, 1)
                act.wait_ge(k_ready, G * g + j + 1)
                act.activation(v_one[:, j, :, 0:P], kv_bank[j % 2][:, D:2 * D].rearrange("p (c n) -> p c n", c=KC), ACT.Copy).then_inc(v_ready, 1)
            xt.scalar(act, g)
            for c in range(KC):
                act.wait_ge(q_min_ready, KC * g + c + 1)
                act.activation(q_exp[:, c, :], q_min[:, c, :], ACT.Exp).then_inc(q_exp_ready, 1)
            for h in range(0, G, 2):
                act.wait_ge(g_sum_ready, (G * g + h) // 2 + 1)
                act.activation(g_tanh[:, h:h + 2, :], g_sum[:, h:h + 2, :], ACT.Tanh, scale=0.5).then_inc(g_tanh_ready, 1)
            for j in range(G):
                act.wait_ge(gt_raw, G * g + j + 1)
                act.activation(gt_hi[:, j, :, :], gt_bank(j), ACT.Copy).then_inc(gt_hi_ready, 1)

    def vector(dve):
        dve.wait_ge(w_in, 32)
        for n, (a, b) in enumerate(((0, 2 * D), (2 * D, 5 * D))):
            dve.wait_ge(w_hi_ready, n + 1)
            dve.tensor_tensor(W_lo[:, :, a:b], W[:, :, a:b], f(W_hi[:, :, a:b]), ALU.subtract).then_inc(w_lo_ready, 1)
        dve.wait_ge(m.tg_ready, 1)
        m.step(dve.tensor_scalar(half_tg[:, :], m.tg[:, 0:1], 0.5, None, ALU.mult))
        for g in range(NG):
            norm.vector(dve, g, lambda j: m.xn[:, j, :])
            for j in range(G):
                dve.wait_ge(kv_proj, G * g + j + 1)
                dve.tensor_scalar(k_min[:, j, :], kv_bank[j % 2][:, 0:D], 0.0, None, ALU.min).then_inc(k_min_ready, 1)
                dve.wait_ge(k_exp_ready, G * g + j + 1)
                dve.scalar_tensor_tensor(k_feat[:, j, :], kv_bank[j % 2][:, 0:D], 0.0, k_exp[:, j, :], ALU.max, ALU.add).then_inc(k_ready, 1)
            xt.vector(dve, g)
            for c in range(KC):
                dve.wait_ge(q_proj, KC * g + c + 1)
                dve.tensor_scalar(q_min[:, c, :], q_bank[c][:, :], 0.0, None, ALU.min).then_inc(q_min_ready, 1)
                dve.wait_ge(q_exp_ready, KC * g + c + 1)
                dve.scalar_tensor_tensor(q_feat[:, c, :], q_bank[c][:, :], 0.0, q_exp[:, c, :], ALU.max, ALU.add).then_inc(q_ready, 1)
            dve.wait_ge(bg_in, 16)
            for h in range(0, G, 2):
                dve.wait_ge(g_proj, G * g + h + 2)
                dve.tensor_tensor(g_sum[:, h:h + 2, :], m.bank[6 + h // 2][:, :].rearrange("p (j n) -> p j n", j=2),
                                  bg[:, :].unsqueeze(1).broadcast_to((P, 2, D)), ALU.add).then_inc(g_sum_ready, 1)
            for j in range(G):
                dve.wait_ge(kv_sum, G * g + j + 1)
                dve.tensor_tensor(summary[:, j, :, 0:P], sum_bank(j)[:, :, 0:P],
                                  m.blockdiag.unsqueeze(1).broadcast_to((P, KC, P)), ALU.mult)
                dve.tensor_tensor(summary[:, j, :, P:P + 8], sum_bank(j)[:, :, P:P + 1].broadcast_to((P, KC, 8)),
                                  m.headcol.unsqueeze(1).broadcast_to((P, KC, 8)), ALU.mult).then_inc(summary_ready, 1)
            for j in range(G):
                dve.wait_ge(num_ready, G * g + j + 1)
                m.step(dve.tensor_scalar(z_den[:, j, :, :], num_bank(j)[:, :, P:P + 8], 1e-6, None, ALU.add))
                m.wait_steps(dve)
                m.step(dve.reciprocal(z[:, j, :, :], z_den[:, j, :, :]))
                m.wait_steps(dve)
                dve.tensor_tensor(attn[:, j, :].rearrange("p (c h d) -> p c h d", c=KC, h=8),
                                  num_bank(j)[:, :, 0:P].rearrange("p c (h d) -> p c h d", h=8),
                                  z[:, j, :, :].unsqueeze(3).broadcast_to((P, KC, 8, HD)), ALU.mult).then_inc(attn_ready, 1)
                dve.wait_ge(attn_ready, G * g + j + 1)
                dve.wait_ge(g_tanh_ready, (G * g + j) // 2 + 1)
                dve.scalar_tensor_tensor(gated[:, j, :], g_tanh[:, j, :], 1.0, attn[:, j, :], ALU.add, ALU.mult).then_inc(gated_ready, 1)
            for j in range(G):
                dve.wait_ge(gt_hi_ready, G * g + j + 1)
                dve.tensor_tensor(gt_lo[:, j, :, :], gt_bank(j), f(gt_hi[:, j, :, :]), ALU.subtract).then_inc(gt_lo_ready, 1)
            m.wait_steps(dve)
            for j in range(G):
                dve.wait_ge(out_ready, G * g + j + 1)
                dve.scalar_tensor_tensor(m.X[:, G * g + j, :], out_bank(j), half_tg[:, 0:1], m.X[:, G * g + j, :],
                                         ALU.mult, ALU.add).then_inc(m.x_done, 1)

    def tensor(pe):
        def w(name, c, n0=0, n1=None):
            a, b = cols[name]
            a, b = a + n0, b if n1 is None else a + n1
            return W_hi[:, c, a:b], W_lo[:, c, a:b]

        pe.wait_ge(m.const_in, 16)
        pe.wait_ge(w_lo_ready, 2)
        for g in range(NG):
            pe.wait_ge(m.x_done, m.x_at(stage, G * g))
            pe.wait_ge(ct_ready, KC * g + KC)
            for j in range(G):
                if j >= 2:
                    pe.wait_ge(k_ready, G * g + j - 1)
                    pe.wait_ge(v_ready, G * g + j - 1)
                for c in range(KC):
                    mm = split_matmul(pe, kv_bank[j % 2][:, :], (ct_hi[:, c, j, :], ct_lo[:, c, j, :]), w("kv", c), c == 0, c == KC - 1)
                mm.then_inc(kv_proj, 1)
            xt.tensor(pe, g, lambda j: m.xn[:, j, :])
            pe.wait_ge(xt.lo_ready, xt.lo_at(g + 1))
            for o in range(KC):
                for c in range(KC):
                    mm = split_matmul(pe, q_bank[o][:, :], w("q", c, o * P, (o + 1) * P), (m.xt_hi[:, c, 0:G, :], m.xt_lo[:, c, 0:G, :]), c == 0, c == KC - 1)
                mm.then_inc(q_proj, 1)
            for j in range(G):
                for c in range(KC):
                    mm = split_matmul(pe, g_bank(j), (m.xt_hi[:, c, j, :], m.xt_lo[:, c, j, :]), w("g", c), c == 0, c == KC - 1)
                mm.then_inc(g_proj, 1)
            for j in range(G):
                pe.wait_ge(k_ready, G * g + (G if j < 2 else j + 1))
                pe.wait_ge(v_ready, G * g + (G if j < 2 else j + 1))
                if j >= 2:
                    pe.wait_ge(summary_ready, G * g + j - 1)
                for c in range(KC):
                    mm = pe.matmul(sum_bank(j)[:, c, 0:P + 1], k_feat[:, j, c * P:(c + 1) * P], v_one[:, j, c, :], start=True, stop=True)
                mm.then_inc(kv_sum, 1)
            pe.wait_ge(q_ready, KC * g + KC)
            for j in range(G):
                pe.wait_ge(summary_ready, G * g + j + 1)
                if j >= 2:
                    pe.wait_ge(attn_ready, G * g + j - 1)
                for c in range(KC):
                    mm = pe.matmul(num_bank(j)[:, c, 0:P + 8], q_feat[:, c, j * P:(j + 1) * P], summary[:, j, c, :], start=True, stop=True)
                mm.then_inc(num_ready, 1)
            for j in range(G):
                pe.wait_ge(gated_ready, G * g + j + 1)
                if j >= 2:
                    pe.wait_ge(gt_lo_ready, G * g + j - 1)
                for c in range(KC):
                    mm = pe.transpose(gt_bank(j)[:, c, :], gated[:, j, c * P:(c + 1) * P], m.ident)
                mm.then_inc(gt_raw, 1)
            for j in range(G):
                pe.wait_ge(gt_lo_ready, G * g + j + 1)
                if j >= 2:
                    pe.wait_ge(m.x_done, m.x_at(stage, G * g + j - 1))
                for c in range(KC):
                    mm = split_matmul(pe, out_bank(j), (gt_hi[:, j, c, :], gt_lo[:, j, c, :]), w("o", c), c == 0, c == KC - 1)
                mm.then_inc(out_ready, 1)

    return {"load": load, "gpsimd": gpsimd, "scalar": scalar, "vector": vector, "tensor": tensor}


def adapters(m, stage, name, first):
    E, R, K = 8, 16, 2
    BONUS = 3.0 * (1.0 - 1 / 625)
    ER = E * R
    s = lambda x: m.sem(f"{name}_{x}")
    gate = m.tg[:, 4:5] if first else m.tg[:, 7:8]
    norm = Norm(m, stage)
    xt = Transposed(m, [m.bank[4], m.bank[5]], norm)
    W = m.sb(f"{name}_w", [P, KC, ER + E])
    W_hi = m.sb(f"{name}_w_hi", [P, KC, ER + E], F32R)
    W_lo = m.sb(f"{name}_w_lo", [P, KC, ER + E], F32R)
    up = m.sb(f"{name}_up", [P, D])
    if first:
        bias = m.sb(f"{name}_bias", [P, ER + E])
        up_bias = m.sb(f"{name}_up_bias", [E, D])
    proj = m.work([P, G, ER + E])
    logits = m.work([P, G, 2 * E])
    top = m.work([P, G, 8])
    chosen = m.work([P, G, 8])
    marked = m.work([P, G, 2 * E])
    mask = m.work([P, G, E])
    shifted = m.work([P, G, E])
    expd = m.work([P, G, E])
    kept = m.work([P, G, E])
    total = m.work([P, G])
    inv = m.work([P, G])
    weight = m.work([P, G, E])
    hidden = m.work([P, G, ER])
    hidden_t = m.work([P, G, P])
    weight_t = m.work([E, G, P])
    plus_x = m.work([P, G, D])
    loaded, w_hi_ready, w_lo_ready, pads = s("loaded"), s("w_hi"), s("w_lo"), s("pads")
    projected, proj_ready = s("projected"), s("proj")
    shifted_ready, exp_ready = s("shifted"), s("exp")
    weight_ready, hidden_ready = s("weight"), s("hidden")
    turned, turned_ready, out_ready = s("turned"), s("turned_copy"), s("out")
    proj_bank = lambda j: m.bank[j][:, 0:ER + E]
    turn_bank = lambda j: m.bank[6 + j % 2]
    out_bank = lambda j: m.bank[j][:, 0:D]
    LOADS = 4 if first else 2

    def load(sp):
        sp.dma_start(W[:, :, :], m.dram[f"{name}_w"].rearrange("p (c n) -> p c n", c=KC)).then_inc(loaded, 16)
        sp.dma_start(up[:, :], m.dram[f"{name}_up"]).then_inc(loaded, 16)
        if first:
            sp.dma_start(bias[:, :], m.dram[f"{name}_bias"].broadcast_to((P, ER + E))).then_inc(loaded, 16)
            sp.dma_start(up_bias[:, :], m.dram[f"{name}_up_bias"]).then_inc(loaded, 16)

    def gpsimd(pool):
        pool.wait_ge(loaded, 16 * LOADS)
        pool.tensor_copy(W_hi[:, :, :], W[:, :, :]).then_inc(w_hi_ready, 1)
        pool.wait_ge(w_hi_ready, 1)
        pool.tensor_tensor(W_lo[:, :, :], W[:, :, :], f(W_hi[:, :, :]), ALU.subtract).then_inc(w_lo_ready, 1)
        pool.wait_ge(m.x_done, m.x_at(stage, 0))
        pool.memset(logits[:, :, E:2 * E], -BIG).then_inc(pads, 1)
        pool.memset(chosen[:, :, :], -BIG).then_inc(pads, 1)
        for g in range(NG):
            norm.gpsimd(pool, g)

    def scalar(act):
        for g in range(NG):
            act.wait_ge(m.x_done, m.x_at(stage, G * g))
            xt.scalar(act, g)
            if not first:
                for j in range(G):
                    act.wait_ge(projected, G * g + j + 1)
                    act.activation(proj[:, j, :], proj_bank(j), ACT.Copy).then_inc(proj_ready, 1)
            act.wait_ge(shifted_ready, g + 1)
            act.activation(expd[:, :, :], shifted[:, :, :], ACT.Exp).then_inc(exp_ready, 1)
            for j in range(G):
                act.wait_ge(turned, G * g + j + 1)
                act.activation(hidden_t[:, j, :], turn_bank(j)[:, 0:P], ACT.Copy).then_inc(turned_ready, 1)
                if first:
                    act.activation(weight_t[:, j, :], turn_bank(j)[0:E, D:D + P], ACT.Copy).then_inc(turned_ready, 1)

    def vector(dve):
        dve.wait_ge(loaded, 16 * LOADS)
        for g in range(NG):
            norm.vector(dve, g, lambda j: m.xn[:, j, :])
            xt.vector(dve, g)
            if first:
                for j in range(G):
                    dve.wait_ge(projected, G * g + j + 1)
                    dve.tensor_tensor(proj[:, j, :], proj_bank(j), bias[:, :], ALU.add).then_inc(proj_ready, 1)
            dve.wait_ge(proj_ready, G * g + G)
            dve.wait_ge(pads, 2)
            m.step(dve.tensor_scalar(logits[:, :, 0:E], proj[:, :, ER:ER + E], BONUS if first else 0.0, None, ALU.add))
            m.wait_steps(dve)
            for j in range(G):
                m.step(dve.max(top[:, j, :], logits[:, j, :]))
            m.wait_steps(dve)
            m.step(dve.tensor_copy(chosen[:, :, 0:K], top[:, :, 0:K]))
            dve.tensor_tensor(shifted[:, :, :], logits[:, :, 0:E], top[:, :, 0:1].broadcast_to((P, G, E)), ALU.subtract).then_inc(shifted_ready, 1)
            m.wait_steps(dve)
            for j in range(G):
                m.step(dve.match_replace(marked[:, j, :], chosen[:, j, :], logits[:, j, :], BIG))
            m.wait_steps(dve)
            m.step(dve.tensor_tensor(mask[:, :, :], marked[:, :, 0:E], logits[:, :, 0:E], ALU.not_equal))
            m.wait_steps(dve)
            dve.wait_ge(exp_ready, g + 1)
            m.step(dve.tensor_tensor(kept[:, :, :], expd[:, :, :], mask[:, :, :], ALU.mult))
            m.wait_steps(dve)
            m.step(dve.reduce_sum(total[:, :], kept[:, :, :], AX_X))
            m.wait_steps(dve)
            m.step(dve.reciprocal(inv[:, :], total[:, :]))
            m.wait_steps(dve)
            dve.tensor_tensor(weight[:, :, :], kept[:, :, :], inv[:, :].unsqueeze(2).broadcast_to((P, G, E)), ALU.mult).then_inc(weight_ready, 1)
            dve.wait_ge(weight_ready, g + 1)
            for j in range(G):
                spread = weight[:, j, :].unsqueeze(2).broadcast_to((P, E, R))
                down = proj[:, j, 0:ER].rearrange("p (e r) -> p e r", e=E)
                into = hidden[:, j, :].rearrange("p (e r) -> p e r", e=E)
                if first:
                    dve.scalar_tensor_tensor(into, down, 0.0, spread, ALU.max, ALU.mult).then_inc(hidden_ready, 1)
                else:
                    dve.tensor_tensor(into, down, spread, ALU.mult).then_inc(hidden_ready, 1)
            for j in range(G):
                b = G * g + j
                dve.wait_ge(out_ready, b + 1)
                if first:
                    dve.scalar_tensor_tensor(m.X[:, b, :], out_bank(j), gate, m.X[:, b, :], ALU.mult, ALU.add).then_inc(m.x_done, 1)
                else:
                    m.step(dve.tensor_tensor(plus_x[:, j, :], out_bank(j), m.xn[:, j, :], ALU.add))
                    m.wait_steps(dve)
                    dve.scalar_tensor_tensor(m.X[:, b, :], plus_x[:, j, :], gate, m.X[:, b, :], ALU.mult, ALU.add).then_inc(m.x_done, 1)

    def tensor(pe):
        pe.wait_ge(w_lo_ready, 1)
        pe.wait_ge(loaded, 16 * LOADS)
        for g in range(NG):
            pe.wait_ge(m.x_done, m.x_at(stage, G * g))
            xt.tensor(pe, g, lambda j: m.xn[:, j, :])
            pe.wait_ge(xt.lo_ready, xt.lo_at(g + 1))
            for j in range(G):
                for c in range(KC):
                    mm = split_matmul(pe, proj_bank(j), (m.xt_hi[:, c, j, :], m.xt_lo[:, c, j, :]), (W_hi[:, c, :], W_lo[:, c, :]), c == 0, c == KC - 1)
                mm.then_inc(projected, 1)
            for j in range(G):
                pe.wait_ge(hidden_ready, G * g + j + 1)
                if j >= 2:
                    pe.wait_ge(turned_ready, (1 + first) * (G * g + j - 1))
                mm = pe.transpose(turn_bank(j)[:, 0:P], hidden[:, j, :], m.ident)
                if first:
                    mm = pe.transpose(turn_bank(j)[0:E, D:D + P], weight[:, j, :], m.ident)
                mm.then_inc(turned, 1)
            for j in range(G):
                pe.wait_ge(turned_ready, (1 + first) * (G * g + j + 1))
                mm = pe.matmul(out_bank(j), hidden_t[:, j, :], up[:, :], start=True, stop=not first)
                if first:
                    mm = pe.matmul(out_bank(j), weight_t[:, j, :], up_bias[:, :], start=False, stop=True)
                mm.then_inc(out_ready, 1)

    return {"load": load, "gpsimd": gpsimd, "scalar": scalar, "vector": vector, "tensor": tensor}


def l1_attention(m, stage):
    H, HD, STACK = 8, 16, 48
    s = lambda x: m.sem(f"l1a_{x}")
    norm = Norm(m, stage)
    sel_raw = m.xn_all[:, :, :].rearrange("p b d -> p (b d)").rearrange("p (k q n) -> p k q n", k=4, q=4)
    sel = m.sb("l1a_sel", [P, 4, 4, P], F32R)
    gamma = m.sb("l1a_gamma", [P, 1])
    scale = m.work([P, 1])
    q_hi = m.xt_hi[:, :, :, :].rearrange("p c b n -> p (c b n)").rearrange("p (b d) -> p b d", b=NB)
    q_lo = m.xt_lo[:, :, :, :].rearrange("p c b n -> p (c b n)").rearrange("p (b d) -> p b d", b=NB)
    k_hi = [ring[:, 2 * D:3 * D] for ring in m.ring_hi]
    k_lo = [ring[:, 2 * D:3 * D] for ring in m.ring_lo]
    k_stack = [m.work([P, 4, D], F32R) for _ in range(2)]
    q_stack = [m.work([P, 4, D], F32R) for _ in range(2)]
    lower = [m.work([H, D], F32R) for _ in range(2)]
    v_hi = m.work([P, 2, KC, H, 2 * HD], F32R)
    v_lo = m.work([P, 2, KC, H, 2 * HD], F32R)
    maxima = [m.work([P, KC, H]) for _ in range(2)]
    PB = 3
    probs = m.work([P, PB, KC, D])
    by_chunk = lambda ring: ring[:, 0:2 * D].rearrange("p (k n) -> p k n", k=KC)
    p_hi = [by_chunk(m.ring_hi[0]), by_chunk(m.ring_hi[1]), m.work([P, KC, D], F32R)]
    p_lo = [by_chunk(m.ring_lo[0]), by_chunk(m.ring_lo[1]), m.work([P, KC, D], F32R)]
    o_raw = m.work([P, 2, D])
    o_hi = m.work([P, 2, D], F32R)
    o_lo = m.work([P, 2, D], F32R)
    out_sel_raw = m.work([P, 2, 2, P])
    out_sel = m.work([P, 2, 2, P], F32R)
    inv = m.work([P, D])
    ratio = m.work([P, D])
    sel_in, sel_ready = s("sel_in"), s("sel")
    k_hi_ready, k_split, v_ready, ones_ready, q_hi_ready, q_split = s("k_hi"), s("k_split"), s("v"), s("ones"), s("q_hi"), s("q_split")
    k_raw, q_raw, k_stacked, q_stacked = s("k_raw"), s("q_raw"), s("k_stacked"), s("q_stacked")
    scored, max_ready, max_turned, lower_ready, row_in = s("scored"), s("max"), s("max_turned"), s("lower"), s("row_in")
    lowered, exp_ready, p_split, summed = s("lowered"), s("exp"), s("p_split"), s("summed")
    out_sel_in, out_sel_ready, v_hi_ready = s("out_sel_in"), s("out_sel"), s("v_hi")
    taken, o_hi_ready, o_split, placed = s("taken"), s("o_hi"), s("o_split"), s("placed")
    k_bank, q_bank = [m.bank[2], m.bank[7]], [m.bank[3], m.bank[6]]
    LAG, LAG_V = 0, 3

    values = lambda b: m.CT[:, :, b, :].rearrange("p c (h d) -> p c h d", h=H)

    def load(sp):
        sp.dma_start(sel_raw[:, :, :, :], m.dram["l1a_sel"].rearrange("p (k q n) -> p k q n", k=4, q=4)).then_inc(sel_in, 16)
        sp.dma_start(gamma[:, :], m.dram["l1a_gamma"].broadcast_to((P, 1))).then_inc(sel_in, 16)

    def sync(sp):
        sp.wait_ge(m.x_done, m.x_at(stage, 0))
        sp.dma_start(out_sel_raw[:, :, :, :], m.dram["l1a_out_sel"].rearrange("p (k g n) -> p k g n", k=2, g=2)).then_inc(out_sel_in, 16)
        for b in range(NB):
            sp.wait_ge(lower_ready, b + 1)
            for a in range(2):
                row = 64 * a + STACK
                sp.dma_start(f(q_stack[b % 2][row:row + 1, :, :]), f(lower[b % 2][4 * a:4 * a + 4, :])).then_inc(row_in, 16)

    def gpsimd(pool):
        pool.wait_ge(m.ctx_in, 32)
        pool.wait_ge(m.x_done, m.x_at(stage, 0))
        for g in range(NG):
            norm.gpsimd(pool, g)
        pool.wait_ge(m.const_in, 32)
        for part, one in ((v_hi, 1.0), (v_lo, 0.0)):
            rows = part[:, :, :, :, HD:2 * HD].rearrange("p n c h d -> p (n c h) d")
            pool.tensor_scalar(rows, m.minus_half[:, 0:1].unsqueeze(2).broadcast_to((P, 2 * KC * H, HD)), 0.0, one, ALU.mult, ALU.add).then_inc(ones_ready, 1)

        def low_parts(b):
            pool.wait_ge(k_hi_ready, b + 1)
            pool.tensor_tensor(k_lo[b % 2], m.CN[:, b, :], f(k_hi[b % 2]), ALU.subtract).then_inc(k_split, 1)
            pool.wait_ge(q_hi_ready, b + 1)
            pool.tensor_tensor(q_lo[:, b, :], m.xn_all[:, b, :], f(q_hi[:, b, :]), ALU.subtract).then_inc(q_split, 1)

        def value_parts(b):
            pool.wait_ge(v_hi_ready, b + 1)
            pool.tensor_tensor(v_lo[:, b % 2, :, :, 0:HD], values(b), f(v_hi[:, b % 2, :, :, 0:HD]), ALU.subtract).then_inc(v_ready, 1)

        def low_exps(b, heads):
            for h in heads:
                pool.wait_ge(exp_ready, 2 * (H * b + h + 1))
                n = (H * b + h) % PB
                pool.tensor_tensor(p_lo[n], probs[:, n, :, :], f(p_hi[n]), ALU.subtract).then_inc(p_split, 1)

        low_parts(0)
        for b in range(NB + 1):
            if b:
                low_exps(b - 1, range(0, H // 2))
            if b + 1 < NB:
                low_parts(b + 1)
            if b:
                low_exps(b - 1, range(H // 2, H))
            if b < NB:
                value_parts(b)

    def vector(dve):
        dve.wait_ge(sel_in, 32)
        dve.wait_ge(sel_ready, 1)
        m.step(dve.tensor_tensor(scale[:, :], m.tg[:, 1:2], gamma[:, :], ALU.mult))
        for g in range(NG):
            norm.vector(dve, g, lambda j: m.xn_all[:, G * g + j, :])
        m.wait_steps(dve)

        def queries(b):
            for half in range(2):
                dve.wait_ge(q_raw, 2 * b + half + 1)
                dve.tensor_copy(q_stack[b % 2][:, 2 * half:2 * half + 2, :], q_bank[half][:, :].rearrange("p (q n) -> p q n", q=2)).then_inc(q_stacked, 1)

        def largest(b, h):
            dve.wait_ge(scored, H * b + h + 1)
            dve.reduce_max(maxima[b % 2][:, :, 4 * (h % 2) + h // 2], m.bank[h % 2][:, :].rearrange("p (c n) -> p c n", c=KC), AX_X).then_inc(max_ready, 1)

        def lowering(b):
            dve.wait_ge(max_turned, b + 1)
            dve.tensor_scalar(lower[b % 2][:, :], m.bank[6][0:H, 0:D], -1.0, None, ALU.mult).then_inc(lower_ready, 1)

        def split_output(b):
            dve.wait_ge(o_hi_ready, b + 1)
            dve.tensor_tensor(o_lo[:, :, :], o_raw[:, :, :], f(o_hi[:, :, :]), ALU.subtract).then_inc(o_split, 1)

        def take(b, pair):
            dve.wait_ge(summed, H * b + 2 * pair + 2)
            after(dve, o_split, b)
            row = 2 * HD * pair
            dve.tensor_copy(o_raw[row:row + 2 * HD, :, :], m.bank[4 + pair % 2][0:2 * HD, :].rearrange("p (h n) -> p h n", h=2)).then_inc(taken, 1)

        def add(b):
            dve.wait_ge(placed, b + 1)
            m.step(dve.reciprocal(inv[:, :], m.bank[7][:, D:2 * D]))
            m.wait_steps(dve)
            m.step(dve.tensor_tensor(ratio[:, :], m.bank[7][:, 0:D], inv[:, :], ALU.mult))
            m.wait_steps(dve)
            dve.scalar_tensor_tensor(m.X[:, b, :], ratio[:, :], scale[:, 0:1], m.X[:, b, :], ALU.mult, ALU.add).then_inc(m.x_done, 1)

        for b in range(NB + 2):
            if b < NB:
                queries(b)
            if b >= 2:
                split_output(b - 2)
            for h in range(H):
                if b < NB:
                    largest(b, h)
                if 1 <= b <= NB and h > LAG_V and (h - LAG_V) % 2:
                    take(b - 1, (h - LAG_V) // 2)
            if b >= 2:
                add(b - 2)
            if b < NB:
                lowering(b)
            if 1 <= b <= NB:
                for pair in range((H - LAG_V) // 2, H // 2):
                    take(b - 1, pair)

    def scalar(act):
        act.wait_ge(sel_in, 32)
        act.activation(sel[:, :, :, :], sel_raw[:, :, :, :], ACT.Copy).then_inc(sel_ready, 1)
        act.wait_ge(m.x_done, m.x_at(stage, 0))

        def high_parts(b):
            after(act, k_raw, 2 * (b - 1))
            act.activation(k_hi[b % 2], m.CN[:, b, :], ACT.Copy).then_inc(k_hi_ready, 1)
            act.wait_ge(norm.xn, norm.xn_at(b + 1))
            act.activation(q_hi[:, b, :], m.xn_all[:, b, :], ACT.Copy).then_inc(q_hi_ready, 1)

        def value_high_parts(b):
            after(act, summed, H * (b - 1))
            act.activation(v_hi[:, b % 2, :, :, 0:HD], values(b), ACT.Copy).then_inc(v_hi_ready, 1)

        def keys(b):
            for half in range(2):
                act.wait_ge(k_raw, 2 * b + half + 1)
                act.activation(k_stack[b % 2][:, 2 * half:2 * half + 2, :], k_bank[half][:, :].rearrange("p (q n) -> p q n", q=2),
                               ACT.Identity, bias=m.one_row).then_inc(k_stacked, 1)

        def exps(b, heads):
            for h in heads:
                act.wait_ge(lowered, H * b + h + 1)
                after(act, summed, H * b + h + 1 - PB)
                n = (H * b + h) % PB
                for out in (p_hi[n], probs[:, n, :, :]):
                    act.activation(out, m.bank[2 + h % 2][:, :].rearrange("p (c n) -> p c n", c=KC), ACT.Exp, scale=0.25).then_inc(exp_ready, 1)

        high_parts(0)
        def outputs(b):
            act.wait_ge(taken, H // 2 * (b + 1))
            after(act, placed, b)
            act.activation(o_hi[:, :, :], o_raw[:, :, :], ACT.Copy).then_inc(o_hi_ready, 1)

        for b in range(NB + 2):
            if b < NB:
                keys(b)
            if b == 1:
                act.wait_ge(out_sel_in, 16)
                act.activation(out_sel[:, :, :, :], out_sel_raw[:, :, :, :], ACT.Copy).then_inc(out_sel_ready, 1)
            if b >= 2:
                outputs(b - 2)
            if 1 <= b <= NB:
                exps(b - 1, range(0, H // 2))
            if b + 1 < NB:
                high_parts(b + 1)
            if b < NB:
                value_high_parts(b)
            if 1 <= b <= NB:
                exps(b - 1, range(H // 2, H))

    def tensor(pe):
        pe.wait_ge(sel_ready, 1)
        pe.wait_ge(m.x_done, m.x_at(stage, 0))
        pe.wait_ge(ones_ready, 2)

        def stacks(b, half):
            if b and half:
                pe.wait_ge(lower_ready, b)
                pe.wait_ge(m.x_done, m.x_at(stage, max(b - 2, 0)))
            if b >= 2 and not half:
                pe.wait_ge(exp_ready, 2 * H * (b - 1))
            for kind, bank, raw, hi, lo in ((2, k_bank[half], k_raw, k_hi[b % 2], k_lo[b % 2]), (0, q_bank[half], q_raw, q_hi[:, b, :], q_lo[:, b, :])):
                for q in range(2):
                    pe.matmul(bank[:, q * D:(q + 1) * D], sel[:, kind, 2 * half + q, :], hi, start=True, stop=False)
                    mm = pe.matmul(bank[:, q * D:(q + 1) * D], sel[:, kind + 1, 2 * half + q, :], lo, start=False, stop=True)
                mm.then_inc(raw, 1)

        def score(b, h):
            a, q = h % 2, h // 2
            if h % 4 == 0:
                pe.wait_ge(q_stacked, 2 * b + h // 4 + 1)
                pe.wait_ge(k_stacked, 2 * b + h // 4 + 1)
            after(pe, max_ready, H * b + h - 1)
            for c in range(KC):
                mm = pe.matmul(m.bank[a][:, c * D:(c + 1) * D], q_stack[b % 2][64 * a:64 * a + STACK, q, c * P:(c + 1) * P],
                               k_stack[b % 2][64 * a:64 * a + STACK, q, :], start=True, stop=True)
            mm.then_inc(scored, 1)

        def lowered_scores(b, h):
            a, q = h % 2, h // 2
            if h == 0:
                pe.wait_ge(row_in, 32 * (b + 1))
                pe.wait_ge(q_stacked, min(2 * b + 3, 2 * NB))
                pe.wait_ge(k_stacked, min(2 * b + 3, 2 * NB))
            after(pe, exp_ready, 2 * (H * b + h - 1))
            for c in range(KC):
                mm = pe.matmul(m.bank[2 + a][:, c * D:(c + 1) * D], k_stack[b % 2][64 * a:64 * a + STACK + 1, q, c * P:(c + 1) * P],
                               q_stack[b % 2][64 * a:64 * a + STACK + 1, q, :], start=True, stop=True)
            mm.then_inc(lowered, 1)

        def products(b, h):
            pe.wait_ge(p_split, H * b + h + 1)
            if h == 0:
                pe.wait_ge(v_ready, b + 1)
            if h % 2 == 0:
                after(pe, taken, H // 2 * b + h // 2 - 1)
            n = (H * b + h) % PB
            out = m.bank[4 + h // 2 % 2][0:2 * HD, (h % 2) * D:(h % 2 + 1) * D]
            for k in range(KC):
                mm = split_matmul(pe, out, (v_hi[:, b % 2, k, h, :], v_lo[:, b % 2, k, h, :]), (p_hi[n][:, k, :], p_lo[n][:, k, :]),
                                  k == 0, k == KC - 1)
            mm.then_inc(summed, 1)

        def place(b):
            pe.wait_ge(out_sel_ready, 1)
            pe.wait_ge(o_split, b + 1)
            pe.wait_ge(m.x_done, m.x_at(stage, b))
            for kind in range(2):
                for g in range(2):
                    pe.matmul(m.bank[7][:, kind * D:(kind + 1) * D], out_sel[:, kind, g, :], o_hi[:, g, :], start=g == 0, stop=False)
                    mm = pe.matmul(m.bank[7][:, kind * D:(kind + 1) * D], out_sel[:, kind, g, :], o_lo[:, g, :], start=False, stop=g == 1)
            mm.then_inc(placed, 1)

        for b in range(NB + 2):
            if b < NB:
                pe.wait_ge(k_split, b + 1)
                pe.wait_ge(q_split, b + 1)
                stacks(b, 0)
                stacks(b, 1)
            for h in range(H + LAG_V):
                if b < NB and h < H:
                    score(b, h)
                if 1 <= b <= NB and LAG <= h < H + LAG:
                    lowered_scores(b - 1, h - LAG)
                if b >= 2 and h == H - 4:
                    place(b - 2)
                if 1 <= b <= NB and h >= LAG_V:
                    products(b - 1, h - LAG_V)
                if b < NB and h == H:
                    pe.wait_ge(max_ready, H * b + H)
                    for c in range(KC):
                        mm = pe.transpose(m.bank[6][0:H, c * P:(c + 1) * P], maxima[b % 2][:, c, :], m.ident)
                    mm.then_inc(max_turned, 1)

    return {"load": load, "sync": sync, "gpsimd": gpsimd, "scalar": scalar, "vector": vector, "tensor": tensor}


def feed_forward(m, stage, name, chunks, experts):
    E, NS, K = 16, 2, 4
    GE = E + NS
    s = lambda x: m.sem(f"{name}_{x}")
    norm = Norm(m, stage)
    xt = Transposed(m, [m.bank[4], m.bank[5]], norm,
                    lambda g, c: m.xt_hi[:, c, G * g:G * g + G, :], lambda g, c: m.xt_lo[:, c, G * g:G * g + G, :])
    gate = m.tg[:, 5:6] if experts else m.tg[:, 6:7]
    IN = 3 * P if experts else 4 * P
    COLS = IN + D
    hidden = m.work([P, NB, P])
    up = m.work([P, NB, P])
    gated = m.work([P, NB, P])
    h_hi = [m.work([P, NB, P], F32R) for _ in range(2)]
    h_lo = [m.work([P, NB, P], F32R) for _ in range(2)]
    summed = m.work([P, NB, D])
    w_in = [s("w_in_even"), s("w_in_odd")]
    cols_in, in_hi, in_lo, out_hi, out_lo = s("cols_in"), s("in_hi"), s("in_lo"), s("out_hi"), s("out_lo")
    h_raw, u_raw, h_ready, u_ready, gated_ready, h_hi_ready, h_lo_ready, used = s("h_raw"), s("u_raw"), s("h"), s("u"), s("gated"), s("h_hi"), s("h_lo"), s("used")
    if experts:
        b1 = m.sb(f"{name}_b1", [P, chunks])
        cen = m.sb(f"{name}_cen", [P, KC, E])
        cen_hi = m.sb(f"{name}_cen_hi", [P, KC, E], F32R)
        cen_lo = m.sb(f"{name}_cen_lo", [P, KC, E], F32R)
        bias = m.sb(f"{name}_bias", [P, E])
        b2 = m.sb(f"{name}_b2", [2 * GE, D])
        b2_hi = m.sb(f"{name}_b2_hi", [2 * GE, D], F32R)
        b2_lo = m.sb(f"{name}_b2_lo", [2 * GE, D], F32R)
        gates_t = m.work([2 * GE, NB, P], F32R)
        th = m.work([P, G, E])
        score = m.work([P, G, E + 8])
        top = m.work([P, G, 8])
        chosen = m.work([P, G, 8])
        marked = m.work([P, G, E + 8])
        mask = m.work([P, G, E])
        kept = m.work([P, G, E])
        total = m.work([P, G])
        guarded = m.work([P, G])
        inv = m.work([P, G])
        gates = m.work([P, G, GE])
        parts = m.work([P, G, 2, GE], F32R)
        small_hi, small_lo, pads = s("small_hi"), s("small_lo"), s("pads")
        routed, th_ready = s("routed"), s("th")
        gates_lo, turned, gates_t_ready = s("gates_lo"), s("turned"), s("gates_t")
    else:
        scales = m.sb(f"{name}_scales", [P, 2, chunks])
        factors = m.sb(f"{name}_factors", [P, 2, chunks])
        half = m.sb(f"{name}_half", [P, chunks])
        out_scale = m.sb(f"{name}_out_scale", [P, D])
        factors_ready = s("factors")

    acc = lambda b: m.bank[4 + b // 2][:, (b % 2) * D:(b % 2 + 1) * D]
    side = lambda t: slice(G * t, G * t + G)
    wide = lambda bank: bank[:, :].rearrange("p (j n) -> p j n", j=G)
    raw, hi, lo = m.ring_raw, m.ring_hi, m.ring_lo

    def load(sp):
        if experts:
            for tile, what in ((b1, "b1"), (cen, "cen"), (b2, "b2")):
                src = m.dram[f"{name}_{what}"]
                sp.dma_start(tile[:, :, :] if what == "cen" else tile[:, :], src.rearrange("p (c n) -> p c n", c=KC) if what == "cen" else src).then_inc(cols_in, 16)
            sp.dma_start(bias[:, :], m.dram[f"{name}_bias"].broadcast_to((P, E))).then_inc(cols_in, 16)
        else:
            sp.dma_start(scales[:, :, :], m.dram[f"{name}_scales"].rearrange("p (k n) -> p k n", k=2)).then_inc(cols_in, 16)
            sp.dma_start(out_scale[:, :], m.dram[f"{name}_out_scale"].broadcast_to((P, D))).then_inc(cols_in, 16)

    def sync(sp):
        sp.wait_ge(m.x_done, m.x_at(stage - 1, 0))
        for c in range(chunks):
            after(sp, out_lo, c - 1)
            sp.dma_start(raw[c % 2][:, 0:COLS], m.dram[f"{name}_w"][c, :, :]).then_inc(w_in[c % 2], 16)

    def gpsimd(pool):
        if experts:
            pool.wait_ge(cols_in, 64)
            for tile, h, l in ((cen[:, :, :], cen_hi[:, :, :], cen_lo[:, :, :]), (b2[:, :], b2_hi[:, :], b2_lo[:, :])):
                pool.tensor_copy(h, tile).then_inc(small_hi, 1)
            pool.wait_ge(small_hi, 2)
            for tile, h, l in ((cen[:, :, :], cen_hi[:, :, :], cen_lo[:, :, :]), (b2[:, :], b2_hi[:, :], b2_lo[:, :])):
                pool.tensor_tensor(l, tile, f(h), ALU.subtract).then_inc(small_lo, 1)
            pool.wait_ge(m.x_done, m.x_at(stage, 0))
            pool.memset(score[:, :, E:E + 8], -BIG).then_inc(pads, 1)
            pool.memset(chosen[:, :, :], -BIG).then_inc(pads, 1)
            pool.memset(gates[:, :, E:GE], 1.0).then_inc(pads, 1)
        for g in range(NG):
            norm.gpsimd(pool, g)
        def low_in(c):
            pool.wait_ge(in_hi, c + 1)
            pool.tensor_tensor(lo[c % 2][:, 0:IN], raw[c % 2][:, 0:IN], f(hi[c % 2][:, 0:IN]), ALU.subtract).then_inc(in_lo, 1)

        def low_out(c):
            pool.wait_ge(out_hi, c + 1)
            pool.tensor_tensor(lo[c % 2][:, IN:COLS], raw[c % 2][:, IN:COLS], f(hi[c % 2][:, IN:COLS]), ALU.subtract).then_inc(out_lo, 1)

        low_in(0)
        for c in range(chunks):
            if c + 1 < chunks:
                low_in(c + 1)
            low_out(c)

    def scalar(act):
        def high_in(c):
            act.wait_ge(w_in[c % 2], 16 * (c // 2 + 1))
            after(act, h_raw, 2 * (c - 1))
            act.activation(hi[c % 2][:, 0:IN], raw[c % 2][:, 0:IN], ACT.Copy).then_inc(in_hi, 1)

        def high_out(c):
            after(act, used, c - 1)
            act.activation(hi[c % 2][:, IN:COLS], raw[c % 2][:, IN:COLS], ACT.Copy).then_inc(out_hi, 1)

        act.wait_ge(m.x_done, m.x_at(stage, 0))
        high_in(0)
        for g in range(NG):
            xt.scalar(act, g)
            if experts:
                act.wait_ge(routed, g + 1)
                act.activation(th[:, :, :], m.bank[g][:, 0:G * E].rearrange("p (j e) -> p j e", j=G), ACT.Tanh, scale=0.5).then_inc(th_ready, 1)
                act.wait_ge(turned, g + 1)
                act.activation(gates_t[:, side(g), :], wide(m.bank[2 + g])[0:2 * GE, :, :], ACT.Copy).then_inc(gates_t_ready, 1)
        for c in range(chunks):
            for t in range(2):
                act.wait_ge(h_raw, 2 * c + t + 1)
                after(act, gated_ready, 2 * (c - 1) + t + 1)
                if experts:
                    act.activation(hidden[:, side(t), :], wide(m.bank[t]), ACT.Relu, bias=b1[:, c:c + 1]).then_inc(h_ready, 1)
                else:
                    act.wait_ge(factors_ready, 1)
                    act.activation(hidden[:, side(t), :], wide(m.bank[t]), ACT.Tanh, scale=half[:, c:c + 1]).then_inc(h_ready, 1)
                    act.wait_ge(u_raw, 2 * c + t + 1)
                    act.activation(up[:, side(t), :], wide(m.bank[2 + t]), ACT.Copy, scale=factors[:, 1, c:c + 1]).then_inc(u_ready, 1)
            if c + 1 < chunks:
                high_in(c + 1)
            high_out(c)
            for t in range(2):
                act.wait_ge(gated_ready, 2 * c + t + 1)
                after(act, used, c - 1)
                act.activation(h_hi[c % 2][:, side(t), :], gated[:, side(t), :], ACT.Copy).then_inc(h_hi_ready, 1)

    def vector(dve):
        dve.wait_ge(cols_in, 64 if experts else 32)
        if experts:
            m.step(dve.tensor_scalar(bias[:, :], bias[:, :], 0.5, None, ALU.add))
        else:
            m.step(dve.tensor_scalar(half[:, :], scales[:, 0, :], 0.5, None, ALU.mult))
            m.wait_steps(dve)
            dve.tensor_tensor(factors[:, 1, :], half[:, :], scales[:, 1, :], ALU.mult).then_inc(factors_ready, 1)
        for g in range(NG):
            norm.vector(dve, g, lambda j: m.xn_all[:, G * g + j, :])
            xt.vector(dve, g)
            if experts:
                dve.wait_ge(th_ready, g + 1)
                m.wait_steps(dve)
                dve.wait_ge(pads, 3)
                m.step(dve.scalar_tensor_tensor(score[:, :, 0:E], th[:, :, :], 0.5, bias[:, :].unsqueeze(1).broadcast_to((P, G, E)), ALU.mult, ALU.add))
                m.wait_steps(dve)
                for j in range(G):
                    m.step(dve.max(top[:, j, :], score[:, j, :]))
                m.wait_steps(dve)
                m.step(dve.tensor_copy(chosen[:, :, 0:K], top[:, :, 0:K]))
                m.wait_steps(dve)
                for j in range(G):
                    m.step(dve.match_replace(marked[:, j, :], chosen[:, j, :], score[:, j, :], BIG))
                m.wait_steps(dve)
                m.step(dve.tensor_tensor(mask[:, :, :], marked[:, :, 0:E], score[:, :, 0:E], ALU.not_equal))
                m.wait_steps(dve)
                m.step(dve.tensor_tensor(kept[:, :, :], score[:, :, 0:E], mask[:, :, :], ALU.mult))
                m.wait_steps(dve)
                m.step(dve.reduce_sum(total[:, :], kept[:, :, :], AX_X))
                m.wait_steps(dve)
                m.step(dve.tensor_scalar(guarded[:, :], total[:, :], 1e-8, None, ALU.max))
                m.wait_steps(dve)
                m.step(dve.reciprocal(inv[:, :], guarded[:, :]))
                m.wait_steps(dve)
                m.step(dve.tensor_tensor(gates[:, :, 0:E], kept[:, :, :], inv[:, :].unsqueeze(2).broadcast_to((P, G, E)), ALU.mult))
                m.wait_steps(dve)
                m.step(dve.tensor_copy(parts[:, :, 0, :], gates[:, :, :]))
                m.wait_steps(dve)
                dve.tensor_tensor(parts[:, :, 1, :], gates[:, :, :], f(parts[:, :, 0, :]), ALU.subtract).then_inc(gates_lo, 1)
        for c in range(chunks):
            for t in range(2):
                dve.wait_ge(h_ready, 2 * c + t + 1)
                after(dve, h_lo_ready, 2 * (c - 1) + t + 1)
                if experts:
                    dve.wait_ge(u_raw, 2 * c + t + 1)
                    dve.tensor_tensor(gated[:, side(t), :], wide(m.bank[2 + t]), hidden[:, side(t), :], ALU.mult).then_inc(gated_ready, 1)
                else:
                    dve.wait_ge(u_ready, 2 * c + t + 1)
                    m.step(dve.scalar_tensor_tensor(up[:, side(t), :], hidden[:, side(t), :], 1.0, up[:, side(t), :], ALU.add, ALU.mult))
                    m.wait_steps(dve)
                    dve.tensor_tensor(gated[:, side(t), :], wide(m.bank[t]), up[:, side(t), :], ALU.mult).then_inc(gated_ready, 1)
            for t in range(2):
                dve.wait_ge(h_hi_ready, 2 * c + t + 1)
                dve.tensor_tensor(h_lo[c % 2][:, side(t), :], gated[:, side(t), :], f(h_hi[c % 2][:, side(t), :]), ALU.subtract).then_inc(h_lo_ready, 1)
        dve.wait_ge(used, chunks)
        for q in range(NB // 2):
            two = m.bank[4 + q][:, :].rearrange("p (j n) -> p j n", j=2)
            if experts:
                m.step(dve.tensor_tensor(summed[:, 2 * q:2 * q + 2, :], two, m.xn_all[:, 2 * q:2 * q + 2, :], ALU.add))
            else:
                m.step(dve.tensor_tensor(summed[:, 2 * q:2 * q + 2, :], two, out_scale[:, :].unsqueeze(1).broadcast_to((P, 2, D)), ALU.mult))
            m.wait_steps(dve)
            dve.scalar_tensor_tensor(m.X[:, 2 * q:2 * q + 2, :], summed[:, 2 * q:2 * q + 2, :], gate, m.X[:, 2 * q:2 * q + 2, :], ALU.mult, ALU.add).then_inc(m.x_done, 2)

    def tensor(pe):
        pe.wait_ge(m.x_done, m.x_at(stage, 0))
        for g in range(NG):
            if g:
                pe.wait_ge(xt.lo_ready, xt.lo_at(g))
            xt.tensor(pe, g, lambda j: m.xn_all[:, G * g + j, :])
            if experts:
                pe.wait_ge(xt.lo_ready, xt.lo_at(g + 1))
                pe.wait_ge(small_lo, 2)
                for j in range(G):
                    for c in range(KC):
                        mm = split_matmul(pe, m.bank[g][:, j * E:(j + 1) * E], (m.xt_hi[:, c, G * g + j, :], m.xt_lo[:, c, G * g + j, :]),
                                          (cen_hi[:, c, :], cen_lo[:, c, :]), c == 0, c == KC - 1)
                mm.then_inc(routed, 1)
                pe.wait_ge(gates_lo, g + 1)
                for j in range(G):
                    mm = pe.transpose(m.bank[2 + g][0:2 * GE, j * P:(j + 1) * P], f(parts[:, j, :, :]).rearrange("p k e -> p (k e)"), m.ident)
                mm.then_inc(turned, 1)
        if experts:
            pe.wait_ge(gates_t_ready, NG)
            for b in range(NB):
                pe.matmul(acc(b), gates_t[:, b, :], b2_hi[:, :], start=b % 2 == 0, stop=False, skip_group_check=True)
                pe.matmul(acc(b), gates_t[:, b, :], b2_lo[:, :], start=False, stop=False, skip_group_check=True)

        def first_products(c):
            pe.wait_ge(in_lo, c + 1)
            for t in range(2):
                after(pe, gated_ready if not experts else h_ready, 2 * (c - 1) + t + 1)
                for k in range(KC):
                    w = slice(k * P, (k + 1) * P)
                    mm = split_matmul(pe, m.bank[t][:, :], (hi[c % 2][:, w], lo[c % 2][:, w]), (m.xt_hi[:, k, side(t), :], m.xt_lo[:, k, side(t), :]), k == 0, k == KC - 1)
                if not experts:
                    mm.then_inc(h_raw, 1)
                    after(pe, u_ready, 2 * (c - 1) + t + 1)
                    for k in range(KC):
                        w = slice((KC + k) * P, (KC + k + 1) * P)
                        mm = split_matmul(pe, m.bank[2 + t][:, :], (hi[c % 2][:, w], lo[c % 2][:, w]), (m.xt_hi[:, k, side(t), :], m.xt_lo[:, k, side(t), :]), k == 0, k == KC - 1)
                    mm.then_inc(u_raw, 1)
                else:
                    after(pe, gated_ready, 2 * (c - 1) + t + 1)
                    pe.matmul(m.bank[2 + t][:, :], hi[c % 2][0:2 * GE, KC * P:(KC + 1) * P], gates_t[:, side(t), :], start=True, stop=True).then_inc(u_raw, 1)
                    mm.then_inc(h_raw, 1)

        def second_products(c):
            pe.wait_ge(out_lo, c + 1)
            for b in range(NB):
                if b % G == 0:
                    pe.wait_ge(h_lo_ready, 2 * c + b // G + 1)
                for n, (x, w) in enumerate(((h_lo, hi), (h_hi, lo), (h_hi, hi))):
                    start = not experts and c == 0 and n == 0 and b % 2 == 0
                    mm = pe.matmul(acc(b), x[c % 2][:, b, :], w[c % 2][:, IN:COLS], start=start, stop=c == chunks - 1 and n == 2, skip_group_check=True)
            mm.then_inc(used, 1)

        pe.wait_ge(xt.lo_ready, xt.lo_at(NG))
        first_products(0)
        for c in range(1, chunks):
            first_products(c)
            second_products(c - 1)
        second_products(chunks - 1)

    return {"load": load, "sync": sync, "gpsimd": gpsimd, "scalar": scalar, "vector": vector, "tensor": tensor}


def l2_attention(m, stage):
    NEG = -1e30
    s = lambda x: m.sem(f"l2a_{x}")
    norm = Norm(m, stage)
    mask_raw = m.sb("l2a_mask_raw", [P, NB, P], U8)
    mask = m.work([P, NB, P])
    below = m.work([P, NB, P])
    valid = m.sb("l2a_valid", [P, NB])
    valid_tg = m.sb("l2a_valid_tg", [P, NB])
    xt = m.work([P, KC, G, P])
    kept = m.work([P, G, P])
    masked = m.work([P, G, P])
    top = m.work([P, G])
    neg_top = m.work([P, G])
    expd = m.work([P, G, P])
    total = m.work([P, G])
    inv = m.work([P, G])
    weight = m.work([P, G])
    probs_t = m.work([P, G, P])
    mask_in, mask_ready, below_ready = s("mask_in"), s("mask"), s("below")
    xt_raw, xt_ready, scored, neg_ready = s("xt_raw"), s("xt"), s("scored"), s("neg")
    exp_ready, turned, probs_ready, out_ready = s("exp"), s("turned"), s("probs"), s("out")
    wide = lambda bank: bank[:, :].rearrange("p (j n) -> p j n", j=G)

    def load(sp):
        sp.dma_start(mask_raw[:, :, :], m.dram["l2a_mask"].rearrange("a (b n) -> a b n", b=NB).broadcast_to((P, NB, P))).then_inc(mask_in, 16)

    def gpsimd(pool):
        pool.wait_ge(mask_in, 16)
        pool.wait_ge(m.x_done, m.x_at(stage, 0))
        pool.tensor_copy(mask[:, :, :], mask_raw[:, :, :]).then_inc(mask_ready, 1)
        pool.wait_ge(mask_ready, 1)
        pool.tensor_scalar(below[:, :, :], mask[:, :, :], -1.0, -NEG, ALU.add, ALU.mult).then_inc(below_ready, 1)
        for g in range(NG):
            norm.gpsimd(pool, g)

    def scalar(act):
        for g in range(NG):
            act.wait_ge(m.x_done, m.x_at(stage, G * g))
            act.wait_ge(xt_raw, g + 1)
            for c in range(KC):
                act.activation(xt[:, c, :, :], wide(m.bank[c]), ACT.Copy).then_inc(xt_ready, 1)
            act.wait_ge(neg_ready, g + 1)
            for j in range(G):
                act.activation(expd[:, j, :], masked[:, j, :], ACT.Exp, bias=neg_top[:, j:j + 1], accum_out=total[:, j:j + 1]).then_inc(exp_ready, 1)
            act.wait_ge(turned, g + 1)
            act.activation(probs_t[:, :, :], wide(m.bank[3]), ACT.Copy).then_inc(probs_ready, 1)

    def vector(dve):
        dve.wait_ge(mask_ready, 1)
        m.step(dve.reduce_max(valid[:, :], mask[:, :, :], AX_X))
        m.wait_steps(dve)
        m.step(dve.tensor_scalar(valid_tg[:, :], valid[:, :], m.tg[:, 2:3], None, ALU.mult))
        for g in range(NG):
            norm.vector(dve, g, lambda j: m.xn[:, j, :])
            dve.wait_ge(scored, g + 1)
            dve.wait_ge(below_ready, 1)
            m.step(dve.scalar_tensor_tensor(kept[:, :, :], wide(m.bank[2]), 1.0 / 16.0, mask[:, G * g:G * g + G, :], ALU.mult, ALU.mult))
            m.wait_steps(dve)
            m.step(dve.tensor_tensor(masked[:, :, :], kept[:, :, :], below[:, G * g:G * g + G, :], ALU.add))
            m.wait_steps(dve)
            m.step(dve.reduce_max(top[:, :], masked[:, :, :], AX_X))
            m.wait_steps(dve)
            dve.tensor_scalar(neg_top[:, :], top[:, :], -1.0, None, ALU.mult).then_inc(neg_ready, 1)
            dve.wait_ge(exp_ready, G * g + G)
            m.step(dve.reciprocal(inv[:, :], total[:, :]))
            m.wait_steps(dve)
            m.step(dve.tensor_tensor(weight[:, :], inv[:, :], valid_tg[:, G * g:G * g + G], ALU.mult))
            m.wait_steps(dve)
            for j in range(G):
                b = G * g + j
                dve.wait_ge(out_ready, b + 1)
                dve.scalar_tensor_tensor(m.X[:, b, :], m.bank[4 + j][:, 0:D], weight[:, j:j + 1], m.X[:, b, :], ALU.mult, ALU.add).then_inc(m.x_done, 1)

    def tensor(pe):
        pe.wait_ge(m.ctx_in, 32)
        for g in range(NG):
            pe.wait_ge(m.x_done, m.x_at(stage, G * g))
            pe.wait_ge(norm.xn, norm.xn_at(G * g + G))
            for c in range(KC):
                for j in range(G):
                    mm = pe.transpose(m.bank[c][:, j * P:(j + 1) * P], m.xn[:, j, c * P:(c + 1) * P], m.ident)
            mm.then_inc(xt_raw, 1)
            pe.wait_ge(xt_ready, KC * g + KC)
            for j in range(G):
                for c in range(KC):
                    mm = pe.matmul(m.bank[2][:, j * P:(j + 1) * P], xt[:, c, j, :], m.CT[:, c, G * g + j, :], start=c == 0, stop=c == KC - 1)
            mm.then_inc(scored, 1)
            for j in range(G):
                pe.wait_ge(exp_ready, G * g + j + 1)
                mm = pe.transpose(m.bank[3][:, j * P:(j + 1) * P], expd[:, j, :], m.ident)
            mm.then_inc(turned, 1)
            pe.wait_ge(probs_ready, g + 1)
            for j in range(G):
                pe.matmul(m.bank[4 + j][:, 0:D], probs_t[:, j, :], m.CN[:, G * g + j, :], start=True, stop=True).then_inc(out_ready, 1)

    return {"load": load, "gpsimd": gpsimd, "scalar": scalar, "vector": vector, "tensor": tensor}


def l3_attention(m, stage):
    T = P + 1
    NEG = -1e38
    s = lambda x: m.sem(f"l3a_{x}")
    norm = Norm(m, stage)
    wu = m.sb("l3a_wu", [P, KC, 2])
    full = lambda: [m.work([P, NB, T]) for _ in range(KC)]
    plain = lambda: [m.work([P, NB, P]) for _ in range(KC)]
    k, decay, o, fade, enter, entered = full(), full(), full(), full(), full(), full()
    p_sum, q_sum = k, decay
    lead, a, e = plain(), plain(), plain()
    flat = lambda t: t[:, :, :].rearrange("p b t -> p (b t)")
    wu_in, edges, decay_ready, xt_raw, k_ready = s("wu_in"), s("edges"), s("decay"), s("xt_raw"), s("k")
    diffs, exps, entered_ready = s("diffs"), s("exps"), s("entered")
    pool_terms, y_ready, turned = s("pool_terms"), s("y"), s("turned")

    def load(sp):
        sp.dma_start(wu[:, :, :], m.dram["l3a_wu"].rearrange("p (c k) -> p c k", c=KC)).then_inc(wu_in, 16)

    def gpsimd(pool):
        pool.wait_ge(wu_in, 16)
        pool.wait_ge(m.x_done, m.x_at(stage, 0))
        for c in range(KC):
            pool.memset(k[c][:, :, 0:1], NEG).then_inc(edges, 1)
            pool.memset(decay[c][:, :, 0:1], NEG).then_inc(edges, 1)
            pool.memset(fade[c][:, :, 0:1], 0.0).then_inc(edges, 1)
            pool.memset(enter[c][:, :, 0:1], 0.0).then_inc(edges, 1)
            pool.memset(entered[c][:, :, 0:1], 0.0).then_inc(edges, 1)
            pool.memset(o[c][:, :, :], 0.0).then_inc(edges, 1)
        pool.wait_ge(edges, 6 * KC)
        for c in range(KC):
            pool.tensor_scalar(decay[c][:, :, 1:T], o[c][:, :, 1:T], wu[:, c, 0:1], None, ALU.add).then_inc(decay_ready, 1)
        for g in range(NG):
            norm.gpsimd(pool, g)
        for c in range(KC):
            v = m.CT[:, c, :, :]
            pool.wait_ge(exps, 4 * c + 2)
            pool.tensor_tensor(entered[c][:, :, 1:T], enter[c][:, :, 1:T], v, ALU.mult).then_inc(entered_ready, 1)
            pool.wait_ge(exps, 4 * c + 4)
            pool.tensor_tensor(lead[c][:, :, :], e[c][:, :, :], v, ALU.mult).then_inc(pool_terms, 1)

    def scalar(act):
        act.wait_ge(m.x_done, m.x_at(stage, 0))
        for g in range(NG):
            act.wait_ge(xt_raw, g + 1)
            for c in range(KC):
                act.activation(k[c][:, G * g:G * g + G, 1:T], m.bank[2 * g + c][:, :].rearrange("p (j n) -> p j n", j=G), ACT.Copy).then_inc(k_ready, 1)
        for c in range(KC):
            for n, (src, dst) in enumerate(((fade[c][:, :, 1:T],) * 2, (enter[c][:, :, 1:T],) * 2, (a[c][:, :, :],) * 2, (e[c][:, :, :],) * 2)):
                act.wait_ge(diffs, 4 * c + n + 1)
                act.activation(dst, src, ACT.Exp).then_inc(exps, 1)

    def vector(dve):
        for g in range(NG):
            norm.vector(dve, g, lambda j: m.xn_all[:, G * g + j, :])
        dve.wait_ge(k_ready, NG * KC)
        dve.wait_ge(decay_ready, KC)
        dve.wait_ge(wu_in, 16)
        for c in range(KC):
            m.step(dve.tensor_tensor_scan(flat(o[c]), flat(decay[c]), flat(k[c]), NEG, ALU.add, ALU.max))
            kc, w, u = k[c][:, :, 1:T], wu[:, c, 0:1], wu[:, c, 1:2]
            before, now = o[c][:, :, 0:P], o[c][:, :, 1:T]
            m.wait_steps(dve)
            dve.scalar_tensor_tensor(fade[c][:, :, 1:T], before, w, now, ALU.add, ALU.subtract).then_inc(diffs, 1)
            dve.tensor_tensor(enter[c][:, :, 1:T], kc, now, ALU.subtract).then_inc(diffs, 1)
            m.step(dve.scalar_tensor_tensor(lead[c][:, :, :], kc, u, before, ALU.add, ALU.max))
            m.wait_steps(dve)
            dve.tensor_tensor(a[c][:, :, :], before, lead[c][:, :, :], ALU.subtract).then_inc(diffs, 1)
            dve.scalar_tensor_tensor(e[c][:, :, :], kc, u, lead[c][:, :, :], ALU.add, ALU.subtract).then_inc(diffs, 1)
        for c in range(KC):
            dve.wait_ge(exps, 4 * c + 2)
            m.step(dve.tensor_tensor_scan(flat(q_sum[c]), flat(fade[c]), flat(enter[c]), 0.0, ALU.mult, ALU.add))
            dve.wait_ge(entered_ready, c + 1)
            dve.wait_ge(exps, 4 * c + 4)
            m.step(dve.tensor_tensor_scan(flat(p_sum[c]), flat(fade[c]), flat(entered[c]), 0.0, ALU.mult, ALU.add))
            dve.wait_ge(exps, 4 * c + 4)
            m.wait_steps(dve)
            num, den = fade[c][:, :, 1:T], enter[c][:, :, 1:T]
            m.wait_steps(dve)
            m.step(dve.tensor_tensor(den, a[c][:, :, :], q_sum[c][:, :, 0:P], ALU.mult))
            m.step(dve.tensor_tensor(num, a[c][:, :, :], p_sum[c][:, :, 0:P], ALU.mult))
            m.wait_steps(dve)
            m.step(dve.tensor_tensor(den, den, e[c][:, :, :], ALU.add))
            dve.wait_ge(pool_terms, c + 1)
            m.wait_steps(dve)
            m.step(dve.tensor_tensor(num, num, lead[c][:, :, :], ALU.add))
            m.wait_steps(dve)
            m.step(dve.reciprocal(den, den))
            m.wait_steps(dve)
            m.wait_steps(dve)
            dve.tensor_tensor(a[c][:, :, :], num, den, ALU.mult).then_inc(y_ready, 1)
        for q in range(NB // 2):
            dve.wait_ge(turned, q + 1)
            dve.scalar_tensor_tensor(m.X[:, 2 * q:2 * q + 2, :], m.bank[4 + q][:, :].rearrange("p (j n) -> p j n", j=2), m.tg[:, 3:4],
                                     m.X[:, 2 * q:2 * q + 2, :], ALU.mult, ALU.add).then_inc(m.x_done, 2)

    def tensor(pe):
        pe.wait_ge(m.x_done, m.x_at(stage, 0))
        for g in range(NG):
            pe.wait_ge(norm.xn, norm.xn_at(G * g + G))
            for c in range(KC):
                for j in range(G):
                    mm = pe.transpose(m.bank[2 * g + c][:, j * P:(j + 1) * P], m.xn_all[:, G * g + j, c * P:(c + 1) * P], m.ident)
            mm.then_inc(xt_raw, 1)
        pe.wait_ge(y_ready, KC)
        for q in range(NB // 2):
            for j in range(2):
                for c in range(KC):
                    mm = pe.transpose(m.bank[4 + q][:, j * D + c * P:j * D + (c + 1) * P], a[c][:, 2 * q + j, :], m.ident)
            mm.then_inc(turned, 1)

    return {"load": load, "gpsimd": gpsimd, "scalar": scalar, "vector": vector, "tensor": tensor}


def program(nc, dram, out):
    with ExitStack() as ctx:
        m = Machine(nc, ctx, dram)
        builders = [
            l0_attention,
            lambda m, n: adapters(m, n, "l0f", True),
            l1_attention,
            lambda m, n: feed_forward(m, n, "l1f", dram["l1f_w"].shape[0], True),
            l2_attention,
            lambda m, n: feed_forward(m, n, "l2f", dram["l2f_w"].shape[0], False),
            l3_attention,
            lambda m, n: adapters(m, n, "l3f", False),
        ]
        stages = []
        for n, build in enumerate(builders[:STAGES]):
            m.used = {"f": 0, "r": 0}
            stages.append(build(m, n))
        stored = m.sem("stored")
        block = ctx.enter_context(nc.Block())

        @block.sync
        def _(sp):
            x = dram["x"].rearrange("b s d -> s b d")
            sp.dma_start(m.X[:, 0:G, :], x[:, 0:G, :]).then_inc(m.x_done, 16)
            sp.dma_start(m.CT[:, :, :, :], dram["ctx_t"].rearrange("p (c b n) -> p c b n", c=KC, b=NB)).then_inc(m.ctx_in, 16)
            sp.dma_start(m.const[:, :], dram["const"]).then_inc(m.const_in, 16)
            sp.dma_start(m.gates_raw[:, :], dram["gates"].broadcast_to((P, 8))).then_inc(m.const_in, 16)
            sp.dma_start(m.CN[:, :, :], dram["ctx"].rearrange("b s d -> s b d")).then_inc(m.ctx_in, 16)
            sp.dma_start(m.X[:, G:NB, :], x[:, G:NB, :]).then_inc(m.x_done, 16)
            for stage in stages:
                stage["load"](sp)
            for stage in stages:
                if "sync" in stage:
                    stage["sync"](sp)
            y = out.rearrange("b s d -> s b d")
            for g in range(NG):
                sp.wait_ge(m.x_done, m.x_at(len(stages) - 1, G * g + G))
                sp.dma_start(y[:, G * g:G * g + G, :], m.X[:, G * g:G * g + G, :]).then_inc(stored, 16)
            sp.wait_ge(stored, 16 * NG)

        @block.gpsimd
        def _(pool):
            pool.wait_ge(m.const_in, 32)
            for stage in stages:
                stage["gpsimd"](pool)

        @block.scalar
        def _(act):
            act.wait_ge(m.const_in, 32)
            act.activation(m.tg[:, :], m.gates_raw[:, :], ACT.Tanh).then_inc(m.tg_ready, 1)
            for stage in stages:
                stage["scalar"](act)

        @block.vector
        def _(dve):
            dve.wait_ge(m.const_in, 32)
            for stage in stages:
                stage["vector"](dve)

        @block.tensor
        def _(pe):
            for stage in stages:
                stage["tensor"](pe)


def widths_on_partitions(w):
    w = np.asarray(w)
    return np.ascontiguousarray(w.reshape(-1, P, w.shape[1]).transpose(1, 0, 2).reshape(P, -1))


def by_rank(w):
    return np.asarray(w).transpose(1, 0, 2).reshape(D, -1)


def constants():
    rows = np.arange(P)
    c = np.zeros((P, CONST_COLS), np.float32)
    c[:, 0:P] = np.eye(P)
    c[:, P:2 * P] = rows[:, None] // 16 == rows[None, :] // 16
    c[:, 2 * P:2 * P + 8] = rows[:, None] // 16 == np.arange(8)[None, :]
    c[:, 2 * P + 8:2 * P + 16] = -0.5
    c[:, 2 * P + 16] = rows % 64 == 48
    return c


def stack_selectors():
    sel = np.zeros((P, 4, 4, P), np.float32)
    for kind, places in enumerate(((0, 2), (1,), (0, 1), (2,))):
        for pair in range(4):
            for a in range(2):
                for t in places:
                    for d in range(16):
                        sel[32 * pair + 16 * a + d, kind, pair, 64 * a + 16 * t + d] = 1
    return sel.reshape(P, -1)


def output_selectors():
    sel = np.zeros((P, 2, 2, P), np.float32)
    for h in range(8):
        for d in range(16):
            for kind in range(2):
                sel[32 * (h // 2) + 16 * kind + d, kind, h % 2, 16 * h + d] = 1
    return sel.reshape(P, -1)


def padded(w, n, axis):
    w = np.asarray(w)
    fill = list(w.shape)
    fill[axis] = n - w.shape[axis]
    return np.concatenate([w, np.zeros(fill, w.dtype)], axis=axis)


def expert_chunks(a):
    w1 = np.concatenate([np.asarray(a["L1_ffn_routed_w1"]), np.asarray(a["L1_ffn_shared_w1"])])
    w2 = np.concatenate([np.asarray(a["L1_ffn_routed_w2"]), np.asarray(a["L1_ffn_shared_w2"])])
    b1 = np.concatenate([np.asarray(a["L1_ffn_routed_b1"]), np.asarray(a["L1_ffn_shared_b1"])])
    b2 = np.concatenate([np.asarray(a["L1_ffn_routed_b2"]), np.asarray(a["L1_ffn_shared_b2"])])
    n, _, f = w1.shape
    chunks = -(-n * f // P)
    w1 = padded(w1.transpose(1, 0, 2).reshape(D, n * f), chunks * P, 1).reshape(KC, P, chunks, P)
    w2 = padded(w2.reshape(n * f, D), chunks * P, 0).reshape(chunks, P, D)
    expert = np.arange(chunks * P) // f
    sel = np.zeros((P, chunks * P), np.float32)
    for part in range(2):
        sel[part * n:(part + 1) * n] = expert[None, :] == np.arange(n)[:, None]
    blob = np.concatenate([w1[0].transpose(1, 0, 2), w1[1].transpose(1, 0, 2), sel.reshape(P, chunks, P).transpose(1, 0, 2), w2], axis=2)
    return blob, padded(b1.reshape(-1), chunks * P, 0).reshape(chunks, P).T, np.concatenate([b2, b2])


def swiglu_chunks(a):
    gate, up, down = (np.asarray(a[f"L2_ffn_{n}_w"]) for n in ("gate", "up", "down"))
    chunks = -(-gate.shape[0] // P)
    first = [padded(w, chunks * P, 0).reshape(chunks, P, KC, P).transpose(0, 3, 2, 1).reshape(chunks, P, KC * P) for w in (gate, up)]
    second = padded(down, chunks * P, 1).T.reshape(chunks, P, D)
    scales = np.stack([padded(a[f"L2_ffn_{n}_s"], chunks * P, 0).reshape(chunks, P).T for n in ("gate", "up")], axis=1)
    return np.concatenate(first + [second], axis=2), scales.reshape(P, -1)


def layouts(a):
    row = lambda v: np.asarray(v).reshape(1, -1)
    l1f_w, l1f_b1, l1f_b2 = expert_chunks(a)
    l2f_w, l2f_scales = swiglu_chunks(a)
    return {
        "x": a["x"],
        "ctx": a["ctx_2048"],
        "ctx_t": np.ascontiguousarray(np.asarray(a["ctx_2048"]).transpose(2, 0, 1).reshape(KC, P, NB, P).transpose(1, 0, 2, 3).reshape(P, -1)),
        "const": constants(),
        "gates": row(np.concatenate([a["g_xattn"], a["g_ffn"]])),
        "l0a_w": widths_on_partitions(np.concatenate([np.asarray(a["L0_xattn_Wkv"]).T, np.asarray(a["L0_xattn_Wq"]).T,
                                                      np.asarray(a["L0_xattn_Wg"]).T, np.asarray(a["L0_xattn_Wo"]).T], axis=1)),
        "l0a_bg": row(a["L0_xattn_bg"]),
        "l0f_w": widths_on_partitions(np.concatenate([by_rank(a["L0_ffn_Wd"]), np.asarray(a["L0_ffn_Wr"])], axis=1)),
        "l0f_up": np.asarray(a["L0_ffn_Wu"]).reshape(P, D),
        "l0f_bias": row(np.concatenate([np.asarray(a["L0_ffn_bd"]).reshape(-1), np.asarray(a["L0_ffn_br"])])),
        "l0f_up_bias": a["L0_ffn_bu"],
        "l1a_sel": stack_selectors(),
        "l1a_out_sel": output_selectors(),
        "l1a_gamma": row(a["L1_xattn_gamma"]),
        "l1f_w": l1f_w,
        "l1f_b1": l1f_b1,
        "l1f_b2": l1f_b2,
        "l1f_cen": widths_on_partitions(np.asarray(a["L1_ffn_centroids"]).T),
        "l1f_bias": row(a["L1_ffn_bias"]),
        "l2a_mask": row(a["mask_BxS2_bk0"]),
        "l2f_w": l2f_w,
        "l2f_scales": l2f_scales,
        "l2f_out_scale": row(a["L2_ffn_down_s"]),
        "l3a_wu": widths_on_partitions(np.stack([np.asarray(a["L3_xattn_w"]), np.asarray(a["L3_xattn_u"])], axis=1)),
        "l3f_w": widths_on_partitions(np.concatenate([by_rank(a["L3_ffn_experts_down"]), np.asarray(a["L3_ffn_router_w"]).T], axis=1)),
        "l3f_up": np.asarray(a["L3_ffn_experts_up"]).reshape(P, D),
    }


def kernel(**inputs):
    import concourse.bacc as bacc
    from concourse.bass_utils import run_bass_kernel_spmd

    arrays = {name: np.ascontiguousarray(v) for name, v in layouts(inputs).items()}
    nc = bacc.Bacc("TRN2", target_bir_lowering=False, num_devices=1)
    dram = {name: nc.dram_tensor(f"in_{name}", v.shape, mybir.dt.from_np(v.dtype), kind="ExternalInput").ap() for name, v in arrays.items()}
    out = nc.dram_tensor("out_x", (NB, P, D), F32, kind="ExternalOutput").ap()
    program(nc, dram, out)
    got = run_bass_kernel_spmd(nc, [{f"in_{name}": v for name, v in arrays.items()}], core_ids=[0])
    return got.results[0]["out_x"]
```

```python
from contextlib import ExitStack

import numpy as np

import concourse.bass as bass
from concourse import mybir

ALU = mybir.AluOpType
ACT = mybir.ActivationFunctionType
F32 = mybir.dt.float32
F32R = mybir.dt.float32r
U8 = mybir.dt.uint8
AX_X = mybir.AxisListType.X

P = 128
NB = 8
D = 256
KC = D // P
G = 4
NG = NB // G
BIG = 3.0e38
LN_EPS = 1e-5

STAGES = 8


class Machine:

    def __init__(self, nc, ctx, dram):
        self.nc, self.ctx, self.dram = nc, ctx, dram

        self.X = self.sb("X", [P, NB, D])
        self.CT = self.sb("CT", [P, KC, NB, P])
        self.CN = self.sb("CN", [P, NB, D])
        self.const = self.sb("const", [P, CONST_COLS])
        self.ident = self.const[:, 0:P]
        self.blockdiag = self.const[:, P:2 * P]
        self.headcol = self.const[:, 2 * P:2 * P + 8]
        self.minus_half = self.const[:, 2 * P + 8:2 * P + 16]
        self.one_row = self.const[:, 2 * P + 16:2 * P + 17]
        self.gates_raw = self.sb("gates_raw", [P, 8])
        self.tg = self.sb("tg", [P, 8])
        self.xn = self.sb("xn", [P, G, D])
        self.xn_all = self.sb("xn_all", [P, NB, D])
        self.stats = self.sb("stats", [P, G, 6])
        self.mv = self.sb("mv", [P, G, 2])
        self.veps = self.sb("veps", [P, G])
        self.rstd = self.sb("rstd", [P, G])
        self.xt_hi = self.sb("xt_hi", [P, KC, NB, P], F32R)
        self.xt_lo = self.sb("xt_lo", [P, KC, NB, P], F32R)
        self.bank = [ctx.enter_context(nc.psum_tensor(f"bank{i}", [P, 512], F32)) for i in range(8)]

        self.arena_f = self.sb("arena_f", [P, ARENA_F])
        self.arena_r = self.sb("arena_r", [P, ARENA_R], F32R)
        self.used = {"f": 0, "r": 0}
        self.ring_raw = [self.sb(f"ring_raw{i}", [P, 6 * P]) for i in range(2)]
        self.ring_hi = [self.sb(f"ring_hi{i}", [P, 6 * P], F32R) for i in range(2)]
        self.ring_lo = [self.sb(f"ring_lo{i}", [P, 6 * P], F32R) for i in range(2)]
        self.x_done = self.sem("x_done")
        self.x_in = [self.sem(f"x_in{g}") for g in range(NG)]
        self.vector_steps = self.sem("vector_steps")
        self.steps = 0
        self.norm_mv, self.norm_veps = self.sem("norm_mv"), self.sem("norm_veps")
        self.norm_rstd, self.norm_xn = self.sem("norm_rstd"), self.sem("norm_xn")
        self.xt_raw, self.xt_hi_ready, self.xt_lo_ready = self.sem("xt_raw"), self.sem("xt_hi"), self.sem("xt_lo")
        self.transposed = 0
        self.const_in = self.sem("const_in")
        self.ctx_in = self.sem("ctx_in")
        self.cn_in = self.sem("cn_in")
        self.tg_ready = self.sem("tg_ready")

    def step(self, instruction):
        instruction.then_inc(self.vector_steps, 1)
        self.steps += 1

    def wait_steps(self, dve):
        dve.wait_ge(self.vector_steps, self.steps)

    def sb(self, name, shape, dt=F32):
        return self.ctx.enter_context(self.nc.sbuf_tensor(name, shape, dt))

    def work(self, shape, dt=F32):
        size = int(np.prod(shape[1:]))
        arena, name = (self.arena_r, "r") if dt == F32R else (self.arena_f, "f")
        a = self.used[name]
        self.used[name] += size
        view = arena[0:shape[0], a:a + size]
        if len(shape) > 2:
            dims = " ".join(f"d{n}" for n in range(len(shape) - 1))
            view = view.rearrange(f"p ({dims}) -> p {dims}", **{f"d{n}": v for n, v in enumerate(shape[1:])})
        return view

    def sem(self, name):
        return self.ctx.enter_context(self.nc.semaphore(name))

    def x_at(self, stage, b):
        return NB * stage + b


CONST_COLS = 2 * P + 20
ARENA_F = 19000
ARENA_R = 9216


def f(view):
    return view.bitcast(F32)


def split_matmul(pe, out, lhs, rhs, start, stop, **kw):
    (lh, ll), (rh, rl) = lhs, rhs
    pe.matmul(out, ll, rh, start=start, stop=False, **kw)
    pe.matmul(out, lh, rl, start=False, stop=False, **kw)
    return pe.matmul(out, lh, rh, start=False, stop=stop, **kw)


class Norm:

    def __init__(self, m, stage):
        self.m, self.stage = m, stage
        self.passed = stage * NG
        self.mv, self.veps, self.rstd, self.xn = m.norm_mv, m.norm_veps, m.norm_rstd, m.norm_xn

    def xn_at(self, n):
        return G * self.passed + n

    def vector(self, dve, g, out):
        m = self.m
        for j in range(G):
            if self.stage:
                dve.wait_ge(m.x_done, m.x_at(self.stage - 1, G * g + j + 1))
            else:
                dve.wait_ge(m.x_in[g], 16)
            m.step(dve.bn_stats(m.stats[:, j, :], m.X[:, G * g + j, :]))
        for j in range(G):
            m.wait_steps(dve)
            dve.bn_aggr(m.mv[:, j, :], m.stats[:, j, :]).then_inc(self.mv, 1)
        dve.wait_ge(self.rstd, self.passed + g + 1)
        for j in range(G):
            b = G * g + j
            dve.tensor_scalar(out(j), m.X[:, b, :], m.mv[:, j, 0:1], m.rstd[:, j:j + 1],
                              ALU.subtract, ALU.mult).then_inc(self.xn, 1)

    def gpsimd(self, pool, g):
        m = self.m
        pool.wait_ge(self.mv, self.xn_at(G * g + G))
        pool.tensor_scalar(m.veps[:, :], m.mv[:, :, 1], LN_EPS, None, ALU.add).then_inc(self.veps, 1)
        pool.wait_ge(self.veps, self.passed + g + 1)
        pool.tensor_tensor(m.rstd[:, :], m.veps[:, :], m.minus_half[:, 0:G], ALU.pow).then_inc(self.rstd, 1)


class Transposed:

    def __init__(self, m, banks, norm, hi=None, lo=None):
        self.m, self.banks, self.norm = m, banks, norm
        self.hi = hi or (lambda g, c: m.xt_hi[:, c, 0:G, :])
        self.lo = lo or (lambda g, c: m.xt_lo[:, c, 0:G, :])
        self.passed = m.transposed
        m.transposed += NG
        self.raw, self.hi_ready, self.lo_ready = m.xt_raw, m.xt_hi_ready, m.xt_lo_ready

    def lo_at(self, groups):
        return KC * (self.passed + groups)

    def tensor(self, pe, g, xn):
        pe.wait_ge(self.norm.xn, self.norm.xn_at(G * g + G))
        for c in range(KC):
            for j in range(G):
                mm = pe.transpose(self.banks[c][:, j * P:(j + 1) * P], xn(j)[:, c * P:(c + 1) * P], self.m.ident)
        mm.then_inc(self.raw, 1)

    def bank(self, c):
        return self.banks[c][:, :].rearrange("p (j n) -> p j n", j=G)

    def scalar(self, act, g):
        act.wait_ge(self.raw, self.passed + g + 1)
        for c in range(KC):
            act.activation(self.hi(g, c), self.bank(c), ACT.Copy).then_inc(self.hi_ready, 1)

    def vector(self, dve, g):
        for c in range(KC):
            dve.wait_ge(self.hi_ready, KC * (self.passed + g) + c + 1)
            dve.tensor_tensor(self.lo(g, c), self.bank(c), f(self.hi(g, c)), ALU.subtract).then_inc(self.lo_ready, 1)


def after(engine, sem, count):
    if not (isinstance(count, int) and count <= 0):
        engine.wait_ge(sem, count)


def l0_attention(m, stage):
    HD = 16
    s = lambda name: m.sem(f"l0a_{name}")
    norm = Norm(m, stage)
    cols = {"kv": (0, 2 * D), "q": (2 * D, 3 * D), "g": (3 * D, 4 * D), "o": (4 * D, 5 * D)}
    W = m.work([P, KC, 5 * D])
    W_hi = m.work([P, KC, 5 * D], F32R)
    W_lo = m.work([P, KC, 5 * D], F32R)
    bg = m.work([P, D])
    ct_hi = m.work([P, KC, G, P], F32R)
    ct_lo = m.work([P, KC, G, P], F32R)
    k_min = m.work([P, G, D])
    k_exp = m.work([P, G, D])
    k_feat = m.work([P, G, D])
    v_one = m.work([P, G, KC, P + 1])
    q_min = m.work([P, KC, G * P])
    q_exp = m.work([P, KC, G * P])
    q_feat = m.work([P, KC, G * P])
    g_sum = m.work([P, G, D])
    g_tanh = m.work([P, G, D])
    summary = m.work([P, G, KC, P + 8])
    z_den = m.work([P, G, KC, 8])
    z = m.work([P, G, KC, 8])
    attn = m.work([P, G, D])
    gated = m.work([P, G, D])
    gt_hi = m.work([P, G, KC, P], F32R)
    gt_lo = m.work([P, G, KC, P], F32R)
    half_tg = m.work([P, 1])
    xn = [m.xn, m.work([P, G, D])]

    kv_w_in, w_in, w_hi_ready, w_lo_ready, bg_in, ones_ready = s("kv_w_in"), s("w_in"), s("w_hi"), s("w_lo"), s("bg_in"), s("ones")
    ct_hi_ready, ct_ready = s("ct_hi"), s("ct")
    kv_proj, k_min_ready, k_exp_ready, k_ready, v_ready = s("kv_proj"), s("k_min"), s("k_exp"), s("k"), s("v")
    q_proj, q_min_ready, q_exp_ready, q_ready = s("q_proj"), s("q_min"), s("q_exp"), s("q")
    g_proj, g_sum_ready, g_tanh_ready = s("g_proj"), s("g_sum"), s("g_tanh")
    kv_sum, summary_ready, num_ready = s("kv_sum"), s("summary"), s("num")
    attn_ready, gated_ready, gt_raw, gt_hi_ready, gt_lo_ready, out_ready = s("attn"), s("gated"), s("gt_raw"), s("gt_hi"), s("gt_lo"), s("out")

    kv_bank = [m.bank[0], m.bank[1]]
    xt = Transposed(m, [m.bank[2], m.bank[3]], norm)
    q_bank = [m.bank[4], m.bank[5]]
    g_bank = lambda j: m.bank[6 + j // 2][:, (j % 2) * D:(j % 2 + 1) * D]
    sum_bank = lambda j: m.bank[j % 2][:, :].rearrange("p (c n) -> p c n", c=KC)
    num_bank = lambda j: m.bank[2 + j % 2][:, :].rearrange("p (c n) -> p c n", c=KC)
    gt_bank = lambda j: m.bank[4 + j % 2][:, 0:D].rearrange("p (c n) -> p c n", c=KC)
    out_bank = lambda j: m.bank[6 + j % 2][:, 0:D]

    def load(sp):
        w = m.dram["l0a_w"].rearrange("p (c n) -> p c n", c=KC)
        x = m.dram["x"].rearrange("b s d -> s b d")
        sp.dma_start(m.CT[:, :, :, :], m.dram["ctx_t"].rearrange("p (c b n) -> p c b n", c=KC, b=NB)).then_inc(m.ctx_in, 16)
        sp.dma_start(W[:, :, 0:2 * D], w[:, :, 0:2 * D]).then_inc(kv_w_in, 16)
        sp.dma_start(m.X[:, 0:G, :], x[:, 0:G, :]).then_inc(m.x_in[0], 16)
        sp.dma_start(m.const[:, :], m.dram["const"]).then_inc(m.const_in, 16)
        sp.dma_start(m.gates_raw[:, :], m.dram["gates"].broadcast_to((P, 8))).then_inc(m.const_in, 16)
        sp.dma_start(W[:, :, 2 * D:5 * D], w[:, :, 2 * D:5 * D]).then_inc(w_in, 16)
        sp.dma_start(bg[:, :], m.dram["l0a_bg"].broadcast_to((P, D))).then_inc(bg_in, 16)
        sp.dma_start(m.X[:, G:NB, :], x[:, G:NB, :]).then_inc(m.x_in[1], 16)
        sp.dma_start(m.CN[:, :, :], m.dram["ctx"].rearrange("b s d -> s b d")).then_inc(m.cn_in, 16)

    def gpsimd(pool):
        pool.memset(v_one[:, :, :, P:P + 1], 1.0).then_inc(ones_ready, 1)
        pool.wait_ge(m.const_in, 32)
        for g in range(NG):
            norm.gpsimd(pool, g)
        pool.wait_ge(kv_proj, G)
        pool.wait_ge(m.ctx_in, 16)
        for c in range(KC):
            pool.tensor_copy(ct_hi[:, c, :, :], m.CT[:, c, G:NB, :]).then_inc(ct_hi_ready, 1)
            pool.wait_ge(ct_hi_ready, KC + c + 1)
            pool.tensor_tensor(ct_lo[:, c, :, :], m.CT[:, c, G:NB, :], f(ct_hi[:, c, :, :]), ALU.subtract).then_inc(ct_ready, 1)

    def scalar(act):
        def keys(g):
            for j in range(G):
                act.wait_ge(k_min_ready, G * g + j + 1)
                act.activation(k_exp[:, j, :], k_min[:, j, :], ACT.Exp).then_inc(k_exp_ready, 1)
                act.wait_ge(k_ready, G * g + j + 1)
                act.activation(v_one[:, j, :, 0:P], kv_bank[j % 2][:, D:2 * D].rearrange("p (c n) -> p c n", c=KC), ACT.Copy).then_inc(v_ready, 1)

        def queries(g):
            xt.scalar(act, g)
            for c in range(KC):
                act.wait_ge(q_min_ready, KC * g + c + 1)
                act.activation(q_exp[:, c, :], q_min[:, c, :], ACT.Exp).then_inc(q_exp_ready, 1)
            for h in range(0, G, 2):
                act.wait_ge(g_sum_ready, (G * g + h) // 2 + 1)
                act.activation(g_tanh[:, h:h + 2, :], g_sum[:, h:h + 2, :], ACT.Tanh, scale=0.5).then_inc(g_tanh_ready, 1)

        def gated_turned(g):
            for j in range(G):
                act.wait_ge(gt_raw, G * g + j + 1)
                act.activation(gt_hi[:, j, :, :], gt_bank(j), ACT.Copy).then_inc(gt_hi_ready, 1)

        act.wait_ge(m.ctx_in, 16)
        for c in range(KC):
            act.activation(ct_hi[:, c, :, :], m.CT[:, c, 0:G, :], ACT.Copy).then_inc(ct_hi_ready, 1)
        act.wait_ge(kv_w_in, 16)
        act.activation(W_hi[:, :, 0:2 * D], W[:, :, 0:2 * D], ACT.Copy).then_inc(w_hi_ready, 1)
        act.wait_ge(m.const_in, 32)
        act.activation(m.tg[:, :], m.gates_raw[:, :], ACT.Tanh).then_inc(m.tg_ready, 1)
        act.wait_ge(w_in, 16)
        act.activation(W_hi[:, :, 2 * D:5 * D], W[:, :, 2 * D:5 * D], ACT.Copy).then_inc(w_hi_ready, 1)
        act.wait_ge(ones_ready, 1)
        keys(0)
        for g in range(NG):
            queries(g)
            if g + 1 < NG:
                keys(g + 1)
            gated_turned(g)

    def vector(dve):
        def weights(n):
            a, b = ((0, 2 * D), (2 * D, 5 * D))[n]
            dve.wait_ge(w_hi_ready, n + 1)
            dve.tensor_tensor(W_lo[:, :, a:b], W[:, :, a:b], f(W_hi[:, :, a:b]), ALU.subtract).then_inc(w_lo_ready, 1)

        def keys(g):
            for j in range(G):
                dve.wait_ge(kv_proj, G * g + j + 1)
                dve.tensor_scalar(k_min[:, j, :], kv_bank[j % 2][:, 0:D], 0.0, None, ALU.min).then_inc(k_min_ready, 1)
                dve.wait_ge(k_exp_ready, G * g + j + 1)
                dve.scalar_tensor_tensor(k_feat[:, j, :], kv_bank[j % 2][:, 0:D], 0.0, k_exp[:, j, :], ALU.max, ALU.add).then_inc(k_ready, 1)

        def queries(g):
            xt.vector(dve, g)
            for c in range(KC):
                dve.wait_ge(q_proj, KC * g + c + 1)
                dve.tensor_scalar(q_min[:, c, :], q_bank[c][:, :], 0.0, None, ALU.min).then_inc(q_min_ready, 1)
                dve.wait_ge(q_exp_ready, KC * g + c + 1)
                dve.scalar_tensor_tensor(q_feat[:, c, :], q_bank[c][:, :], 0.0, q_exp[:, c, :], ALU.max, ALU.add).then_inc(q_ready, 1)
            dve.wait_ge(bg_in, 16)
            for h in range(0, G, 2):
                dve.wait_ge(g_proj, G * g + h + 2)
                dve.tensor_tensor(g_sum[:, h:h + 2, :], m.bank[6 + h // 2][:, :].rearrange("p (j n) -> p j n", j=2),
                                  bg[:, :].unsqueeze(1).broadcast_to((P, 2, D)), ALU.add).then_inc(g_sum_ready, 1)

        def summaries(g):
            for j in range(G):
                dve.wait_ge(kv_sum, G * g + j + 1)
                dve.tensor_tensor(summary[:, j, :, 0:P], sum_bank(j)[:, :, 0:P],
                                  m.blockdiag.unsqueeze(1).broadcast_to((P, KC, P)), ALU.mult)
                dve.tensor_tensor(summary[:, j, :, P:P + 8], sum_bank(j)[:, :, P:P + 1].broadcast_to((P, KC, 8)),
                                  m.headcol.unsqueeze(1).broadcast_to((P, KC, 8)), ALU.mult).then_inc(summary_ready, 1)

        def attention(g):
            for j in range(G):
                dve.wait_ge(num_ready, G * g + j + 1)
                m.step(dve.tensor_scalar(z_den[:, j, :, :], num_bank(j)[:, :, P:P + 8], 1e-6, None, ALU.add))
                m.wait_steps(dve)
                m.step(dve.reciprocal(z[:, j, :, :], z_den[:, j, :, :]))
                m.wait_steps(dve)
                dve.tensor_tensor(attn[:, j, :].rearrange("p (c h d) -> p c h d", c=KC, h=8),
                                  num_bank(j)[:, :, 0:P].rearrange("p c (h d) -> p c h d", h=8),
                                  z[:, j, :, :].unsqueeze(3).broadcast_to((P, KC, 8, HD)), ALU.mult).then_inc(attn_ready, 1)
                dve.wait_ge(attn_ready, G * g + j + 1)
                dve.wait_ge(g_tanh_ready, (G * g + j) // 2 + 1)
                dve.scalar_tensor_tensor(gated[:, j, :], g_tanh[:, j, :], 1.0, attn[:, j, :], ALU.add, ALU.mult).then_inc(gated_ready, 1)

        def outputs(g):
            for j in range(G):
                dve.wait_ge(gt_hi_ready, G * g + j + 1)
                dve.tensor_tensor(gt_lo[:, j, :, :], gt_bank(j), f(gt_hi[:, j, :, :]), ALU.subtract).then_inc(gt_lo_ready, 1)
            m.wait_steps(dve)
            for j in range(G):
                dve.wait_ge(out_ready, G * g + j + 1)
                dve.scalar_tensor_tensor(m.X[:, G * g + j, :], out_bank(j), half_tg[:, 0:1], m.X[:, G * g + j, :],
                                         ALU.mult, ALU.add).then_inc(m.x_done, 1)

        for c in range(KC):
            dve.wait_ge(ct_hi_ready, c + 1)
            dve.tensor_tensor(ct_lo[:, c, :, :], m.CT[:, c, 0:G, :], f(ct_hi[:, c, :, :]), ALU.subtract).then_inc(ct_ready, 1)
        weights(0)
        norm.vector(dve, 0, lambda j: xn[0][:, j, :])
        weights(1)
        dve.wait_ge(m.tg_ready, 1)
        m.step(dve.tensor_scalar(half_tg[:, :], m.tg[:, 0:1], 0.5, None, ALU.mult))
        keys(0)
        for g in range(NG):
            queries(g)
            if g + 1 < NG:
                norm.vector(dve, g + 1, lambda j: xn[1][:, j, :])
            summaries(g)
            attention(g)
            if g + 1 < NG:
                keys(g + 1)
            outputs(g)

    def tensor(pe):
        def w(name, c, n0=0, n1=None):
            a, b = cols[name]
            a, b = a + n0, b if n1 is None else a + n1
            return W_hi[:, c, a:b], W_lo[:, c, a:b]

        def keys(g):
            pe.wait_ge(ct_ready, KC * g + KC)
            after(pe, summary_ready, G * g)
            for j in range(G):
                if j >= 2:
                    pe.wait_ge(k_ready, G * g + j - 1)
                    pe.wait_ge(v_ready, G * g + j - 1)
                for c in range(KC):
                    mm = split_matmul(pe, kv_bank[j % 2][:, :], (ct_hi[:, c, j, :], ct_lo[:, c, j, :]), w("kv", c), c == 0, c == KC - 1)
                mm.then_inc(kv_proj, 1)

        def queries(g):
            xt.tensor(pe, g, lambda j: xn[g][:, j, :])
            pe.wait_ge(w_lo_ready, 2)
            pe.wait_ge(xt.lo_ready, xt.lo_at(g + 1))
            for o in range(KC):
                for c in range(KC):
                    mm = split_matmul(pe, q_bank[o][:, :], w("q", c, o * P, (o + 1) * P), (m.xt_hi[:, c, 0:G, :], m.xt_lo[:, c, 0:G, :]), c == 0, c == KC - 1)
                mm.then_inc(q_proj, 1)
            after(pe, m.x_done, m.x_at(stage, G * g))
            for j in range(G):
                for c in range(KC):
                    mm = split_matmul(pe, g_bank(j), (m.xt_hi[:, c, j, :], m.xt_lo[:, c, j, :]), w("g", c), c == 0, c == KC - 1)
                mm.then_inc(g_proj, 1)

        def summaries(g):
            for j in range(G):
                pe.wait_ge(k_ready, G * g + (G if j < 2 else j + 1))
                pe.wait_ge(v_ready, G * g + (G if j < 2 else j + 1))
                if j >= 2:
                    pe.wait_ge(summary_ready, G * g + j - 1)
                for c in range(KC):
                    mm = pe.matmul(sum_bank(j)[:, c, 0:P + 1], k_feat[:, j, c * P:(c + 1) * P], v_one[:, j, c, :], start=True, stop=True)
                mm.then_inc(kv_sum, 1)

        def attention(g):
            pe.wait_ge(q_ready, KC * g + KC)
            for j in range(G):
                pe.wait_ge(summary_ready, G * g + j + 1)
                if j >= 2:
                    pe.wait_ge(attn_ready, G * g + j - 1)
                for c in range(KC):
                    mm = pe.matmul(num_bank(j)[:, c, 0:P + 8], q_feat[:, c, j * P:(j + 1) * P], summary[:, j, c, :], start=True, stop=True)
                mm.then_inc(num_ready, 1)

        def outputs(g):
            for j in range(G):
                pe.wait_ge(gated_ready, G * g + j + 1)
                if j >= 2:
                    pe.wait_ge(gt_lo_ready, G * g + j - 1)
                for c in range(KC):
                    mm = pe.transpose(gt_bank(j)[:, c, :], gated[:, j, c * P:(c + 1) * P], m.ident)
                mm.then_inc(gt_raw, 1)
            for j in range(G):
                pe.wait_ge(gt_lo_ready, G * g + j + 1)
                if j >= 2:
                    pe.wait_ge(m.x_done, m.x_at(stage, G * g + j - 1))
                for c in range(KC):
                    mm = split_matmul(pe, out_bank(j), (gt_hi[:, j, c, :], gt_lo[:, j, c, :]), w("o", c), c == 0, c == KC - 1)
                mm.then_inc(out_ready, 1)

        pe.wait_ge(w_lo_ready, 1)
        keys(0)
        pe.wait_ge(m.const_in, 32)
        for g in range(NG):
            queries(g)
            summaries(g)
            attention(g)
            if g + 1 < NG:
                keys(g + 1)
            outputs(g)

    return {"load": load, "gpsimd": gpsimd, "scalar": scalar, "vector": vector, "tensor": tensor}


def adapters(m, stage, name, first):
    E, R, K = 8, 16, 2
    BONUS = 3.0 * (1.0 - 1 / 625)
    ER = E * R
    s = lambda x: m.sem(f"{name}_{x}")
    gate = m.tg[:, 4:5] if first else m.tg[:, 7:8]
    norm = Norm(m, stage)
    xt = Transposed(m, [m.bank[4], m.bank[5]], norm,
                    lambda g, c: m.xt_hi[:, c, G * g:G * g + G, :], lambda g, c: m.xt_lo[:, c, G * g:G * g + G, :])
    W = m.sb(f"{name}_w", [P, KC, ER + E])
    W_hi = m.sb(f"{name}_w_hi", [P, KC, ER + E], F32R)
    W_lo = m.sb(f"{name}_w_lo", [P, KC, ER + E], F32R)
    up = m.sb(f"{name}_up", [P, D])
    if first:
        bias = m.sb(f"{name}_bias", [P, ER + E])
        up_bias = m.sb(f"{name}_up_bias", [E, D])
    per_group = lambda shape: [m.work(shape) for _ in range(NG)]
    xn = [m.xn, m.work([P, G, D])]
    proj = per_group([P, G, ER + E])
    logits = per_group([P, G, 2 * E])
    top = per_group([P, G, 8])
    chosen = per_group([P, G, 8])
    marked = per_group([P, G, 2 * E])
    mask = per_group([P, G, E])
    shifted = per_group([P, G, E])
    expd = per_group([P, G, E])
    kept = per_group([P, G, E])
    total = per_group([P, G])
    inv = per_group([P, G])
    weight = per_group([P, G, E])
    hidden = per_group([P, G, ER])
    hidden_t = per_group([P, G, P])
    weight_t = per_group([E, G, P])
    plus_x = per_group([P, G, D])
    loaded, w_parts, pads = s("loaded"), s("w_parts"), s("pads")
    projected, proj_ready = s("projected"), s("proj")
    shifted_ready, exp_ready = s("shifted"), s("exp")
    hidden_ready = s("hidden")
    turned, turned_ready, out_ready = s("turned"), s("turned_copy"), s("out")
    proj_bank = lambda j: m.bank[j][:, 0:ER + E]
    turn_bank = lambda j: m.bank[6 + j % 2]
    out_bank = lambda j: m.bank[j][:, 0:D]
    LOADS = 4 if first else 2

    def load(sp):
        sp.dma_start(W[:, :, :], m.dram[f"{name}_w"].rearrange("p (c n) -> p c n", c=KC)).then_inc(loaded, 16)
        sp.dma_start(up[:, :], m.dram[f"{name}_up"]).then_inc(loaded, 16)
        if first:
            sp.dma_start(bias[:, :], m.dram[f"{name}_bias"].broadcast_to((P, ER + E))).then_inc(loaded, 16)
            sp.dma_start(up_bias[:, :], m.dram[f"{name}_up_bias"]).then_inc(loaded, 16)

    def gpsimd(pool):
        pool.wait_ge(loaded, 16 * LOADS)
        pool.tensor_copy(W_hi[:, :, :], W[:, :, :]).then_inc(w_parts, 1)
        pool.wait_ge(w_parts, 1)
        pool.tensor_tensor(W_lo[:, :, :], W[:, :, :], f(W_hi[:, :, :]), ALU.subtract).then_inc(w_parts, 1)
        norm.gpsimd(pool, 0)
        pool.wait_ge(m.x_done, m.x_at(stage, 0))
        for g in range(NG):
            pool.memset(logits[g][:, :, E:2 * E], -BIG).then_inc(pads, 1)
            pool.memset(chosen[g][:, :, :], -BIG).then_inc(pads, 1)
        norm.gpsimd(pool, 1)

    def scalar(act):
        def project(g):
            if not first:
                for j in range(G):
                    act.wait_ge(projected, G * g + j + 1)
                    act.activation(proj[g][:, j, :], proj_bank(j), ACT.Copy).then_inc(proj_ready, 1)

        def exponentials(g):
            act.wait_ge(shifted_ready, g + 1)
            act.activation(expd[g][:, :, :], shifted[g][:, :, :], ACT.Exp).then_inc(exp_ready, 1)

        def turn(g):
            for j in range(G):
                act.wait_ge(turned, G * g + j + 1)
                act.activation(hidden_t[g][:, j, :], turn_bank(j)[:, 0:P], ACT.Copy).then_inc(turned_ready, 1)
                if first:
                    act.activation(weight_t[g][:, j, :], turn_bank(j)[0:E, D:D + P], ACT.Copy).then_inc(turned_ready, 1)

        act.wait_ge(m.x_done, m.x_at(stage, 0))
        xt.scalar(act, 0)
        project(0)
        xt.scalar(act, 1)
        exponentials(0)
        project(1)
        turn(0)
        exponentials(1)
        turn(1)

    def vector(dve):
        def project(g):
            if first:
                for j in range(G):
                    dve.wait_ge(projected, G * g + j + 1)
                    dve.tensor_tensor(proj[g][:, j, :], proj_bank(j), bias[:, :], ALU.add).then_inc(proj_ready, 1)

        def route(g):
            dve.wait_ge(proj_ready, G * g + G)
            dve.wait_ge(pads, 2 * NG)
            m.step(dve.tensor_scalar(logits[g][:, :, 0:E], proj[g][:, :, ER:ER + E], BONUS if first else 0.0, None, ALU.add))
            m.wait_steps(dve)
            for j in range(G):
                m.step(dve.max(top[g][:, j, :], logits[g][:, j, :]))
            m.wait_steps(dve)
            m.step(dve.tensor_copy(chosen[g][:, :, 0:K], top[g][:, :, 0:K]))
            dve.tensor_tensor(shifted[g][:, :, :], logits[g][:, :, 0:E], top[g][:, :, 0:1].broadcast_to((P, G, E)), ALU.subtract).then_inc(shifted_ready, 1)
            m.wait_steps(dve)
            for j in range(G):
                m.step(dve.match_replace(marked[g][:, j, :], chosen[g][:, j, :], logits[g][:, j, :], BIG))
            m.wait_steps(dve)
            m.step(dve.tensor_tensor(mask[g][:, :, :], marked[g][:, :, 0:E], logits[g][:, :, 0:E], ALU.not_equal))
            m.wait_steps(dve)
            dve.wait_ge(exp_ready, g + 1)
            m.step(dve.tensor_tensor(kept[g][:, :, :], expd[g][:, :, :], mask[g][:, :, :], ALU.mult))
            m.wait_steps(dve)
            m.step(dve.reduce_sum(total[g][:, :], kept[g][:, :, :], AX_X))
            m.wait_steps(dve)
            m.step(dve.reciprocal(inv[g][:, :], total[g][:, :]))
            m.wait_steps(dve)
            m.step(dve.tensor_tensor(weight[g][:, :, :], kept[g][:, :, :], inv[g][:, :].unsqueeze(2).broadcast_to((P, G, E)), ALU.mult))
            m.wait_steps(dve)
            for j in range(G):
                spread = weight[g][:, j, :].unsqueeze(2).broadcast_to((P, E, R))
                down = proj[g][:, j, 0:ER].rearrange("p (e r) -> p e r", e=E)
                into = hidden[g][:, j, :].rearrange("p (e r) -> p e r", e=E)
                if first:
                    dve.scalar_tensor_tensor(into, down, 0.0, spread, ALU.max, ALU.mult).then_inc(hidden_ready, 1)
                else:
                    dve.tensor_tensor(into, down, spread, ALU.mult).then_inc(hidden_ready, 1)

        def outputs(g):
            for j in range(G):
                b = G * g + j
                dve.wait_ge(out_ready, b + 1)
                if first:
                    dve.scalar_tensor_tensor(m.X[:, b, :], out_bank(j), gate, m.X[:, b, :], ALU.mult, ALU.add).then_inc(m.x_done, 1)
                else:
                    m.step(dve.tensor_tensor(plus_x[g][:, j, :], out_bank(j), xn[g][:, j, :], ALU.add))
                    m.wait_steps(dve)
                    dve.scalar_tensor_tensor(m.X[:, b, :], plus_x[g][:, j, :], gate, m.X[:, b, :], ALU.mult, ALU.add).then_inc(m.x_done, 1)

        dve.wait_ge(loaded, 16 * LOADS)
        norm.vector(dve, 0, lambda j: xn[0][:, j, :])
        norm.vector(dve, 1, lambda j: xn[1][:, j, :])
        xt.vector(dve, 0)
        project(0)
        xt.vector(dve, 1)
        route(0)
        project(1)
        route(1)
        for g in range(NG):
            outputs(g)

    def tensor(pe):
        def project(g):
            pe.wait_ge(xt.lo_ready, xt.lo_at(g + 1))
            for j in range(G):
                after(pe, proj_ready, G * (g - 1) + j + 1)
                for c in range(KC):
                    mm = split_matmul(pe, proj_bank(j), (m.xt_hi[:, c, G * g + j, :], m.xt_lo[:, c, G * g + j, :]), (W_hi[:, c, :], W_lo[:, c, :]), c == 0, c == KC - 1)
                mm.then_inc(projected, 1)

        def outputs(g):
            for j in range(G):
                pe.wait_ge(hidden_ready, G * g + j + 1)
                after(pe, turned_ready, (1 + first) * (G * g + j - 1))
                mm = pe.transpose(turn_bank(j)[:, 0:P], hidden[g][:, j, :], m.ident)
                if first:
                    mm = pe.transpose(turn_bank(j)[0:E, D:D + P], weight[g][:, j, :], m.ident)
                mm.then_inc(turned, 1)
            pe.wait_ge(proj_ready, NB)
            for j in range(G):
                pe.wait_ge(turned_ready, (1 + first) * (G * g + j + 1))
                if g:
                    pe.wait_ge(m.x_done, m.x_at(stage, G * (g - 1) + j + 1))
                mm = pe.matmul(out_bank(j), hidden_t[g][:, j, :], up[:, :], start=True, stop=not first)
                if first:
                    mm = pe.matmul(out_bank(j), weight_t[g][:, j, :], up_bias[:, :], start=False, stop=True)
                mm.then_inc(out_ready, 1)

        pe.wait_ge(w_parts, 2)
        pe.wait_ge(loaded, 16 * LOADS)
        pe.wait_ge(m.x_done, m.x_at(stage, 0))
        for g in range(NG):
            if g:
                pe.wait_ge(xt.lo_ready, xt.lo_at(g))
            xt.tensor(pe, g, lambda j: xn[g][:, j, :])
            project(g)
        for g in range(NG):
            outputs(g)

    return {"load": load, "gpsimd": gpsimd, "scalar": scalar, "vector": vector, "tensor": tensor}


def l1_attention(m, stage):
    H, HD, STACK = 8, 16, 48
    s = lambda x: m.sem(f"l1a_{x}")
    norm = Norm(m, stage)
    sel_raw = m.xn_all[:, :, :].rearrange("p b d -> p (b d)").rearrange("p (k q n) -> p k q n", k=4, q=4)
    sel = m.sb("l1a_sel", [P, 4, 4, P], F32R)
    gamma = m.sb("l1a_gamma", [P, 1])
    scale = m.work([P, 1])
    q_hi = m.xt_hi[:, :, :, :].rearrange("p c b n -> p (c b n)").rearrange("p (b d) -> p b d", b=NB)
    q_lo = m.xt_lo[:, :, :, :].rearrange("p c b n -> p (c b n)").rearrange("p (b d) -> p b d", b=NB)
    k_hi = [ring[:, 2 * D:3 * D] for ring in m.ring_hi]
    k_lo = [ring[:, 2 * D:3 * D] for ring in m.ring_lo]
    k_stack = [m.work([P, 4, D], F32R) for _ in range(2)]
    q_stack = [m.work([P, 4, D], F32R) for _ in range(2)]
    lower = [m.work([H, D], F32R) for _ in range(2)]
    v_hi = m.work([P, 2, KC, H, 2 * HD], F32R)
    v_lo = m.work([P, 2, KC, H, 2 * HD], F32R)
    maxima = [m.work([P, KC, H]) for _ in range(2)]
    PB = 3
    probs = m.work([P, PB, KC, D])
    by_chunk = lambda ring: ring[:, 0:2 * D].rearrange("p (k n) -> p k n", k=KC)
    p_hi = [by_chunk(m.ring_hi[0]), by_chunk(m.ring_hi[1]), m.work([P, KC, D], F32R)]
    p_lo = [by_chunk(m.ring_lo[0]), by_chunk(m.ring_lo[1]), m.work([P, KC, D], F32R)]
    o_raw = m.work([P, 2, D])
    o_hi = m.work([P, 2, D], F32R)
    o_lo = m.work([P, 2, D], F32R)
    out_sel_raw = m.work([P, 2, 2, P])
    out_sel = m.work([P, 2, 2, P], F32R)
    inv = m.work([P, D])
    ratio = m.work([P, D])
    sel_in, sel_ready = s("sel_in"), s("sel")
    k_hi_ready, k_split, v_ready, ones_ready, q_hi_ready, q_split = s("k_hi"), s("k_split"), s("v"), s("ones"), s("q_hi"), s("q_split")
    k_raw, q_raw, k_stacked, q_stacked = s("k_raw"), s("q_raw"), s("k_stacked"), s("q_stacked")
    scored, max_ready, max_turned, lower_ready, row_in = s("scored"), s("max"), s("max_turned"), s("lower"), s("row_in")
    lowered, exp_ready, p_split, summed = s("lowered"), s("exp"), s("p_split"), s("summed")
    out_sel_in, out_sel_ready, v_hi_ready = s("out_sel_in"), s("out_sel"), s("v_hi")
    taken, o_hi_ready, o_split, placed = s("taken"), s("o_hi"), s("o_split"), s("placed")
    k_bank, q_bank = [m.bank[2], m.bank[7]], [m.bank[3], m.bank[6]]
    LAG, LAG_V = 0, 3

    values = lambda b: m.CT[:, :, b, :].rearrange("p c (h d) -> p c h d", h=H)

    def load(sp):
        sp.dma_start(sel_raw[:, :, :, :], m.dram["l1a_sel"].rearrange("p (k q n) -> p k q n", k=4, q=4)).then_inc(sel_in, 16)
        sp.dma_start(gamma[:, :], m.dram["l1a_gamma"].broadcast_to((P, 1))).then_inc(sel_in, 16)

    def sync(sp):
        sp.wait_ge(m.x_done, m.x_at(stage, 0))
        sp.dma_start(out_sel_raw[:, :, :, :], m.dram["l1a_out_sel"].rearrange("p (k g n) -> p k g n", k=2, g=2)).then_inc(out_sel_in, 16)
        for b in range(NB):
            sp.wait_ge(lower_ready, b + 1)
            for a in range(2):
                row = 64 * a + STACK
                sp.dma_start(f(q_stack[b % 2][row:row + 1, :, :]), f(lower[b % 2][4 * a:4 * a + 4, :])).then_inc(row_in, 16)

    def gpsimd(pool):
        pool.wait_ge(m.cn_in, 16)
        pool.wait_ge(m.x_done, m.x_at(stage, 0))
        for g in range(NG):
            norm.gpsimd(pool, g)
        pool.wait_ge(m.const_in, 32)
        for part, one in ((v_hi, 1.0), (v_lo, 0.0)):
            rows = part[:, :, :, :, HD:2 * HD].rearrange("p n c h d -> p (n c h) d")
            pool.tensor_scalar(rows, m.minus_half[:, 0:1].unsqueeze(2).broadcast_to((P, 2 * KC * H, HD)), 0.0, one, ALU.mult, ALU.add).then_inc(ones_ready, 1)

        def low_parts(b):
            pool.wait_ge(k_hi_ready, b + 1)
            pool.tensor_tensor(k_lo[b % 2], m.CN[:, b, :], f(k_hi[b % 2]), ALU.subtract).then_inc(k_split, 1)
            pool.wait_ge(q_hi_ready, b + 1)
            pool.tensor_tensor(q_lo[:, b, :], m.xn_all[:, b, :], f(q_hi[:, b, :]), ALU.subtract).then_inc(q_split, 1)

        def value_parts(b):
            pool.wait_ge(v_hi_ready, b + 1)
            pool.tensor_tensor(v_lo[:, b % 2, :, :, 0:HD], values(b), f(v_hi[:, b % 2, :, :, 0:HD]), ALU.subtract).then_inc(v_ready, 1)

        def low_exps(b, heads):
            for h in heads:
                pool.wait_ge(exp_ready, 2 * (H * b + h + 1))
                n = (H * b + h) % PB
                pool.tensor_tensor(p_lo[n], probs[:, n, :, :], f(p_hi[n]), ALU.subtract).then_inc(p_split, 1)

        low_parts(0)
        for b in range(NB + 1):
            if b:
                low_exps(b - 1, range(0, H // 2))
            if b + 1 < NB:
                low_parts(b + 1)
            if b:
                low_exps(b - 1, range(H // 2, H))
            if b < NB:
                value_parts(b)

    def vector(dve):
        dve.wait_ge(sel_in, 32)
        dve.wait_ge(sel_ready, 1)
        m.step(dve.tensor_tensor(scale[:, :], m.tg[:, 1:2], gamma[:, :], ALU.mult))
        for g in range(NG):
            norm.vector(dve, g, lambda j: m.xn_all[:, G * g + j, :])
        m.wait_steps(dve)

        def queries(b):
            for half in range(2):
                dve.wait_ge(q_raw, 2 * b + half + 1)
                dve.tensor_copy(q_stack[b % 2][:, 2 * half:2 * half + 2, :], q_bank[half][:, :].rearrange("p (q n) -> p q n", q=2)).then_inc(q_stacked, 1)

        def largest(b, h):
            dve.wait_ge(scored, H * b + h + 1)
            dve.reduce_max(maxima[b % 2][:, :, 4 * (h % 2) + h // 2], m.bank[h % 2][:, :].rearrange("p (c n) -> p c n", c=KC), AX_X).then_inc(max_ready, 1)

        def lowering(b):
            dve.wait_ge(max_turned, b + 1)
            dve.tensor_scalar(lower[b % 2][:, :], m.bank[6][0:H, 0:D], -1.0, None, ALU.mult).then_inc(lower_ready, 1)

        def split_output(b):
            dve.wait_ge(o_hi_ready, b + 1)
            dve.tensor_tensor(o_lo[:, :, :], o_raw[:, :, :], f(o_hi[:, :, :]), ALU.subtract).then_inc(o_split, 1)

        def take(b, pair):
            dve.wait_ge(summed, H * b + 2 * pair + 2)
            after(dve, o_split, b)
            row = 2 * HD * pair
            dve.tensor_copy(o_raw[row:row + 2 * HD, :, :], m.bank[4 + pair % 2][0:2 * HD, :].rearrange("p (h n) -> p h n", h=2)).then_inc(taken, 1)

        def add(b):
            dve.wait_ge(placed, b + 1)
            m.step(dve.reciprocal(inv[:, :], m.bank[7][:, D:2 * D]))
            m.wait_steps(dve)
            m.step(dve.tensor_tensor(ratio[:, :], m.bank[7][:, 0:D], inv[:, :], ALU.mult))
            m.wait_steps(dve)
            dve.scalar_tensor_tensor(m.X[:, b, :], ratio[:, :], scale[:, 0:1], m.X[:, b, :], ALU.mult, ALU.add).then_inc(m.x_done, 1)

        for b in range(NB + 2):
            if b < NB:
                queries(b)
            if b >= 2:
                split_output(b - 2)
            for h in range(H):
                if b < NB:
                    largest(b, h)
                if 1 <= b <= NB and h > LAG_V and (h - LAG_V) % 2:
                    take(b - 1, (h - LAG_V) // 2)
            if b >= 2:
                add(b - 2)
            if b < NB:
                lowering(b)
            if 1 <= b <= NB:
                for pair in range((H - LAG_V) // 2, H // 2):
                    take(b - 1, pair)

    def scalar(act):
        act.wait_ge(m.cn_in, 16)
        act.wait_ge(sel_in, 32)
        act.activation(sel[:, :, :, :], sel_raw[:, :, :, :], ACT.Copy).then_inc(sel_ready, 1)
        act.wait_ge(m.x_done, m.x_at(stage, 0))

        def high_parts(b):
            after(act, k_raw, 2 * (b - 1))
            act.activation(k_hi[b % 2], m.CN[:, b, :], ACT.Copy).then_inc(k_hi_ready, 1)
            act.wait_ge(norm.xn, norm.xn_at(b + 1))
            act.activation(q_hi[:, b, :], m.xn_all[:, b, :], ACT.Copy).then_inc(q_hi_ready, 1)

        def value_high_parts(b):
            after(act, summed, H * (b - 1))
            act.activation(v_hi[:, b % 2, :, :, 0:HD], values(b), ACT.Copy).then_inc(v_hi_ready, 1)

        def keys(b):
            for half in range(2):
                act.wait_ge(k_raw, 2 * b + half + 1)
                act.activation(k_stack[b % 2][:, 2 * half:2 * half + 2, :], k_bank[half][:, :].rearrange("p (q n) -> p q n", q=2),
                               ACT.Identity, bias=m.one_row).then_inc(k_stacked, 1)

        def exps(b, heads):
            for h in heads:
                act.wait_ge(lowered, H * b + h + 1)
                after(act, summed, H * b + h + 1 - PB)
                n = (H * b + h) % PB
                for out in (p_hi[n], probs[:, n, :, :]):
                    act.activation(out, m.bank[2 + h % 2][:, :].rearrange("p (c n) -> p c n", c=KC), ACT.Exp, scale=0.25).then_inc(exp_ready, 1)

        high_parts(0)
        def outputs(b):
            act.wait_ge(taken, H // 2 * (b + 1))
            after(act, placed, b)
            act.activation(o_hi[:, :, :], o_raw[:, :, :], ACT.Copy).then_inc(o_hi_ready, 1)

        for b in range(NB + 2):
            if b < NB:
                keys(b)
            if b == 1:
                act.wait_ge(out_sel_in, 16)
                act.activation(out_sel[:, :, :, :], out_sel_raw[:, :, :, :], ACT.Copy).then_inc(out_sel_ready, 1)
            if b >= 2:
                outputs(b - 2)
            if 1 <= b <= NB:
                exps(b - 1, range(0, H // 2))
            if b + 1 < NB:
                high_parts(b + 1)
            if b < NB:
                value_high_parts(b)
            if 1 <= b <= NB:
                exps(b - 1, range(H // 2, H))

    def tensor(pe):
        pe.wait_ge(sel_ready, 1)
        pe.wait_ge(m.x_done, m.x_at(stage, 0))
        pe.wait_ge(ones_ready, 2)

        def stacks(b, half):
            if b and half:
                pe.wait_ge(lower_ready, b)
                pe.wait_ge(m.x_done, m.x_at(stage, max(b - 2, 0)))
            if b >= 2 and not half:
                pe.wait_ge(exp_ready, 2 * H * (b - 1))
            for kind, bank, raw, hi, lo in ((2, k_bank[half], k_raw, k_hi[b % 2], k_lo[b % 2]), (0, q_bank[half], q_raw, q_hi[:, b, :], q_lo[:, b, :])):
                for q in range(2):
                    pe.matmul(bank[:, q * D:(q + 1) * D], sel[:, kind, 2 * half + q, :], hi, start=True, stop=False)
                    mm = pe.matmul(bank[:, q * D:(q + 1) * D], sel[:, kind + 1, 2 * half + q, :], lo, start=False, stop=True)
                mm.then_inc(raw, 1)

        def score(b, h):
            a, q = h % 2, h // 2
            if h % 4 == 0:
                pe.wait_ge(q_stacked, 2 * b + h // 4 + 1)
                pe.wait_ge(k_stacked, 2 * b + h // 4 + 1)
            after(pe, max_ready, H * b + h - 1)
            for c in range(KC):
                mm = pe.matmul(m.bank[a][:, c * D:(c + 1) * D], q_stack[b % 2][64 * a:64 * a + STACK, q, c * P:(c + 1) * P],
                               k_stack[b % 2][64 * a:64 * a + STACK, q, :], start=True, stop=True)
            mm.then_inc(scored, 1)

        def lowered_scores(b, h):
            a, q = h % 2, h // 2
            if h == 0:
                pe.wait_ge(row_in, 32 * (b + 1))
                pe.wait_ge(q_stacked, min(2 * b + 3, 2 * NB))
                pe.wait_ge(k_stacked, min(2 * b + 3, 2 * NB))
            after(pe, exp_ready, 2 * (H * b + h - 1))
            for c in range(KC):
                mm = pe.matmul(m.bank[2 + a][:, c * D:(c + 1) * D], k_stack[b % 2][64 * a:64 * a + STACK + 1, q, c * P:(c + 1) * P],
                               q_stack[b % 2][64 * a:64 * a + STACK + 1, q, :], start=True, stop=True)
            mm.then_inc(lowered, 1)

        def products(b, h):
            pe.wait_ge(p_split, H * b + h + 1)
            if h == 0:
                pe.wait_ge(v_ready, b + 1)
            if h % 2 == 0:
                after(pe, taken, H // 2 * b + h // 2 - 1)
            n = (H * b + h) % PB
            out = m.bank[4 + h // 2 % 2][0:2 * HD, (h % 2) * D:(h % 2 + 1) * D]
            for k in range(KC):
                mm = split_matmul(pe, out, (v_hi[:, b % 2, k, h, :], v_lo[:, b % 2, k, h, :]), (p_hi[n][:, k, :], p_lo[n][:, k, :]),
                                  k == 0, k == KC - 1)
            mm.then_inc(summed, 1)

        def place(b):
            pe.wait_ge(out_sel_ready, 1)
            pe.wait_ge(o_split, b + 1)
            pe.wait_ge(m.x_done, m.x_at(stage, b))
            for kind in range(2):
                for g in range(2):
                    pe.matmul(m.bank[7][:, kind * D:(kind + 1) * D], out_sel[:, kind, g, :], o_hi[:, g, :], start=g == 0, stop=False)
                    mm = pe.matmul(m.bank[7][:, kind * D:(kind + 1) * D], out_sel[:, kind, g, :], o_lo[:, g, :], start=False, stop=g == 1)
            mm.then_inc(placed, 1)

        for b in range(NB + 2):
            if b < NB:
                pe.wait_ge(k_split, b + 1)
                pe.wait_ge(q_split, b + 1)
                stacks(b, 0)
                stacks(b, 1)
            for h in range(H + LAG_V):
                if b < NB and h < H:
                    score(b, h)
                if 1 <= b <= NB and LAG <= h < H + LAG:
                    lowered_scores(b - 1, h - LAG)
                if b >= 2 and h == H - 4:
                    place(b - 2)
                if 1 <= b <= NB and h >= LAG_V:
                    products(b - 1, h - LAG_V)
                if b < NB and h == H:
                    pe.wait_ge(max_ready, H * b + H)
                    for c in range(KC):
                        mm = pe.transpose(m.bank[6][0:H, c * P:(c + 1) * P], maxima[b % 2][:, c, :], m.ident)
                    mm.then_inc(max_turned, 1)

    return {"load": load, "sync": sync, "gpsimd": gpsimd, "scalar": scalar, "vector": vector, "tensor": tensor}


def feed_forward(m, stage, name, chunks, experts):
    E, NS, K = 16, 2, 4
    GE = E + NS
    s = lambda x: m.sem(f"{name}_{x}")
    norm = Norm(m, stage)
    xt = Transposed(m, [m.bank[4], m.bank[5]], norm,
                    lambda g, c: m.xt_hi[:, c, G * g:G * g + G, :], lambda g, c: m.xt_lo[:, c, G * g:G * g + G, :])
    gate = m.tg[:, 5:6] if experts else m.tg[:, 6:7]
    IN = 3 * P if experts else 4 * P
    COLS = IN + D
    hidden = m.work([P, NB, P])
    up = m.work([P, NB, P])
    gated = m.work([P, NB, P])
    h_hi = [m.work([P, NB, P], F32R) for _ in range(2)]
    h_lo = [m.work([P, NB, P], F32R) for _ in range(2)]
    summed = m.work([P, NB, D])
    w_in = [s("w_in_even"), s("w_in_odd")]
    cols_in, in_hi, in_lo, out_hi, out_lo = s("cols_in"), s("in_hi"), s("in_lo"), s("out_hi"), s("out_lo")
    h_raw, u_raw, h_ready, u_ready, gated_ready, h_hi_ready, h_lo_ready, used = s("h_raw"), s("u_raw"), s("h"), s("u"), s("gated"), s("h_hi"), s("h_lo"), s("used")
    if experts:
        b1 = m.sb(f"{name}_b1", [P, chunks])
        cen = m.sb(f"{name}_cen", [P, KC, E])
        cen_hi = m.sb(f"{name}_cen_hi", [P, KC, E], F32R)
        cen_lo = m.sb(f"{name}_cen_lo", [P, KC, E], F32R)
        bias = m.sb(f"{name}_bias", [P, E])
        b2 = m.sb(f"{name}_b2", [2 * GE, D])
        b2_hi = m.sb(f"{name}_b2_hi", [2 * GE, D], F32R)
        b2_lo = m.sb(f"{name}_b2_lo", [2 * GE, D], F32R)
        gates_t = m.work([2 * GE, NB, P], F32R)
        th = m.work([P, G, E])
        score = m.work([P, G, E + 8])
        top = m.work([P, G, 8])
        chosen = m.work([P, G, 8])
        marked = m.work([P, G, E + 8])
        mask = m.work([P, G, E])
        kept = m.work([P, G, E])
        total = m.work([P, G])
        guarded = m.work([P, G])
        inv = m.work([P, G])
        gates = m.work([P, G, GE])
        parts = m.work([P, G, 2, GE], F32R)
        small_parts, pads = s("small_parts"), s("pads")
        routed, th_ready = s("routed"), s("th")
        gates_lo, turned, gates_t_ready = s("gates_lo"), s("turned"), s("gates_t")
    else:
        scales = m.sb(f"{name}_scales", [P, 2, chunks])
        factors = m.sb(f"{name}_factors", [P, 2, chunks])
        half = m.sb(f"{name}_half", [P, chunks])
        out_scale = m.sb(f"{name}_out_scale", [P, D])
        factors_ready = s("factors")

    acc = lambda b: m.bank[4 + b // 2][:, (b % 2) * D:(b % 2 + 1) * D]
    side = lambda t: slice(G * t, G * t + G)
    wide = lambda bank: bank[:, :].rearrange("p (j n) -> p j n", j=G)
    raw, hi, lo = m.ring_raw, m.ring_hi, m.ring_lo

    def load(sp):
        if experts:
            for tile, what in ((b1, "b1"), (cen, "cen"), (b2, "b2")):
                src = m.dram[f"{name}_{what}"]
                sp.dma_start(tile[:, :, :] if what == "cen" else tile[:, :], src.rearrange("p (c n) -> p c n", c=KC) if what == "cen" else src).then_inc(cols_in, 16)
            sp.dma_start(bias[:, :], m.dram[f"{name}_bias"].broadcast_to((P, E))).then_inc(cols_in, 16)
        else:
            sp.dma_start(scales[:, :, :], m.dram[f"{name}_scales"].rearrange("p (k n) -> p k n", k=2)).then_inc(cols_in, 16)
            sp.dma_start(out_scale[:, :], m.dram[f"{name}_out_scale"].broadcast_to((P, D))).then_inc(cols_in, 16)

    def sync(sp):
        sp.wait_ge(m.x_done, m.x_at(stage - 1, 0))
        for c in range(chunks):
            after(sp, out_lo, c - 1)
            sp.dma_start(raw[c % 2][:, 0:COLS], m.dram[f"{name}_w"][c, :, :]).then_inc(w_in[c % 2], 16)

    def gpsimd(pool):
        if experts:
            pool.wait_ge(cols_in, 64)
            for tile, h, l in ((cen[:, :, :], cen_hi[:, :, :], cen_lo[:, :, :]), (b2[:, :], b2_hi[:, :], b2_lo[:, :])):
                pool.tensor_copy(h, tile).then_inc(small_parts, 1)
            pool.wait_ge(small_parts, 2)
            for tile, h, l in ((cen[:, :, :], cen_hi[:, :, :], cen_lo[:, :, :]), (b2[:, :], b2_hi[:, :], b2_lo[:, :])):
                pool.tensor_tensor(l, tile, f(h), ALU.subtract).then_inc(small_parts, 1)
            pool.wait_ge(m.x_done, m.x_at(stage, 0))
            pool.memset(score[:, :, E:E + 8], -BIG).then_inc(pads, 1)
            pool.memset(chosen[:, :, :], -BIG).then_inc(pads, 1)
            pool.memset(gates[:, :, E:GE], 1.0).then_inc(pads, 1)
        for g in range(NG):
            norm.gpsimd(pool, g)
        def low_in(c):
            pool.wait_ge(in_hi, c + 1)
            pool.tensor_tensor(lo[c % 2][:, 0:IN], raw[c % 2][:, 0:IN], f(hi[c % 2][:, 0:IN]), ALU.subtract).then_inc(in_lo, 1)

        def low_out(c):
            pool.wait_ge(out_hi, c + 1)
            pool.tensor_tensor(lo[c % 2][:, IN:COLS], raw[c % 2][:, IN:COLS], f(hi[c % 2][:, IN:COLS]), ALU.subtract).then_inc(out_lo, 1)

        low_in(0)
        for c in range(chunks):
            if c + 1 < chunks:
                low_in(c + 1)
            low_out(c)

    def scalar(act):
        def high_in(c):
            act.wait_ge(w_in[c % 2], 16 * (c // 2 + 1))
            after(act, h_raw, 2 * (c - 1))
            act.activation(hi[c % 2][:, 0:IN], raw[c % 2][:, 0:IN], ACT.Copy).then_inc(in_hi, 1)

        def high_out(c):
            after(act, used, c - 1)
            act.activation(hi[c % 2][:, IN:COLS], raw[c % 2][:, IN:COLS], ACT.Copy).then_inc(out_hi, 1)

        act.wait_ge(m.x_done, m.x_at(stage, 0))
        high_in(0)
        for g in range(NG):
            xt.scalar(act, g)
            if experts:
                act.wait_ge(routed, g + 1)
                act.activation(th[:, :, :], m.bank[g][:, 0:G * E].rearrange("p (j e) -> p j e", j=G), ACT.Tanh, scale=0.5).then_inc(th_ready, 1)
                act.wait_ge(turned, g + 1)
                act.activation(gates_t[:, side(g), :], wide(m.bank[2 + g])[0:2 * GE, :, :], ACT.Copy).then_inc(gates_t_ready, 1)
        for c in range(chunks):
            for t in range(2):
                act.wait_ge(h_raw, 2 * c + t + 1)
                after(act, gated_ready, 2 * (c - 1) + t + 1)
                if experts:
                    act.activation(hidden[:, side(t), :], wide(m.bank[t]), ACT.Relu, bias=b1[:, c:c + 1]).then_inc(h_ready, 1)
                else:
                    act.wait_ge(factors_ready, 1)
                    act.activation(hidden[:, side(t), :], wide(m.bank[t]), ACT.Tanh, scale=half[:, c:c + 1]).then_inc(h_ready, 1)
                    act.wait_ge(u_raw, 2 * c + t + 1)
                    act.activation(up[:, side(t), :], wide(m.bank[2 + t]), ACT.Copy, scale=factors[:, 1, c:c + 1]).then_inc(u_ready, 1)
            if c + 1 < chunks:
                high_in(c + 1)
            high_out(c)
            for t in range(2):
                act.wait_ge(gated_ready, 2 * c + t + 1)
                after(act, used, c - 1)
                act.activation(h_hi[c % 2][:, side(t), :], gated[:, side(t), :], ACT.Copy).then_inc(h_hi_ready, 1)

    def vector(dve):
        dve.wait_ge(cols_in, 64 if experts else 32)
        if experts:
            m.step(dve.tensor_scalar(bias[:, :], bias[:, :], 0.5, None, ALU.add))
        else:
            m.step(dve.tensor_scalar(half[:, :], scales[:, 0, :], 0.5, None, ALU.mult))
            m.wait_steps(dve)
            dve.tensor_tensor(factors[:, 1, :], half[:, :], scales[:, 1, :], ALU.mult).then_inc(factors_ready, 1)
        for g in range(NG):
            norm.vector(dve, g, lambda j: m.xn_all[:, G * g + j, :])
            xt.vector(dve, g)
            if experts:
                dve.wait_ge(th_ready, g + 1)
                m.wait_steps(dve)
                dve.wait_ge(pads, 3)
                m.step(dve.scalar_tensor_tensor(score[:, :, 0:E], th[:, :, :], 0.5, bias[:, :].unsqueeze(1).broadcast_to((P, G, E)), ALU.mult, ALU.add))
                m.wait_steps(dve)
                for j in range(G):
                    m.step(dve.max(top[:, j, :], score[:, j, :]))
                m.wait_steps(dve)
                m.step(dve.tensor_copy(chosen[:, :, 0:K], top[:, :, 0:K]))
                m.wait_steps(dve)
                for j in range(G):
                    m.step(dve.match_replace(marked[:, j, :], chosen[:, j, :], score[:, j, :], BIG))
                m.wait_steps(dve)
                m.step(dve.tensor_tensor(mask[:, :, :], marked[:, :, 0:E], score[:, :, 0:E], ALU.not_equal))
                m.wait_steps(dve)
                m.step(dve.tensor_tensor(kept[:, :, :], score[:, :, 0:E], mask[:, :, :], ALU.mult))
                m.wait_steps(dve)
                m.step(dve.reduce_sum(total[:, :], kept[:, :, :], AX_X))
                m.wait_steps(dve)
                m.step(dve.tensor_scalar(guarded[:, :], total[:, :], 1e-8, None, ALU.max))
                m.wait_steps(dve)
                m.step(dve.reciprocal(inv[:, :], guarded[:, :]))
                m.wait_steps(dve)
                m.step(dve.tensor_tensor(gates[:, :, 0:E], kept[:, :, :], inv[:, :].unsqueeze(2).broadcast_to((P, G, E)), ALU.mult))
                m.wait_steps(dve)
                m.step(dve.tensor_copy(parts[:, :, 0, :], gates[:, :, :]))
                m.wait_steps(dve)
                dve.tensor_tensor(parts[:, :, 1, :], gates[:, :, :], f(parts[:, :, 0, :]), ALU.subtract).then_inc(gates_lo, 1)
        for c in range(chunks):
            for t in range(2):
                dve.wait_ge(h_ready, 2 * c + t + 1)
                after(dve, h_lo_ready, 2 * (c - 1) + t + 1)
                if experts:
                    dve.wait_ge(u_raw, 2 * c + t + 1)
                    dve.tensor_tensor(gated[:, side(t), :], wide(m.bank[2 + t]), hidden[:, side(t), :], ALU.mult).then_inc(gated_ready, 1)
                else:
                    dve.wait_ge(u_ready, 2 * c + t + 1)
                    m.step(dve.scalar_tensor_tensor(up[:, side(t), :], hidden[:, side(t), :], 1.0, up[:, side(t), :], ALU.add, ALU.mult))
                    m.wait_steps(dve)
                    dve.tensor_tensor(gated[:, side(t), :], wide(m.bank[t]), up[:, side(t), :], ALU.mult).then_inc(gated_ready, 1)
            for t in range(2):
                dve.wait_ge(h_hi_ready, 2 * c + t + 1)
                dve.tensor_tensor(h_lo[c % 2][:, side(t), :], gated[:, side(t), :], f(h_hi[c % 2][:, side(t), :]), ALU.subtract).then_inc(h_lo_ready, 1)
        dve.wait_ge(used, chunks)
        for q in range(NB // 2):
            two = m.bank[4 + q][:, :].rearrange("p (j n) -> p j n", j=2)
            if experts:
                m.step(dve.tensor_tensor(summed[:, 2 * q:2 * q + 2, :], two, m.xn_all[:, 2 * q:2 * q + 2, :], ALU.add))
            else:
                m.step(dve.tensor_tensor(summed[:, 2 * q:2 * q + 2, :], two, out_scale[:, :].unsqueeze(1).broadcast_to((P, 2, D)), ALU.mult))
            m.wait_steps(dve)
            dve.scalar_tensor_tensor(m.X[:, 2 * q:2 * q + 2, :], summed[:, 2 * q:2 * q + 2, :], gate, m.X[:, 2 * q:2 * q + 2, :], ALU.mult, ALU.add).then_inc(m.x_done, 2)

    def tensor(pe):
        pe.wait_ge(m.x_done, m.x_at(stage, 0))
        for g in range(NG):
            if g:
                pe.wait_ge(xt.lo_ready, xt.lo_at(g))
            xt.tensor(pe, g, lambda j: m.xn_all[:, G * g + j, :])
            if experts:
                pe.wait_ge(xt.lo_ready, xt.lo_at(g + 1))
                pe.wait_ge(small_parts, 4)
                for j in range(G):
                    for c in range(KC):
                        mm = split_matmul(pe, m.bank[g][:, j * E:(j + 1) * E], (m.xt_hi[:, c, G * g + j, :], m.xt_lo[:, c, G * g + j, :]),
                                          (cen_hi[:, c, :], cen_lo[:, c, :]), c == 0, c == KC - 1)
                mm.then_inc(routed, 1)
                pe.wait_ge(gates_lo, g + 1)
                for j in range(G):
                    mm = pe.transpose(m.bank[2 + g][0:2 * GE, j * P:(j + 1) * P], f(parts[:, j, :, :]).rearrange("p k e -> p (k e)"), m.ident)
                mm.then_inc(turned, 1)
        if experts:
            pe.wait_ge(gates_t_ready, NG)
            for b in range(NB):
                pe.matmul(acc(b), gates_t[:, b, :], b2_hi[:, :], start=b % 2 == 0, stop=False, skip_group_check=True)
                pe.matmul(acc(b), gates_t[:, b, :], b2_lo[:, :], start=False, stop=False, skip_group_check=True)

        def first_products(c):
            pe.wait_ge(in_lo, c + 1)
            for t in range(2):
                after(pe, gated_ready if not experts else h_ready, 2 * (c - 1) + t + 1)
                for k in range(KC):
                    w = slice(k * P, (k + 1) * P)
                    mm = split_matmul(pe, m.bank[t][:, :], (hi[c % 2][:, w], lo[c % 2][:, w]), (m.xt_hi[:, k, side(t), :], m.xt_lo[:, k, side(t), :]), k == 0, k == KC - 1)
                if not experts:
                    mm.then_inc(h_raw, 1)
                    after(pe, u_ready, 2 * (c - 1) + t + 1)
                    for k in range(KC):
                        w = slice((KC + k) * P, (KC + k + 1) * P)
                        mm = split_matmul(pe, m.bank[2 + t][:, :], (hi[c % 2][:, w], lo[c % 2][:, w]), (m.xt_hi[:, k, side(t), :], m.xt_lo[:, k, side(t), :]), k == 0, k == KC - 1)
                    mm.then_inc(u_raw, 1)
                else:
                    after(pe, gated_ready, 2 * (c - 1) + t + 1)
                    pe.matmul(m.bank[2 + t][:, :], hi[c % 2][0:2 * GE, KC * P:(KC + 1) * P], gates_t[:, side(t), :], start=True, stop=True).then_inc(u_raw, 1)
                    mm.then_inc(h_raw, 1)

        def second_products(c):
            pe.wait_ge(out_lo, c + 1)
            for b in range(NB):
                if b % G == 0:
                    pe.wait_ge(h_lo_ready, 2 * c + b // G + 1)
                for n, (x, w) in enumerate(((h_lo, hi), (h_hi, lo), (h_hi, hi))):
                    start = not experts and c == 0 and n == 0 and b % 2 == 0
                    mm = pe.matmul(acc(b), x[c % 2][:, b, :], w[c % 2][:, IN:COLS], start=start, stop=c == chunks - 1 and n == 2, skip_group_check=True)
            mm.then_inc(used, 1)

        pe.wait_ge(xt.lo_ready, xt.lo_at(NG))
        first_products(0)
        for c in range(1, chunks):
            first_products(c)
            second_products(c - 1)
        second_products(chunks - 1)

    return {"load": load, "sync": sync, "gpsimd": gpsimd, "scalar": scalar, "vector": vector, "tensor": tensor}


def l2_attention(m, stage):
    NEG = -1e30
    s = lambda x: m.sem(f"l2a_{x}")
    norm = Norm(m, stage)
    mask_raw = m.sb("l2a_mask_raw", [P, NB, P], U8)
    mask = m.work([P, NB, P])
    below = m.work([P, NB, P])
    valid = m.sb("l2a_valid", [P, NB])
    valid_tg = m.sb("l2a_valid_tg", [P, NB])
    per_group = lambda shape: [m.work(shape) for _ in range(NG)]
    xn = [m.xn, m.work([P, G, D])]
    xt = per_group([P, KC, G, P])
    kept = per_group([P, G, P])
    masked = per_group([P, G, P])
    top = per_group([P, G])
    neg_top = per_group([P, G])
    expd = per_group([P, G, P])
    total = per_group([P, G])
    inv = per_group([P, G])
    weight = per_group([P, G])
    probs_t = per_group([P, G, P])
    mask_in, mask_ready = s("mask_in"), s("mask")
    xt_raw, xt_ready, scored, neg_ready = s("xt_raw"), s("xt"), s("scored"), s("neg")
    exp_ready, turned, probs_ready, out_ready = s("exp"), s("turned"), s("probs"), s("out")
    wide = lambda bank: bank[:, :].rearrange("p (j n) -> p j n", j=G)

    def load(sp):
        sp.dma_start(mask_raw[:, :, :], m.dram["l2a_mask"].rearrange("a (b n) -> a b n", b=NB).broadcast_to((P, NB, P))).then_inc(mask_in, 16)

    def gpsimd(pool):
        norm.gpsimd(pool, 0)
        pool.wait_ge(mask_in, 16)
        pool.wait_ge(m.x_done, m.x_at(stage, 0))
        norm.gpsimd(pool, 1)
        pool.tensor_copy(mask[:, :, :], mask_raw[:, :, :]).then_inc(mask_ready, 1)
        pool.wait_ge(mask_ready, 1)
        pool.tensor_scalar(below[:, :, :], mask[:, :, :], -1.0, -NEG, ALU.add, ALU.mult).then_inc(mask_ready, 1)

    def scalar(act):
        act.wait_ge(m.x_done, m.x_at(stage, 0))
        for g in range(NG):
            act.wait_ge(xt_raw, g + 1)
            for c in range(KC):
                act.activation(xt[g][:, c, :, :], wide(m.bank[c]), ACT.Copy).then_inc(xt_ready, 1)
        for g in range(NG):
            act.wait_ge(neg_ready, g + 1)
            for j in range(G):
                act.activation(expd[g][:, j, :], masked[g][:, j, :], ACT.Exp, bias=neg_top[g][:, j:j + 1], accum_out=total[g][:, j:j + 1]).then_inc(exp_ready, 1)
            act.wait_ge(turned, g + 1)
            act.activation(probs_t[g][:, :, :], wide(m.bank[3]), ACT.Copy).then_inc(probs_ready, 1)

    def vector(dve):
        for g in range(NG):
            norm.vector(dve, g, lambda j: xn[g][:, j, :])
        dve.wait_ge(mask_ready, 1)
        m.step(dve.reduce_max(valid[:, :], mask[:, :, :], AX_X))
        m.wait_steps(dve)
        m.step(dve.tensor_scalar(valid_tg[:, :], valid[:, :], m.tg[:, 2:3], None, ALU.mult))
        for g in range(NG):
            dve.wait_ge(scored, g + 1)
            dve.wait_ge(mask_ready, 2)
            m.step(dve.scalar_tensor_tensor(kept[g][:, :, :], wide(m.bank[2]), 1.0 / 16.0, mask[:, G * g:G * g + G, :], ALU.mult, ALU.mult))
            m.wait_steps(dve)
            m.step(dve.tensor_tensor(masked[g][:, :, :], kept[g][:, :, :], below[:, G * g:G * g + G, :], ALU.add))
            m.wait_steps(dve)
            m.step(dve.reduce_max(top[g][:, :], masked[g][:, :, :], AX_X))
            m.wait_steps(dve)
            dve.tensor_scalar(neg_top[g][:, :], top[g][:, :], -1.0, None, ALU.mult).then_inc(neg_ready, 1)
        for g in range(NG):
            dve.wait_ge(exp_ready, G * g + G)
            m.step(dve.reciprocal(inv[g][:, :], total[g][:, :]))
            m.wait_steps(dve)
            m.step(dve.tensor_tensor(weight[g][:, :], inv[g][:, :], valid_tg[:, G * g:G * g + G], ALU.mult))
            m.wait_steps(dve)
            for j in range(G):
                b = G * g + j
                dve.wait_ge(out_ready, b + 1)
                dve.scalar_tensor_tensor(m.X[:, b, :], m.bank[4 + j][:, 0:D], weight[g][:, j:j + 1], m.X[:, b, :], ALU.mult, ALU.add).then_inc(m.x_done, 1)

    def tensor(pe):
        pe.wait_ge(m.ctx_in, 16)
        pe.wait_ge(m.cn_in, 16)
        pe.wait_ge(m.x_done, m.x_at(stage, 0))
        for g in range(NG):
            pe.wait_ge(norm.xn, norm.xn_at(G * g + G))
            after(pe, xt_ready, KC * g)
            for c in range(KC):
                for j in range(G):
                    mm = pe.transpose(m.bank[c][:, j * P:(j + 1) * P], xn[g][:, j, c * P:(c + 1) * P], m.ident)
            mm.then_inc(xt_raw, 1)
            pe.wait_ge(xt_ready, KC * g + KC)
            after(pe, neg_ready, g)
            for j in range(G):
                for c in range(KC):
                    mm = pe.matmul(m.bank[2][:, j * P:(j + 1) * P], xt[g][:, c, j, :], m.CT[:, c, G * g + j, :], start=c == 0, stop=c == KC - 1)
            mm.then_inc(scored, 1)
        for g in range(NG):
            after(pe, probs_ready, g)
            for j in range(G):
                pe.wait_ge(exp_ready, G * g + j + 1)
                mm = pe.transpose(m.bank[3][:, j * P:(j + 1) * P], expd[g][:, j, :], m.ident)
            mm.then_inc(turned, 1)
            pe.wait_ge(probs_ready, g + 1)
            for j in range(G):
                if g:
                    pe.wait_ge(m.x_done, m.x_at(stage, G * (g - 1) + j + 1))
                pe.matmul(m.bank[4 + j][:, 0:D], probs_t[g][:, j, :], m.CN[:, G * g + j, :], start=True, stop=True).then_inc(out_ready, 1)

    return {"load": load, "gpsimd": gpsimd, "scalar": scalar, "vector": vector, "tensor": tensor}


def l3_attention(m, stage):
    T = P + 1
    NEG = -1e38
    s = lambda x: m.sem(f"l3a_{x}")
    norm = Norm(m, stage)
    wu = m.sb("l3a_wu", [P, KC, 2])
    full = lambda: [m.work([P, NB, T]) for _ in range(KC)]
    plain = lambda: [m.work([P, NB, P]) for _ in range(KC)]
    k, decay, o, fade, enter, entered = full(), full(), full(), full(), full(), full()
    p_sum, q_sum = k, decay
    lead, a, e = plain(), plain(), plain()
    wu_in, edges, decay_ready, xt_raw, k_ready = s("wu_in"), s("edges"), s("decay"), s("xt_raw"), s("k")
    diffs, pool_diffs, exps, entered_ready = s("diffs"), s("pool_diffs"), s("exps"), s("entered")
    p_ready, pool_terms, y_ready, turned = s("p"), s("pool_terms"), s("y"), s("turned")
    PIECES = NG * KC
    of = lambda t, n: t[n % KC][:, n // KC * G:n // KC * G + G, :]
    row = lambda t, n: of(t, n).rearrange("p b t -> p (b t)")
    past = lambda t, n: of(t, n)[:, :, 0:P]
    here = lambda t, n: of(t, n)[:, :, 1:T]

    def load(sp):
        sp.dma_start(wu[:, :, :], m.dram["l3a_wu"].rearrange("p (c k) -> p c k", c=KC)).then_inc(wu_in, 16)

    def in_turn(front, back):
        for n in range(PIECES + 1):
            if n < PIECES:
                front(n)
            if n:
                back(n - 1)

    def gpsimd(pool):
        norm.gpsimd(pool, 0)
        pool.wait_ge(m.x_done, m.x_at(stage, 0))
        for c in range(KC):
            pool.memset(k[c][:, :, 0:1], NEG).then_inc(edges, 1)
            pool.memset(decay[c][:, :, 0:1], NEG).then_inc(edges, 1)
            pool.memset(fade[c][:, :, 0:1], 0.0).then_inc(edges, 1)
            pool.memset(enter[c][:, :, 0:1], 0.0).then_inc(edges, 1)
            pool.memset(entered[c][:, :, 0:1], 0.0).then_inc(edges, 1)
            pool.memset(o[c][:, :, :], 0.0).then_inc(edges, 1)
        norm.gpsimd(pool, 1)

        def front(n):
            pool.wait_ge(diffs, 3 * n + 1)
            pool.tensor_tensor(here(enter, n), here(k, n), here(o, n), ALU.subtract).then_inc(pool_diffs, 1)
            pool.wait_ge(diffs, 3 * n + 2)
            pool.tensor_tensor(of(a, n), past(o, n), of(lead, n), ALU.subtract).then_inc(pool_diffs, 1)

        def back(n):
            v = m.CT[:, n % KC, n // KC * G:n // KC * G + G, :]
            pool.wait_ge(exps, 4 * n + 2)
            pool.tensor_tensor(here(entered, n), here(enter, n), v, ALU.mult).then_inc(entered_ready, 1)
            pool.wait_ge(exps, 4 * n + 4)
            pool.tensor_tensor(of(lead, n), of(e, n), v, ALU.mult).then_inc(pool_terms, 1)
            pool.wait_ge(p_ready, n + 1)
            pool.tensor_tensor(here(fade, n), of(a, n), past(p_sum, n), ALU.mult).then_inc(pool_terms, 1)
            pool.wait_ge(pool_terms, 3 * n + 2)
            pool.tensor_tensor(here(fade, n), here(fade, n), of(lead, n), ALU.add).then_inc(pool_terms, 1)

        in_turn(front, back)

    def scalar(act):
        act.wait_ge(m.x_done, m.x_at(stage, 0))
        act.wait_ge(wu_in, 16)
        act.wait_ge(edges, 6 * KC)
        for c in range(KC):
            act.activation(decay[c][:, :, 1:T], o[c][:, :, 1:T], ACT.Identity, bias=wu[:, c, 0:1]).then_inc(decay_ready, 1)
        for g in range(NG):
            act.wait_ge(xt_raw, g + 1)
            for c in range(KC):
                act.activation(k[c][:, G * g:G * g + G, 1:T], m.bank[2 * g + c][:, :].rearrange("p (j n) -> p j n", j=G), ACT.Copy).then_inc(k_ready, 1)
        for n in range(PIECES):
            for ready, count, x in ((diffs, 3 * n + 1, here(fade, n)), (pool_diffs, 2 * n + 1, here(enter, n)),
                                    (pool_diffs, 2 * n + 2, of(a, n)), (diffs, 3 * n + 3, of(e, n))):
                act.wait_ge(ready, count)
                act.activation(x, x, ACT.Exp).then_inc(exps, 1)

    def vector(dve):
        for g in range(NG):
            norm.vector(dve, g, lambda j: m.xn_all[:, G * g + j, :])
        dve.wait_ge(decay_ready, KC)
        dve.wait_ge(wu_in, 16)

        def front(n):
            w, u = wu[:, n % KC, 0:1], wu[:, n % KC, 1:2]
            dve.wait_ge(k_ready, n + 1)
            m.step(dve.tensor_tensor_scan(row(o, n), row(decay, n), row(k, n), NEG, ALU.add, ALU.max))
            m.wait_steps(dve)
            dve.scalar_tensor_tensor(here(fade, n), past(o, n), w, here(o, n), ALU.add, ALU.subtract).then_inc(diffs, 1)
            dve.scalar_tensor_tensor(of(lead, n), here(k, n), u, past(o, n), ALU.add, ALU.max).then_inc(diffs, 1)
            dve.wait_ge(diffs, 3 * n + 2)
            dve.scalar_tensor_tensor(of(e, n), here(k, n), u, of(lead, n), ALU.add, ALU.subtract).then_inc(diffs, 1)

        def back(n):
            dve.wait_ge(exps, 4 * n + 2)
            m.step(dve.tensor_tensor_scan(row(q_sum, n), row(fade, n), row(enter, n), 0.0, ALU.mult, ALU.add))
            dve.wait_ge(entered_ready, n + 1)
            dve.wait_ge(exps, 4 * n + 4)
            dve.tensor_tensor_scan(row(p_sum, n), row(fade, n), row(entered, n), 0.0, ALU.mult, ALU.add).then_inc(p_ready, 1)
            den = here(enter, n)
            m.wait_steps(dve)
            m.step(dve.tensor_tensor(den, of(a, n), past(q_sum, n), ALU.mult))
            m.wait_steps(dve)
            m.step(dve.tensor_tensor(den, den, of(e, n), ALU.add))
            m.wait_steps(dve)
            m.step(dve.reciprocal(den, den))
            m.wait_steps(dve)
            dve.wait_ge(pool_terms, 3 * n + 3)
            dve.tensor_tensor(of(a, n), here(fade, n), den, ALU.mult).then_inc(y_ready, 1)
            if n % KC == 0 and n:
                add(n // KC - 1)

        def add(g):
            for q in range(G // 2 * g, G // 2 * (g + 1)):
                dve.wait_ge(turned, q + 1)
                dve.scalar_tensor_tensor(m.X[:, 2 * q:2 * q + 2, :], m.bank[4 + q][:, :].rearrange("p (j n) -> p j n", j=2), m.tg[:, 3:4],
                                         m.X[:, 2 * q:2 * q + 2, :], ALU.mult, ALU.add).then_inc(m.x_done, 2)

        in_turn(front, back)
        add(NG - 1)

    def tensor(pe):
        pe.wait_ge(m.x_done, m.x_at(stage, 0))
        for g in range(NG):
            pe.wait_ge(norm.xn, norm.xn_at(G * g + G))
            for c in range(KC):
                for j in range(G):
                    mm = pe.transpose(m.bank[2 * g + c][:, j * P:(j + 1) * P], m.xn_all[:, G * g + j, c * P:(c + 1) * P], m.ident)
            mm.then_inc(xt_raw, 1)
        for q in range(NB // 2):
            pe.wait_ge(y_ready, KC * (2 * q // G + 1))
            for j in range(2):
                for c in range(KC):
                    mm = pe.transpose(m.bank[4 + q][:, j * D + c * P:j * D + (c + 1) * P], a[c][:, 2 * q + j, :], m.ident)
            mm.then_inc(turned, 1)

    return {"load": load, "gpsimd": gpsimd, "scalar": scalar, "vector": vector, "tensor": tensor}


def program(nc, dram, out):
    with ExitStack() as ctx:
        m = Machine(nc, ctx, dram)
        builders = [
            l0_attention,
            lambda m, n: adapters(m, n, "l0f", True),
            l1_attention,
            lambda m, n: feed_forward(m, n, "l1f", dram["l1f_w"].shape[0], True),
            l2_attention,
            lambda m, n: feed_forward(m, n, "l2f", dram["l2f_w"].shape[0], False),
            l3_attention,
            lambda m, n: adapters(m, n, "l3f", False),
        ]
        stages = []
        for n, build in enumerate(builders[:STAGES]):
            m.used = {"f": 0, "r": 0}
            stages.append(build(m, n))
        stored = m.sem("stored")
        block = ctx.enter_context(nc.Block())

        @block.sync
        def _(sp):
            for stage in stages:
                stage["load"](sp)
            for stage in stages:
                if "sync" in stage:
                    stage["sync"](sp)
            y = out.rearrange("b s d -> s b d")
            for g in range(NG):
                sp.wait_ge(m.x_done, m.x_at(len(stages) - 1, G * g + G))
                sp.dma_start(y[:, G * g:G * g + G, :], m.X[:, G * g:G * g + G, :]).then_inc(stored, 16)
            sp.wait_ge(stored, 16 * NG)

        @block.gpsimd
        def _(pool):
            for stage in stages:
                stage["gpsimd"](pool)

        @block.scalar
        def _(act):
            for stage in stages:
                stage["scalar"](act)

        @block.vector
        def _(dve):
            for stage in stages:
                stage["vector"](dve)

        @block.tensor
        def _(pe):
            for stage in stages:
                stage["tensor"](pe)


def widths_on_partitions(w):
    w = np.asarray(w)
    return np.ascontiguousarray(w.reshape(-1, P, w.shape[1]).transpose(1, 0, 2).reshape(P, -1))


def by_rank(w):
    return np.asarray(w).transpose(1, 0, 2).reshape(D, -1)


def constants():
    rows = np.arange(P)
    c = np.zeros((P, CONST_COLS), np.float32)
    c[:, 0:P] = np.eye(P)
    c[:, P:2 * P] = rows[:, None] // 16 == rows[None, :] // 16
    c[:, 2 * P:2 * P + 8] = rows[:, None] // 16 == np.arange(8)[None, :]
    c[:, 2 * P + 8:2 * P + 16] = -0.5
    c[:, 2 * P + 16] = rows % 64 == 48
    return c


def stack_selectors():
    sel = np.zeros((P, 4, 4, P), np.float32)
    for kind, places in enumerate(((0, 2), (1,), (0, 1), (2,))):
        for pair in range(4):
            for a in range(2):
                for t in places:
                    for d in range(16):
                        sel[32 * pair + 16 * a + d, kind, pair, 64 * a + 16 * t + d] = 1
    return sel.reshape(P, -1)


def output_selectors():
    sel = np.zeros((P, 2, 2, P), np.float32)
    for h in range(8):
        for d in range(16):
            for kind in range(2):
                sel[32 * (h // 2) + 16 * kind + d, kind, h % 2, 16 * h + d] = 1
    return sel.reshape(P, -1)


def padded(w, n, axis):
    w = np.asarray(w)
    fill = list(w.shape)
    fill[axis] = n - w.shape[axis]
    return np.concatenate([w, np.zeros(fill, w.dtype)], axis=axis)


def expert_chunks(a):
    w1 = np.concatenate([np.asarray(a["L1_ffn_routed_w1"]), np.asarray(a["L1_ffn_shared_w1"])])
    w2 = np.concatenate([np.asarray(a["L1_ffn_routed_w2"]), np.asarray(a["L1_ffn_shared_w2"])])
    b1 = np.concatenate([np.asarray(a["L1_ffn_routed_b1"]), np.asarray(a["L1_ffn_shared_b1"])])
    b2 = np.concatenate([np.asarray(a["L1_ffn_routed_b2"]), np.asarray(a["L1_ffn_shared_b2"])])
    n, _, f = w1.shape
    chunks = -(-n * f // P)
    w1 = padded(w1.transpose(1, 0, 2).reshape(D, n * f), chunks * P, 1).reshape(KC, P, chunks, P)
    w2 = padded(w2.reshape(n * f, D), chunks * P, 0).reshape(chunks, P, D)
    expert = np.arange(chunks * P) // f
    sel = np.zeros((P, chunks * P), np.float32)
    for part in range(2):
        sel[part * n:(part + 1) * n] = expert[None, :] == np.arange(n)[:, None]
    blob = np.concatenate([w1[0].transpose(1, 0, 2), w1[1].transpose(1, 0, 2), sel.reshape(P, chunks, P).transpose(1, 0, 2), w2], axis=2)
    return blob, padded(b1.reshape(-1), chunks * P, 0).reshape(chunks, P).T, np.concatenate([b2, b2])


def swiglu_chunks(a):
    gate, up, down = (np.asarray(a[f"L2_ffn_{n}_w"]) for n in ("gate", "up", "down"))
    chunks = -(-gate.shape[0] // P)
    first = [padded(w, chunks * P, 0).reshape(chunks, P, KC, P).transpose(0, 3, 2, 1).reshape(chunks, P, KC * P) for w in (gate, up)]
    second = padded(down, chunks * P, 1).T.reshape(chunks, P, D)
    scales = np.stack([padded(a[f"L2_ffn_{n}_s"], chunks * P, 0).reshape(chunks, P).T for n in ("gate", "up")], axis=1)
    return np.concatenate(first + [second], axis=2), scales.reshape(P, -1)


def layouts(a):
    row = lambda v: np.asarray(v).reshape(1, -1)
    l1f_w, l1f_b1, l1f_b2 = expert_chunks(a)
    l2f_w, l2f_scales = swiglu_chunks(a)
    return {
        "x": a["x"],
        "ctx": a["ctx_2048"],
        "ctx_t": np.ascontiguousarray(np.asarray(a["ctx_2048"]).transpose(2, 0, 1).reshape(KC, P, NB, P).transpose(1, 0, 2, 3).reshape(P, -1)),
        "const": constants(),
        "gates": row(np.concatenate([a["g_xattn"], a["g_ffn"]])),
        "l0a_w": widths_on_partitions(np.concatenate([np.asarray(a["L0_xattn_Wkv"]).T, np.asarray(a["L0_xattn_Wq"]).T,
                                                      np.asarray(a["L0_xattn_Wg"]).T, np.asarray(a["L0_xattn_Wo"]).T], axis=1)),
        "l0a_bg": row(a["L0_xattn_bg"]),
        "l0f_w": widths_on_partitions(np.concatenate([by_rank(a["L0_ffn_Wd"]), np.asarray(a["L0_ffn_Wr"])], axis=1)),
        "l0f_up": np.asarray(a["L0_ffn_Wu"]).reshape(P, D),
        "l0f_bias": row(np.concatenate([np.asarray(a["L0_ffn_bd"]).reshape(-1), np.asarray(a["L0_ffn_br"])])),
        "l0f_up_bias": a["L0_ffn_bu"],
        "l1a_sel": stack_selectors(),
        "l1a_out_sel": output_selectors(),
        "l1a_gamma": row(a["L1_xattn_gamma"]),
        "l1f_w": l1f_w,
        "l1f_b1": l1f_b1,
        "l1f_b2": l1f_b2,
        "l1f_cen": widths_on_partitions(np.asarray(a["L1_ffn_centroids"]).T),
        "l1f_bias": row(a["L1_ffn_bias"]),
        "l2a_mask": row(a["mask_BxS2_bk0"]),
        "l2f_w": l2f_w,
        "l2f_scales": l2f_scales,
        "l2f_out_scale": row(a["L2_ffn_down_s"]),
        "l3a_wu": widths_on_partitions(np.stack([np.asarray(a["L3_xattn_w"]), np.asarray(a["L3_xattn_u"])], axis=1)),
        "l3f_w": widths_on_partitions(np.concatenate([by_rank(a["L3_ffn_experts_down"]), np.asarray(a["L3_ffn_router_w"]).T], axis=1)),
        "l3f_up": np.asarray(a["L3_ffn_experts_up"]).reshape(P, D),
    }


def kernel(**inputs):
    import concourse.bacc as bacc
    from concourse.bass_utils import run_bass_kernel_spmd

    arrays = {name: np.ascontiguousarray(v) for name, v in layouts(inputs).items()}
    nc = bacc.Bacc("TRN2", target_bir_lowering=False, num_devices=1)
    dram = {name: nc.dram_tensor(f"in_{name}", v.shape, mybir.dt.from_np(v.dtype), kind="ExternalInput").ap() for name, v in arrays.items()}
    out = nc.dram_tensor("out_x", (NB, P, D), F32, kind="ExternalOutput").ap()
    program(nc, dram, out)
    got = run_bass_kernel_spmd(nc, [{f"in_{name}": v for name, v in arrays.items()}], core_ids=[0])
    return got.results[0]["out_x"]
```

```python
from contextlib import ExitStack

import numpy as np

import concourse.bass as bass
from concourse import mybir

ALU = mybir.AluOpType
ACT = mybir.ActivationFunctionType
F32 = mybir.dt.float32
F32R = mybir.dt.float32r
U8 = mybir.dt.uint8
AX_X = mybir.AxisListType.X

P = 128
NB = 8
D = 256
KC = D // P
G = 4
NG = NB // G
BIG = 3.0e38
LN_EPS = 1e-5

STAGES = 8


class Machine:

    def __init__(self, nc, ctx, dram):
        self.nc, self.ctx, self.dram = nc, ctx, dram

        self.X = self.sb("X", [P, NB, D])
        self.CT = self.sb("CT", [P, KC, NB, P])
        self.CN = self.sb("CN", [P, NB, D])
        self.const = self.sb("const", [P, CONST_COLS])
        self.ident = self.const[:, 0:P]
        self.blockdiag = self.const[:, P:2 * P]
        self.headcol = self.const[:, 2 * P:2 * P + 8]
        self.minus_half = self.const[:, 2 * P + 8:2 * P + 16]
        self.one_row = self.const[:, 2 * P + 16:2 * P + 17]
        self.gates_raw = self.sb("gates_raw", [P, 8])
        self.tg = self.sb("tg", [P, 8])
        self.xn = self.sb("xn", [P, G, D])
        self.xn_all = self.sb("xn_all", [P, NB, D])
        self.stats = self.sb("stats", [P, G, 6])
        self.mv = self.sb("mv", [P, G, 2])
        self.veps = self.sb("veps", [P, G])
        self.rstd = self.sb("rstd", [P, G])
        self.xt_hi = self.sb("xt_hi", [P, KC, NB, P], F32R)
        self.xt_lo = self.sb("xt_lo", [P, KC, NB, P], F32R)
        self.bank = [ctx.enter_context(nc.psum_tensor(f"bank{i}", [P, 512], F32)) for i in range(8)]

        self.arena_f = self.sb("arena_f", [P, ARENA_F])
        self.arena_r = self.sb("arena_r", [P, ARENA_R], F32R)
        self.used = {"f": 0, "r": 0}
        self.ring_raw = [self.sb(f"ring_raw{i}", [P, 6 * P]) for i in range(2)]
        self.ring_hi = [self.sb(f"ring_hi{i}", [P, 6 * P], F32R) for i in range(2)]
        self.ring_lo = [self.sb(f"ring_lo{i}", [P, 6 * P], F32R) for i in range(2)]
        self.x_done = self.sem("x_done")
        self.x_in = [self.sem(f"x_in{g}") for g in range(NG)]
        self.vector_steps = self.sem("vector_steps")
        self.steps = 0
        self.norm_mv, self.norm_veps = self.sem("norm_mv"), self.sem("norm_veps")
        self.norm_rstd, self.norm_xn = self.sem("norm_rstd"), self.sem("norm_xn")
        self.xt_raw, self.xt_hi_ready, self.xt_lo_ready = self.sem("xt_raw"), self.sem("xt_hi"), self.sem("xt_lo")
        self.transposed = 0
        self.const_in = self.sem("const_in")
        self.ctx_in = self.sem("ctx_in")
        self.cn_in = self.sem("cn_in")
        self.tg_ready = self.sem("tg_ready")

    def step(self, instruction):
        instruction.then_inc(self.vector_steps, 1)
        self.steps += 1

    def wait_steps(self, dve):
        dve.wait_ge(self.vector_steps, self.steps)

    def sb(self, name, shape, dt=F32):
        return self.ctx.enter_context(self.nc.sbuf_tensor(name, shape, dt))

    def work(self, shape, dt=F32):
        size = int(np.prod(shape[1:]))
        arena, name = (self.arena_r, "r") if dt == F32R else (self.arena_f, "f")
        a = self.used[name]
        self.used[name] += size
        view = arena[0:shape[0], a:a + size]
        if len(shape) > 2:
            dims = " ".join(f"d{n}" for n in range(len(shape) - 1))
            view = view.rearrange(f"p ({dims}) -> p {dims}", **{f"d{n}": v for n, v in enumerate(shape[1:])})
        return view

    def sem(self, name):
        return self.ctx.enter_context(self.nc.semaphore(name))

    def x_at(self, stage, b):
        return NB * stage + b


CONST_COLS = 2 * P + 20
ARENA_F = 19000
ARENA_R = 9216


def f(view):
    return view.bitcast(F32)


def split_matmul(pe, out, lhs, rhs, start, stop, **kw):
    (lh, ll), (rh, rl) = lhs, rhs
    pe.matmul(out, ll, rh, start=start, stop=False, **kw)
    pe.matmul(out, lh, rl, start=False, stop=False, **kw)
    return pe.matmul(out, lh, rh, start=False, stop=stop, **kw)


class Norm:

    def __init__(self, m, stage):
        self.m, self.stage = m, stage
        self.passed = stage * NG
        self.mv, self.veps, self.rstd, self.xn = m.norm_mv, m.norm_veps, m.norm_rstd, m.norm_xn

    def xn_at(self, n):
        return G * self.passed + n

    def vector(self, dve, g, out):
        self.moments(dve, g)
        self.scale(dve, g, out)

    def moments(self, dve, g):
        m = self.m
        for j in range(G):
            if self.stage:
                dve.wait_ge(m.x_done, m.x_at(self.stage - 1, G * g + j + 1))
            else:
                dve.wait_ge(m.x_in[g], 16)
            m.step(dve.bn_stats(m.stats[:, j, :], m.X[:, G * g + j, :]))
        for j in range(G):
            m.wait_steps(dve)
            dve.bn_aggr(m.mv[:, j, :], m.stats[:, j, :]).then_inc(self.mv, 1)

    def scale(self, dve, g, out):
        m = self.m
        dve.wait_ge(self.rstd, self.passed + g + 1)
        for j in range(G):
            b = G * g + j
            dve.tensor_scalar(out(j), m.X[:, b, :], m.mv[:, j, 0:1], m.rstd[:, j:j + 1],
                              ALU.subtract, ALU.mult).then_inc(self.xn, 1)

    def gpsimd(self, pool, g):
        m = self.m
        pool.wait_ge(self.mv, self.xn_at(G * g + G))
        pool.tensor_scalar(m.veps[:, :], m.mv[:, :, 1], LN_EPS, None, ALU.add).then_inc(self.veps, 1)
        pool.wait_ge(self.veps, self.passed + g + 1)
        pool.tensor_tensor(m.rstd[:, :], m.veps[:, :], m.minus_half[:, 0:G], ALU.pow).then_inc(self.rstd, 1)


class Transposed:

    def __init__(self, m, banks, norm, hi=None, lo=None):
        self.m, self.banks, self.norm = m, banks, norm
        self.hi = hi or (lambda g, c: m.xt_hi[:, c, 0:G, :])
        self.lo = lo or (lambda g, c: m.xt_lo[:, c, 0:G, :])
        self.passed = m.transposed
        m.transposed += NG
        self.raw, self.hi_ready, self.lo_ready = m.xt_raw, m.xt_hi_ready, m.xt_lo_ready

    def lo_at(self, groups):
        return KC * (self.passed + groups)

    def tensor(self, pe, g, xn):
        pe.wait_ge(self.norm.xn, self.norm.xn_at(G * g + G))
        for c in range(KC):
            for j in range(G):
                mm = pe.transpose(self.banks[g][c][:, j * P:(j + 1) * P], xn(j)[:, c * P:(c + 1) * P], self.m.ident)
        mm.then_inc(self.raw, 1)

    def bank(self, g, c):
        return self.banks[g][c][:, :].rearrange("p (j n) -> p j n", j=G)

    def scalar(self, act, g):
        act.wait_ge(self.raw, self.passed + g + 1)
        for c in range(KC):
            act.activation(self.hi(g, c), self.bank(g, c), ACT.Copy).then_inc(self.hi_ready, 1)

    def vector(self, dve, g):
        for c in range(KC):
            dve.wait_ge(self.hi_ready, KC * (self.passed + g) + c + 1)
            dve.tensor_tensor(self.lo(g, c), self.bank(g, c), f(self.hi(g, c)), ALU.subtract).then_inc(self.lo_ready, 1)


def after(engine, sem, count):
    if not (isinstance(count, int) and count <= 0):
        engine.wait_ge(sem, count)


def over_chunks(engine, chunks, body):
    for c in range(2):
        body(c, c)
    end = 2 + (chunks - 3) // 2 * 2
    if end > 4:
        with engine.Fori(2, end, 2) as c:
            body(c, 0)
            body(c + 1, 1)
    else:
        for c in range(2, end):
            body(c, c % 2)
    for c in range(end, chunks):
        body(c, c % 2)


def l0_attention(m, stage):
    HD = 16
    s = lambda name: m.sem(f"l0a_{name}")
    norm = Norm(m, stage)
    cols = {"kv": (0, 2 * D), "q": (2 * D, 3 * D), "g": (3 * D, 4 * D), "o": (4 * D, 5 * D)}
    W = m.work([P, KC, 5 * D])
    W_hi = m.work([P, KC, 5 * D], F32R)
    W_lo = m.work([P, KC, 5 * D], F32R)
    bg = m.work([P, D])
    ct_hi = m.work([P, KC, G, P], F32R)
    ct_lo = m.work([P, KC, G, P], F32R)
    k_min = m.work([P, G, D])
    k_exp = m.work([P, G, D])
    k_feat = m.work([P, G, D])
    v_one = m.work([P, G, KC, P + 1])
    q_min = m.work([P, KC, G * P])
    q_exp = m.work([P, KC, G * P])
    q_feat = m.work([P, KC, G * P])
    g_sum = m.work([P, G, D])
    g_tanh = m.work([P, G, D])
    summary = m.work([P, G, KC, P + 8])
    z_den = m.work([P, G, KC, 8])
    z = m.work([P, G, KC, 8])
    attn = m.work([P, G, D])
    gated = m.work([P, G, D])
    gt_hi = m.work([P, G, KC, P], F32R)
    gt_lo = m.work([P, G, KC, P], F32R)
    half_tg = m.work([P, 1])
    xn = [m.xn, m.work([P, G, D])]

    kv_w_in, w_in, w_hi_ready, w_lo_ready, bg_in, ones_ready = s("kv_w_in"), s("w_in"), s("w_hi"), s("w_lo"), s("bg_in"), s("ones")
    ct_hi_ready, ct_ready = s("ct_hi"), s("ct")
    kv_proj, k_min_ready, k_exp_ready, k_ready, v_ready = s("kv_proj"), s("k_min"), s("k_exp"), s("k"), s("v")
    q_proj, q_min_ready, q_exp_ready, q_ready = s("q_proj"), s("q_min"), s("q_exp"), s("q")
    g_proj, g_sum_ready, g_tanh_ready = s("g_proj"), s("g_sum"), s("g_tanh")
    kv_sum, summary_ready, num_ready = s("kv_sum"), s("summary"), s("num")
    attn_ready, gated_ready, gt_raw, gt_hi_ready, gt_lo_ready, out_ready = s("attn"), s("gated"), s("gt_raw"), s("gt_hi"), s("gt_lo"), s("out")

    kv_bank = [m.bank[0], m.bank[1]]
    xt = Transposed(m, [[m.bank[2], m.bank[3]]] * NG, norm)
    q_bank = [m.bank[4], m.bank[5]]
    g_bank = lambda j: m.bank[6 + j // 2][:, (j % 2) * D:(j % 2 + 1) * D]
    sum_bank = lambda j: m.bank[j % 2][:, :].rearrange("p (c n) -> p c n", c=KC)
    num_bank = lambda j: m.bank[2 + j % 2][:, :].rearrange("p (c n) -> p c n", c=KC)
    gt_bank = lambda j: m.bank[4 + j % 2][:, 0:D].rearrange("p (c n) -> p c n", c=KC)
    out_bank = lambda j: m.bank[6 + j % 2][:, 0:D]

    def load(sp):
        w = m.dram["l0a_w"].rearrange("p (c n) -> p c n", c=KC)
        x = m.dram["x"].rearrange("b s d -> s b d")
        sp.dma_start(m.CT[:, :, :, :], m.dram["ctx_t"].rearrange("p (c b n) -> p c b n", c=KC, b=NB)).then_inc(m.ctx_in, 16)
        sp.dma_start(W[:, :, 0:2 * D], w[:, :, 0:2 * D]).then_inc(kv_w_in, 16)
        sp.dma_start(m.X[:, 0:G, :], x[:, 0:G, :]).then_inc(m.x_in[0], 16)
        sp.dma_start(m.const[:, :], m.dram["const"]).then_inc(m.const_in, 16)
        sp.dma_start(m.gates_raw[:, :], m.dram["gates"].broadcast_to((P, 8))).then_inc(m.const_in, 16)
        sp.dma_start(W[:, :, 2 * D:5 * D], w[:, :, 2 * D:5 * D]).then_inc(w_in, 16)
        sp.dma_start(bg[:, :], m.dram["l0a_bg"].broadcast_to((P, D))).then_inc(bg_in, 16)
        sp.dma_start(m.X[:, G:NB, :], x[:, G:NB, :]).then_inc(m.x_in[1], 16)
        sp.dma_start(m.CN[:, :, :], m.dram["ctx"].rearrange("b s d -> s b d")).then_inc(m.cn_in, 16)

    def gpsimd(pool):
        pool.memset(v_one[:, :, :, P:P + 1], 1.0).then_inc(ones_ready, 1)
        pool.wait_ge(m.const_in, 32)
        for g in range(NG):
            norm.gpsimd(pool, g)
        pool.wait_ge(kv_proj, G)
        pool.wait_ge(m.ctx_in, 16)
        for c in range(KC):
            pool.tensor_copy(ct_hi[:, c, :, :], m.CT[:, c, G:NB, :]).then_inc(ct_hi_ready, 1)
            pool.wait_ge(ct_hi_ready, KC + c + 1)
            pool.tensor_tensor(ct_lo[:, c, :, :], m.CT[:, c, G:NB, :], f(ct_hi[:, c, :, :]), ALU.subtract).then_inc(ct_ready, 1)

    def scalar(act):
        def keys(g):
            for j in range(G):
                act.wait_ge(k_min_ready, G * g + j + 1)
                act.activation(k_exp[:, j, :], k_min[:, j, :], ACT.Exp).then_inc(k_exp_ready, 1)
                act.wait_ge(k_ready, G * g + j + 1)
                act.activation(v_one[:, j, :, 0:P], kv_bank[j % 2][:, D:2 * D].rearrange("p (c n) -> p c n", c=KC), ACT.Copy).then_inc(v_ready, 1)

        def queries(g):
            xt.scalar(act, g)
            for c in range(KC):
                act.wait_ge(q_min_ready, KC * g + c + 1)
                act.activation(q_exp[:, c, :], q_min[:, c, :], ACT.Exp).then_inc(q_exp_ready, 1)
            for h in range(0, G, 2):
                act.wait_ge(g_sum_ready, (G * g + h) // 2 + 1)
                act.activation(g_tanh[:, h:h + 2, :], g_sum[:, h:h + 2, :], ACT.Tanh, scale=0.5).then_inc(g_tanh_ready, 1)

        def gated_turned(g):
            for j in range(G):
                act.wait_ge(gt_raw, G * g + j + 1)
                act.activation(gt_hi[:, j, :, :], gt_bank(j), ACT.Copy).then_inc(gt_hi_ready, 1)

        act.wait_ge(m.ctx_in, 16)
        for c in range(KC):
            act.activation(ct_hi[:, c, :, :], m.CT[:, c, 0:G, :], ACT.Copy).then_inc(ct_hi_ready, 1)
        act.wait_ge(kv_w_in, 16)
        act.activation(W_hi[:, :, 0:2 * D], W[:, :, 0:2 * D], ACT.Copy).then_inc(w_hi_ready, 1)
        act.wait_ge(m.const_in, 32)
        act.activation(m.tg[:, :], m.gates_raw[:, :], ACT.Tanh).then_inc(m.tg_ready, 1)
        act.wait_ge(w_in, 16)
        act.activation(W_hi[:, :, 2 * D:5 * D], W[:, :, 2 * D:5 * D], ACT.Copy).then_inc(w_hi_ready, 1)
        act.wait_ge(ones_ready, 1)
        keys(0)
        for g in range(NG):
            queries(g)
            if g + 1 < NG:
                keys(g + 1)
            gated_turned(g)

    def vector(dve, next_moments, next_head):
        def weights(n):
            a, b = ((0, 2 * D), (2 * D, 5 * D))[n]
            dve.wait_ge(w_hi_ready, n + 1)
            dve.tensor_tensor(W_lo[:, :, a:b], W[:, :, a:b], f(W_hi[:, :, a:b]), ALU.subtract).then_inc(w_lo_ready, 1)

        def keys(g):
            for j in range(G):
                dve.wait_ge(kv_proj, G * g + j + 1)
                dve.tensor_scalar(k_min[:, j, :], kv_bank[j % 2][:, 0:D], 0.0, None, ALU.min).then_inc(k_min_ready, 1)
                dve.wait_ge(k_exp_ready, G * g + j + 1)
                dve.scalar_tensor_tensor(k_feat[:, j, :], kv_bank[j % 2][:, 0:D], 0.0, k_exp[:, j, :], ALU.max, ALU.add).then_inc(k_ready, 1)

        def queries(g):
            if g == NG - 1:
                next_moments(dve, 0)
            xt.vector(dve, g)
            if g == NG - 1:
                next_head(dve)
            for c in range(KC):
                dve.wait_ge(q_proj, KC * g + c + 1)
                dve.tensor_scalar(q_min[:, c, :], q_bank[c][:, :], 0.0, None, ALU.min).then_inc(q_min_ready, 1)
                dve.wait_ge(q_exp_ready, KC * g + c + 1)
                dve.scalar_tensor_tensor(q_feat[:, c, :], q_bank[c][:, :], 0.0, q_exp[:, c, :], ALU.max, ALU.add).then_inc(q_ready, 1)
            dve.wait_ge(bg_in, 16)
            for h in range(0, G, 2):
                dve.wait_ge(g_proj, G * g + h + 2)
                dve.tensor_tensor(g_sum[:, h:h + 2, :], m.bank[6 + h // 2][:, :].rearrange("p (j n) -> p j n", j=2),
                                  bg[:, :].unsqueeze(1).broadcast_to((P, 2, D)), ALU.add).then_inc(g_sum_ready, 1)

        def summaries(g):
            for j in range(G):
                dve.wait_ge(kv_sum, G * g + j + 1)
                dve.tensor_tensor(summary[:, j, :, 0:P], sum_bank(j)[:, :, 0:P],
                                  m.blockdiag.unsqueeze(1).broadcast_to((P, KC, P)), ALU.mult)
                dve.tensor_tensor(summary[:, j, :, P:P + 8], sum_bank(j)[:, :, P:P + 1].broadcast_to((P, KC, 8)),
                                  m.headcol.unsqueeze(1).broadcast_to((P, KC, 8)), ALU.mult).then_inc(summary_ready, 1)

        def attention(g):
            for j in range(G):
                dve.wait_ge(num_ready, G * g + j + 1)
                m.step(dve.tensor_scalar(z_den[:, j, :, :], num_bank(j)[:, :, P:P + 8], 1e-6, None, ALU.add))
                m.wait_steps(dve)
                m.step(dve.reciprocal(z[:, j, :, :], z_den[:, j, :, :]))
                m.wait_steps(dve)
                dve.tensor_tensor(attn[:, j, :].rearrange("p (c h d) -> p c h d", c=KC, h=8),
                                  num_bank(j)[:, :, 0:P].rearrange("p c (h d) -> p c h d", h=8),
                                  z[:, j, :, :].unsqueeze(3).broadcast_to((P, KC, 8, HD)), ALU.mult).then_inc(attn_ready, 1)
                dve.wait_ge(attn_ready, G * g + j + 1)
                dve.wait_ge(g_tanh_ready, (G * g + j) // 2 + 1)
                dve.scalar_tensor_tensor(gated[:, j, :], g_tanh[:, j, :], 1.0, attn[:, j, :], ALU.add, ALU.mult).then_inc(gated_ready, 1)

        def outputs(g):
            for j in range(G):
                dve.wait_ge(gt_hi_ready, G * g + j + 1)
                dve.tensor_tensor(gt_lo[:, j, :, :], gt_bank(j), f(gt_hi[:, j, :, :]), ALU.subtract).then_inc(gt_lo_ready, 1)
            m.wait_steps(dve)
            for j in range(G):
                dve.wait_ge(out_ready, G * g + j + 1)
                dve.scalar_tensor_tensor(m.X[:, G * g + j, :], out_bank(j), half_tg[:, 0:1], m.X[:, G * g + j, :],
                                         ALU.mult, ALU.add).then_inc(m.x_done, 1)

        for c in range(KC):
            dve.wait_ge(ct_hi_ready, c + 1)
            dve.tensor_tensor(ct_lo[:, c, :, :], m.CT[:, c, 0:G, :], f(ct_hi[:, c, :, :]), ALU.subtract).then_inc(ct_ready, 1)
        weights(0)
        norm.vector(dve, 0, lambda j: xn[0][:, j, :])
        weights(1)
        dve.wait_ge(m.tg_ready, 1)
        m.step(dve.tensor_scalar(half_tg[:, :], m.tg[:, 0:1], 0.5, None, ALU.mult))
        keys(0)
        for g in range(NG):
            queries(g)
            if g + 1 < NG:
                norm.vector(dve, g + 1, lambda j: xn[1][:, j, :])
            summaries(g)
            attention(g)
            if g + 1 < NG:
                keys(g + 1)
            outputs(g)

    def tensor(pe):
        def w(name, c, n0=0, n1=None):
            a, b = cols[name]
            a, b = a + n0, b if n1 is None else a + n1
            return W_hi[:, c, a:b], W_lo[:, c, a:b]

        def keys(g):
            pe.wait_ge(ct_ready, KC * g + KC)
            after(pe, summary_ready, G * g)
            for j in range(G):
                if j >= 2:
                    pe.wait_ge(k_ready, G * g + j - 1)
                    pe.wait_ge(v_ready, G * g + j - 1)
                for c in range(KC):
                    mm = split_matmul(pe, kv_bank[j % 2][:, :], (ct_hi[:, c, j, :], ct_lo[:, c, j, :]), w("kv", c), c == 0, c == KC - 1)
                mm.then_inc(kv_proj, 1)

        def queries(g):
            xt.tensor(pe, g, lambda j: xn[g][:, j, :])
            pe.wait_ge(w_lo_ready, 2)
            pe.wait_ge(xt.lo_ready, xt.lo_at(g + 1))
            for o in range(KC):
                for c in range(KC):
                    mm = split_matmul(pe, q_bank[o][:, :], w("q", c, o * P, (o + 1) * P), (m.xt_hi[:, c, 0:G, :], m.xt_lo[:, c, 0:G, :]), c == 0, c == KC - 1)
                mm.then_inc(q_proj, 1)
            after(pe, m.x_done, m.x_at(stage, G * g))
            for j in range(G):
                for c in range(KC):
                    mm = split_matmul(pe, g_bank(j), (m.xt_hi[:, c, j, :], m.xt_lo[:, c, j, :]), w("g", c), c == 0, c == KC - 1)
                mm.then_inc(g_proj, 1)

        def summaries(g):
            for j in range(G):
                pe.wait_ge(k_ready, G * g + (G if j < 2 else j + 1))
                pe.wait_ge(v_ready, G * g + (G if j < 2 else j + 1))
                if j >= 2:
                    pe.wait_ge(summary_ready, G * g + j - 1)
                for c in range(KC):
                    mm = pe.matmul(sum_bank(j)[:, c, 0:P + 1], k_feat[:, j, c * P:(c + 1) * P], v_one[:, j, c, :], start=True, stop=True)
                mm.then_inc(kv_sum, 1)

        def attention(g):
            pe.wait_ge(q_ready, KC * g + KC)
            for j in range(G):
                pe.wait_ge(summary_ready, G * g + j + 1)
                if j >= 2:
                    pe.wait_ge(attn_ready, G * g + j - 1)
                for c in range(KC):
                    mm = pe.matmul(num_bank(j)[:, c, 0:P + 8], q_feat[:, c, j * P:(j + 1) * P], summary[:, j, c, :], start=True, stop=True)
                mm.then_inc(num_ready, 1)

        def outputs(g):
            for j in range(G):
                pe.wait_ge(gated_ready, G * g + j + 1)
                if j >= 2:
                    pe.wait_ge(gt_lo_ready, G * g + j - 1)
                for c in range(KC):
                    mm = pe.transpose(gt_bank(j)[:, c, :], gated[:, j, c * P:(c + 1) * P], m.ident)
                mm.then_inc(gt_raw, 1)
            for j in range(G):
                pe.wait_ge(gt_lo_ready, G * g + j + 1)
                if j >= 2:
                    pe.wait_ge(m.x_done, m.x_at(stage, G * g + j - 1))
                for c in range(KC):
                    mm = split_matmul(pe, out_bank(j), (gt_hi[:, j, c, :], gt_lo[:, j, c, :]), w("o", c), c == 0, c == KC - 1)
                mm.then_inc(out_ready, 1)

        pe.wait_ge(w_lo_ready, 1)
        keys(0)
        pe.wait_ge(m.const_in, 32)
        for g in range(NG):
            queries(g)
            summaries(g)
            attention(g)
            if g + 1 < NG:
                keys(g + 1)
            outputs(g)

    return {"load": load, "gpsimd": gpsimd, "scalar": scalar, "vector": vector, "tensor": tensor}


def adapters(m, stage, name, first):
    E, R, K = 8, 16, 2
    BONUS = 3.0 * (1.0 - 1 / 625)
    ER = E * R
    s = lambda x: m.sem(f"{name}_{x}")
    gate = m.tg[:, 4:5] if first else m.tg[:, 7:8]
    norm = Norm(m, stage)
    xt = Transposed(m, [[m.bank[4], m.bank[5]], [m.bank[6], m.bank[7]]], norm,
                    lambda g, c: m.xt_hi[:, c, G * g:G * g + G, :], lambda g, c: m.xt_lo[:, c, G * g:G * g + G, :])
    W = m.sb(f"{name}_w", [P, KC, ER + E])
    W_hi = m.sb(f"{name}_w_hi", [P, KC, ER + E], F32R)
    W_lo = m.sb(f"{name}_w_lo", [P, KC, ER + E], F32R)
    up = m.sb(f"{name}_up", [P, D])
    if first:
        bias = m.sb(f"{name}_bias", [P, ER + E])
        up_bias = m.sb(f"{name}_up_bias", [E, D])
    per_group = lambda shape: [m.work(shape) for _ in range(NG)]
    xn = [m.xn, m.work([P, G, D])]
    proj = per_group([P, G, ER + E])
    logits = per_group([P, G, 2 * E])
    top = per_group([P, G, 8])
    chosen = per_group([P, G, 8])
    marked = per_group([P, G, 2 * E])
    mask = per_group([P, G, E])
    shifted = per_group([P, G, E])
    expd = per_group([P, G, E])
    kept = per_group([P, G, E])
    total = per_group([P, G])
    inv = per_group([P, G])
    weight = per_group([P, G, E])
    hidden = per_group([P, G, ER])
    hidden_t = per_group([P, G, P])
    weight_t = per_group([E, G, P])
    loaded, w_parts, pads = s("loaded"), s("w_parts"), s("pads")
    projected, proj_ready = s("projected"), s("proj")
    shifted_ready, exp_ready = s("shifted"), s("exp")
    hidden_ready = s("hidden")
    turned, turned_ready, out_ready = s("turned"), s("turned_copy"), s("out")
    proj_bank = lambda j: m.bank[j][:, 0:ER + E]
    turn_bank = lambda j: m.bank[6 + j % 2]
    out_bank = lambda j: m.bank[j][:, 0:D]
    LOADS = 4 if first else 2

    def load(sp):
        sp.dma_start(W[:, :, :], m.dram[f"{name}_w"].rearrange("p (c n) -> p c n", c=KC)).then_inc(loaded, 16)
        sp.dma_start(up[:, :], m.dram[f"{name}_up"]).then_inc(loaded, 16)
        if first:
            sp.dma_start(bias[:, :], m.dram[f"{name}_bias"].broadcast_to((P, ER + E))).then_inc(loaded, 16)
            sp.dma_start(up_bias[:, :], m.dram[f"{name}_up_bias"]).then_inc(loaded, 16)

    def gpsimd(pool):
        pool.wait_ge(loaded, 16 * LOADS)
        pool.tensor_copy(W_hi[:, :, :], W[:, :, :]).then_inc(w_parts, 1)
        pool.wait_ge(w_parts, 1)
        pool.tensor_tensor(W_lo[:, :, :], W[:, :, :], f(W_hi[:, :, :]), ALU.subtract).then_inc(w_parts, 1)
        norm.gpsimd(pool, 0)
        pool.wait_ge(norm.xn, norm.xn_at(G))
        for g in range(NG):
            pool.memset(logits[g][:, :, E:2 * E], -BIG).then_inc(pads, 1)
            pool.memset(chosen[g][:, :, :], -BIG).then_inc(pads, 1)
        norm.gpsimd(pool, 1)

    def scalar(act):
        def project(g):
            if not first:
                for j in range(G):
                    act.wait_ge(projected, G * g + j + 1)
                    act.activation(proj[g][:, j, :], proj_bank(j), ACT.Copy).then_inc(proj_ready, 1)

        def exponentials(g):
            act.wait_ge(shifted_ready, g + 1)
            act.activation(expd[g][:, :, :], shifted[g][:, :, :], ACT.Exp).then_inc(exp_ready, 1)

        def turn(g):
            for j in range(G):
                act.wait_ge(turned, G * g + j + 1)
                act.activation(hidden_t[g][:, j, :], turn_bank(j)[:, 0:P], ACT.Copy).then_inc(turned_ready, 1)
                if first:
                    act.activation(weight_t[g][:, j, :], turn_bank(j)[0:E, D:D + P], ACT.Copy).then_inc(turned_ready, 1)

        act.wait_ge(norm.xn, norm.xn_at(G))
        xt.scalar(act, 0)
        project(0)
        xt.scalar(act, 1)
        exponentials(0)
        project(1)
        turn(0)
        exponentials(1)
        turn(1)

    def head(dve):
        norm.scale(dve, 0, lambda j: xn[0][:, j, :])

    def vector(dve, next_moments, next_head):
        def project(g):
            if first:
                for j in range(G):
                    dve.wait_ge(projected, G * g + j + 1)
                    dve.tensor_tensor(proj[g][:, j, :], proj_bank(j), bias[:, :], ALU.add).then_inc(proj_ready, 1)

        def route(g):
            dve.wait_ge(proj_ready, G * g + G)
            dve.wait_ge(pads, 2 * NG)
            m.step(dve.tensor_scalar(logits[g][:, :, 0:E], proj[g][:, :, ER:ER + E], BONUS if first else 0.0, None, ALU.add))
            m.wait_steps(dve)
            for j in range(G):
                m.step(dve.max(top[g][:, j, :], logits[g][:, j, :]))
            m.wait_steps(dve)
            m.step(dve.tensor_copy(chosen[g][:, :, 0:K], top[g][:, :, 0:K]))
            dve.tensor_tensor(shifted[g][:, :, :], logits[g][:, :, 0:E], top[g][:, :, 0:1].broadcast_to((P, G, E)), ALU.subtract).then_inc(shifted_ready, 1)
            m.wait_steps(dve)
            for j in range(G):
                m.step(dve.match_replace(marked[g][:, j, :], chosen[g][:, j, :], logits[g][:, j, :], BIG))
            m.wait_steps(dve)
            m.step(dve.tensor_tensor(mask[g][:, :, :], marked[g][:, :, 0:E], logits[g][:, :, 0:E], ALU.not_equal))
            m.wait_steps(dve)
            dve.wait_ge(exp_ready, g + 1)
            m.step(dve.tensor_tensor(kept[g][:, :, :], expd[g][:, :, :], mask[g][:, :, :], ALU.mult))
            m.wait_steps(dve)
            m.step(dve.reduce_sum(total[g][:, :], kept[g][:, :, :], AX_X))
            m.wait_steps(dve)
            m.step(dve.reciprocal(inv[g][:, :], total[g][:, :]))
            m.wait_steps(dve)
            m.step(dve.tensor_tensor(weight[g][:, :, :], kept[g][:, :, :], inv[g][:, :].unsqueeze(2).broadcast_to((P, G, E)), ALU.mult))
            m.wait_steps(dve)
            for j in range(G):
                spread = weight[g][:, j, :].unsqueeze(2).broadcast_to((P, E, R))
                down = proj[g][:, j, 0:ER].rearrange("p (e r) -> p e r", e=E)
                into = hidden[g][:, j, :].rearrange("p (e r) -> p e r", e=E)
                if first:
                    dve.scalar_tensor_tensor(into, down, 0.0, spread, ALU.max, ALU.mult).then_inc(hidden_ready, 1)
                else:
                    dve.tensor_tensor(into, down, spread, ALU.mult).then_inc(hidden_ready, 1)

        def outputs(g):
            for j in range(G):
                b = G * g + j
                dve.wait_ge(out_ready, b + 1)
                dve.scalar_tensor_tensor(m.X[:, b, :], out_bank(j), gate, m.X[:, b, :], ALU.mult, ALU.add).then_inc(m.x_done, 1)

        norm.moments(dve, 1)
        xt.vector(dve, 0)
        norm.scale(dve, 1, lambda j: xn[1][:, j, :])
        dve.wait_ge(loaded, 16 * LOADS)
        project(0)
        if not first:
            dve.wait_ge(norm.xn, norm.xn_at(NB))
            for b in range(NB):
                m.step(dve.scalar_tensor_tensor(m.X[:, b, :], xn[b // G][:, b % G, :], gate, m.X[:, b, :], ALU.mult, ALU.add))
        xt.vector(dve, 1)
        route(0)
        project(1)
        route(1)
        outputs(0)
        next_moments(dve, 0)
        next_head(dve)
        outputs(1)

    def tensor(pe):
        def project(g):
            pe.wait_ge(xt.lo_ready, xt.lo_at(g + 1))
            for j in range(G):
                after(pe, proj_ready, G * (g - 1) + j + 1)
                for c in range(KC):
                    mm = split_matmul(pe, proj_bank(j), (m.xt_hi[:, c, G * g + j, :], m.xt_lo[:, c, G * g + j, :]), (W_hi[:, c, :], W_lo[:, c, :]), c == 0, c == KC - 1)
                mm.then_inc(projected, 1)

        def outputs(g):
            for j in range(G):
                pe.wait_ge(hidden_ready, G * g + j + 1)
                after(pe, turned_ready, (1 + first) * (G * g + j - 1))
                mm = pe.transpose(turn_bank(j)[:, 0:P], hidden[g][:, j, :], m.ident)
                if first:
                    mm = pe.transpose(turn_bank(j)[0:E, D:D + P], weight[g][:, j, :], m.ident)
                mm.then_inc(turned, 1)
            pe.wait_ge(proj_ready, NB)
            for j in range(G):
                pe.wait_ge(turned_ready, (1 + first) * (G * g + j + 1))
                if g:
                    pe.wait_ge(m.x_done, m.x_at(stage, G * (g - 1) + j + 1))
                mm = pe.matmul(out_bank(j), hidden_t[g][:, j, :], up[:, :], start=True, stop=not first)
                if first:
                    mm = pe.matmul(out_bank(j), weight_t[g][:, j, :], up_bias[:, :], start=False, stop=True)
                mm.then_inc(out_ready, 1)

        pe.wait_ge(w_parts, 2)
        pe.wait_ge(loaded, 16 * LOADS)
        pe.wait_ge(m.x_done, m.x_at(stage, 0))
        for g in range(NG):
            xt.tensor(pe, g, lambda j: xn[g][:, j, :])
            project(g)
        for g in range(NG):
            outputs(g)

    return {"load": load, "moments": norm.moments, "head": head, "gpsimd": gpsimd, "scalar": scalar, "vector": vector, "tensor": tensor}


def l1_attention(m, stage):
    H, HD, STACK = 8, 16, 48
    s = lambda x: m.sem(f"l1a_{x}")
    norm = Norm(m, stage)
    sel_raw = m.xn_all[:, :, :].rearrange("p b d -> p (b d)").rearrange("p (k q n) -> p k q n", k=4, q=4)
    sel = m.sb("l1a_sel", [P, 4, 4, P], F32R)
    gamma = m.sb("l1a_gamma", [P, 1])
    scale = m.work([P, 1])
    q_hi = m.xt_hi[:, :, :, :].rearrange("p c b n -> p (c b n)").rearrange("p (b d) -> p b d", b=NB)
    q_lo = m.xt_lo[:, :, :, :].rearrange("p c b n -> p (c b n)").rearrange("p (b d) -> p b d", b=NB)
    k_hi = [ring[:, 2 * D:3 * D] for ring in m.ring_hi]
    k_lo = [ring[:, 2 * D:3 * D] for ring in m.ring_lo]
    k_stack = [m.work([P, 4, D], F32R) for _ in range(2)]
    q_stack = [m.work([P, 4, D], F32R) for _ in range(2)]
    lower = [m.work([H, D], F32R) for _ in range(2)]
    v_hi = m.work([P, 2, KC, H, 2 * HD], F32R)
    v_lo = m.work([P, 2, KC, H, 2 * HD], F32R)
    maxima = [m.work([P, KC, H]) for _ in range(2)]
    PB = 3
    probs = m.work([P, PB, KC, D])
    by_chunk = lambda ring: ring[:, 0:2 * D].rearrange("p (k n) -> p k n", k=KC)
    p_hi = [by_chunk(m.ring_hi[0]), by_chunk(m.ring_hi[1]), m.work([P, KC, D], F32R)]
    p_lo = [by_chunk(m.ring_lo[0]), by_chunk(m.ring_lo[1]), m.work([P, KC, D], F32R)]
    o_raw = m.work([P, 2, D])
    o_hi = m.work([P, 2, D], F32R)
    o_lo = m.work([P, 2, D], F32R)
    out_sel_raw = m.work([P, 2, 2, P])
    out_sel = m.work([P, 2, 2, P], F32R)
    inv = m.work([P, D])
    ratio = m.work([P, D])
    sel_in, sel_ready = s("sel_in"), s("sel")
    k_hi_ready, k_split, v_ready, ones_ready, q_hi_ready, q_split = s("k_hi"), s("k_split"), s("v"), s("ones"), s("q_hi"), s("q_split")
    k_raw, q_raw, k_stacked, q_stacked = s("k_raw"), s("q_raw"), s("k_stacked"), s("q_stacked")
    scored, max_ready, max_turned, lower_ready, row_in = s("scored"), s("max"), s("max_turned"), s("lower"), s("row_in")
    lowered, exp_ready, p_split, summed = s("lowered"), s("exp"), s("p_split"), s("summed")
    out_sel_in, out_sel_ready, v_hi_ready = s("out_sel_in"), s("out_sel"), s("v_hi")
    taken, o_hi_ready, o_split, placed = s("taken"), s("o_hi"), s("o_split"), s("placed")
    k_bank, q_bank = [m.bank[2], m.bank[7]], [m.bank[3], m.bank[6]]
    LAG, LAG_V = 0, 3

    values = lambda b: m.CT[:, :, b, :].rearrange("p c (h d) -> p c h d", h=H)

    def load(sp):
        sp.dma_start(sel_raw[:, :, :, :], m.dram["l1a_sel"].rearrange("p (k q n) -> p k q n", k=4, q=4)).then_inc(sel_in, 16)
        sp.dma_start(gamma[:, :], m.dram["l1a_gamma"].broadcast_to((P, 1))).then_inc(sel_in, 16)

    def sync(sp):
        sp.wait_ge(norm.xn, norm.xn_at(G))
        sp.dma_start(out_sel_raw[:, :, :, :], m.dram["l1a_out_sel"].rearrange("p (k g n) -> p k g n", k=2, g=2)).then_inc(out_sel_in, 16)
        for b in range(NB):
            sp.wait_ge(lower_ready, b + 1)
            for a in range(2):
                row = 64 * a + STACK
                sp.dma_start(f(q_stack[b % 2][row:row + 1, :, :]), f(lower[b % 2][4 * a:4 * a + 4, :])).then_inc(row_in, 16)

    def gpsimd(pool):
        norm.gpsimd(pool, 0)
        norm.gpsimd(pool, 1)
        pool.wait_ge(m.cn_in, 16)
        pool.wait_ge(norm.xn, norm.xn_at(G))
        pool.wait_ge(m.const_in, 32)
        for part, one in ((v_hi, 1.0), (v_lo, 0.0)):
            rows = part[:, :, :, :, HD:2 * HD].rearrange("p n c h d -> p (n c h) d")
            pool.tensor_scalar(rows, m.minus_half[:, 0:1].unsqueeze(2).broadcast_to((P, 2 * KC * H, HD)), 0.0, one, ALU.mult, ALU.add).then_inc(ones_ready, 1)

        def low_parts(b):
            pool.wait_ge(k_hi_ready, b + 1)
            pool.tensor_tensor(k_lo[b % 2], m.CN[:, b, :], f(k_hi[b % 2]), ALU.subtract).then_inc(k_split, 1)
            pool.wait_ge(q_hi_ready, b + 1)
            pool.tensor_tensor(q_lo[:, b, :], m.xn_all[:, b, :], f(q_hi[:, b, :]), ALU.subtract).then_inc(q_split, 1)

        def value_parts(b):
            pool.wait_ge(v_hi_ready, b + 1)
            pool.tensor_tensor(v_lo[:, b % 2, :, :, 0:HD], values(b), f(v_hi[:, b % 2, :, :, 0:HD]), ALU.subtract).then_inc(v_ready, 1)

        def low_exps(b, heads):
            for h in heads:
                pool.wait_ge(exp_ready, 2 * (H * b + h + 1))
                n = (H * b + h) % PB
                pool.tensor_tensor(p_lo[n], probs[:, n, :, :], f(p_hi[n]), ALU.subtract).then_inc(p_split, 1)

        low_parts(0)
        for b in range(NB + 1):
            if b:
                low_exps(b - 1, range(0, H // 2))
            if b + 1 < NB:
                low_parts(b + 1)
            if b:
                low_exps(b - 1, range(H // 2, H))
            if b < NB:
                value_parts(b)

    def head(dve):
        dve.wait_ge(sel_ready, 1)
        norm.scale(dve, 0, lambda j: m.xn_all[:, j, :])

    def vector(dve, next_moments, next_head):
        norm.vector(dve, 1, lambda j: m.xn_all[:, G + j, :])
        dve.wait_ge(sel_in, 32)
        m.step(dve.tensor_tensor(scale[:, :], m.tg[:, 1:2], gamma[:, :], ALU.mult))
        m.wait_steps(dve)

        def queries(b):
            for half in range(2):
                dve.wait_ge(q_raw, 2 * b + half + 1)
                dve.tensor_copy(q_stack[b % 2][:, 2 * half:2 * half + 2, :], q_bank[half][:, :].rearrange("p (q n) -> p q n", q=2)).then_inc(q_stacked, 1)

        def largest(b, h):
            dve.wait_ge(scored, H * b + h + 1)
            dve.reduce_max(maxima[b % 2][:, :, 4 * (h % 2) + h // 2], m.bank[h % 2][:, :].rearrange("p (c n) -> p c n", c=KC), AX_X).then_inc(max_ready, 1)

        def lowering(b):
            dve.wait_ge(max_turned, b + 1)
            dve.tensor_scalar(lower[b % 2][:, :], m.bank[6][0:H, 0:D], -1.0, None, ALU.mult).then_inc(lower_ready, 1)

        def split_output(b):
            dve.wait_ge(o_hi_ready, b + 1)
            dve.tensor_tensor(o_lo[:, :, :], o_raw[:, :, :], f(o_hi[:, :, :]), ALU.subtract).then_inc(o_split, 1)

        def take(b, pair):
            dve.wait_ge(summed, H * b + 2 * pair + 2)
            after(dve, o_split, b)
            row = 2 * HD * pair
            dve.tensor_copy(o_raw[row:row + 2 * HD, :, :], m.bank[4 + pair % 2][0:2 * HD, :].rearrange("p (h n) -> p h n", h=2)).then_inc(taken, 1)

        def add(b):
            dve.wait_ge(placed, b + 1)
            m.step(dve.reciprocal(inv[:, :], m.bank[7][:, D:2 * D]))
            m.wait_steps(dve)
            m.step(dve.tensor_tensor(ratio[:, :], m.bank[7][:, 0:D], inv[:, :], ALU.mult))
            m.wait_steps(dve)
            dve.scalar_tensor_tensor(m.X[:, b, :], ratio[:, :], scale[:, 0:1], m.X[:, b, :], ALU.mult, ALU.add).then_inc(m.x_done, 1)

        for b in range(NB + 2):
            if b < NB:
                queries(b)
            if b >= 2:
                split_output(b - 2)
            for h in range(H):
                if b < NB:
                    largest(b, h)
                if 1 <= b <= NB and h > LAG_V and (h - LAG_V) % 2:
                    take(b - 1, (h - LAG_V) // 2)
            if b == NB:
                next_moments(dve, 0)
            if b == NB + 1:
                next_head(dve)
            if b >= 2:
                add(b - 2)
            if b < NB:
                lowering(b)
            if 1 <= b <= NB:
                for pair in range((H - LAG_V) // 2, H // 2):
                    take(b - 1, pair)

    def scalar(act):
        act.wait_ge(m.cn_in, 16)
        act.wait_ge(sel_in, 32)
        act.activation(sel[:, :, :, :], sel_raw[:, :, :, :], ACT.Copy).then_inc(sel_ready, 1)
        act.wait_ge(norm.xn, norm.xn_at(G))

        def high_parts(b):
            after(act, k_raw, 2 * (b - 1))
            act.activation(k_hi[b % 2], m.CN[:, b, :], ACT.Copy).then_inc(k_hi_ready, 1)
            act.wait_ge(norm.xn, norm.xn_at(b + 1))
            act.activation(q_hi[:, b, :], m.xn_all[:, b, :], ACT.Copy).then_inc(q_hi_ready, 1)

        def value_high_parts(b):
            after(act, summed, H * (b - 1))
            act.activation(v_hi[:, b % 2, :, :, 0:HD], values(b), ACT.Copy).then_inc(v_hi_ready, 1)

        def keys(b):
            for half in range(2):
                act.wait_ge(k_raw, 2 * b + half + 1)
                act.activation(k_stack[b % 2][:, 2 * half:2 * half + 2, :], k_bank[half][:, :].rearrange("p (q n) -> p q n", q=2),
                               ACT.Identity, bias=m.one_row).then_inc(k_stacked, 1)

        def exps(b, heads):
            for h in heads:
                act.wait_ge(lowered, H * b + h + 1)
                after(act, summed, H * b + h + 1 - PB)
                n = (H * b + h) % PB
                for out in (p_hi[n], probs[:, n, :, :]):
                    act.activation(out, m.bank[2 + h % 2][:, :].rearrange("p (c n) -> p c n", c=KC), ACT.Exp, scale=0.25).then_inc(exp_ready, 1)

        high_parts(0)
        def outputs(b):
            act.wait_ge(taken, H // 2 * (b + 1))
            after(act, placed, b)
            act.activation(o_hi[:, :, :], o_raw[:, :, :], ACT.Copy).then_inc(o_hi_ready, 1)

        for b in range(NB + 2):
            if b < NB:
                keys(b)
            if b == 1:
                act.wait_ge(out_sel_in, 16)
                act.activation(out_sel[:, :, :, :], out_sel_raw[:, :, :, :], ACT.Copy).then_inc(out_sel_ready, 1)
            if b >= 2:
                outputs(b - 2)
            if 1 <= b <= NB:
                exps(b - 1, range(0, H // 2))
            if b + 1 < NB:
                high_parts(b + 1)
            if b < NB:
                value_high_parts(b)
            if 1 <= b <= NB:
                exps(b - 1, range(H // 2, H))

    def tensor(pe):
        pe.wait_ge(sel_ready, 1)
        pe.wait_ge(norm.xn, norm.xn_at(G))
        pe.wait_ge(ones_ready, 2)

        def stacks(b, half):
            if b and half:
                pe.wait_ge(lower_ready, b)
                pe.wait_ge(m.x_done, m.x_at(stage, max(b - 2, 0)))
            if b >= 2 and not half:
                pe.wait_ge(exp_ready, 2 * H * (b - 1))
            for kind, bank, raw, hi, lo in ((2, k_bank[half], k_raw, k_hi[b % 2], k_lo[b % 2]), (0, q_bank[half], q_raw, q_hi[:, b, :], q_lo[:, b, :])):
                for q in range(2):
                    pe.matmul(bank[:, q * D:(q + 1) * D], sel[:, kind, 2 * half + q, :], hi, start=True, stop=False)
                    mm = pe.matmul(bank[:, q * D:(q + 1) * D], sel[:, kind + 1, 2 * half + q, :], lo, start=False, stop=True)
                mm.then_inc(raw, 1)

        def score(b, h):
            a, q = h % 2, h // 2
            if h % 4 == 0:
                pe.wait_ge(q_stacked, 2 * b + h // 4 + 1)
                pe.wait_ge(k_stacked, 2 * b + h // 4 + 1)
            after(pe, max_ready, H * b + h - 1)
            for c in range(KC):
                mm = pe.matmul(m.bank[a][:, c * D:(c + 1) * D], q_stack[b % 2][64 * a:64 * a + STACK, q, c * P:(c + 1) * P],
                               k_stack[b % 2][64 * a:64 * a + STACK, q, :], start=True, stop=True)
            mm.then_inc(scored, 1)

        def lowered_scores(b, h):
            a, q = h % 2, h // 2
            if h == 0:
                pe.wait_ge(row_in, 32 * (b + 1))
                pe.wait_ge(q_stacked, min(2 * b + 3, 2 * NB))
                pe.wait_ge(k_stacked, min(2 * b + 3, 2 * NB))
            after(pe, exp_ready, 2 * (H * b + h - 1))
            for c in range(KC):
                mm = pe.matmul(m.bank[2 + a][:, c * D:(c + 1) * D], k_stack[b % 2][64 * a:64 * a + STACK + 1, q, c * P:(c + 1) * P],
                               q_stack[b % 2][64 * a:64 * a + STACK + 1, q, :], start=True, stop=True)
            mm.then_inc(lowered, 1)

        def products(b, h):
            pe.wait_ge(p_split, H * b + h + 1)
            if h == 0:
                pe.wait_ge(v_ready, b + 1)
            if h % 2 == 0:
                after(pe, taken, H // 2 * b + h // 2 - 1)
            n = (H * b + h) % PB
            out = m.bank[4 + h // 2 % 2][0:2 * HD, (h % 2) * D:(h % 2 + 1) * D]
            for k in range(KC):
                mm = split_matmul(pe, out, (v_hi[:, b % 2, k, h, :], v_lo[:, b % 2, k, h, :]), (p_hi[n][:, k, :], p_lo[n][:, k, :]),
                                  k == 0, k == KC - 1)
            mm.then_inc(summed, 1)

        def place(b):
            pe.wait_ge(out_sel_ready, 1)
            pe.wait_ge(o_split, b + 1)
            pe.wait_ge(m.x_done, m.x_at(stage, b))
            for kind in range(2):
                for g in range(2):
                    pe.matmul(m.bank[7][:, kind * D:(kind + 1) * D], out_sel[:, kind, g, :], o_hi[:, g, :], start=g == 0, stop=False)
                    mm = pe.matmul(m.bank[7][:, kind * D:(kind + 1) * D], out_sel[:, kind, g, :], o_lo[:, g, :], start=False, stop=g == 1)
            mm.then_inc(placed, 1)

        for b in range(NB + 2):
            if b < NB:
                pe.wait_ge(k_split, b + 1)
                pe.wait_ge(q_split, b + 1)
                stacks(b, 0)
                stacks(b, 1)
            for h in range(H + LAG_V):
                if b < NB and h < H:
                    score(b, h)
                if 1 <= b <= NB and LAG <= h < H + LAG:
                    lowered_scores(b - 1, h - LAG)
                if b >= 2 and h == H - 4:
                    place(b - 2)
                if 1 <= b <= NB and h >= LAG_V:
                    products(b - 1, h - LAG_V)
                if b < NB and h == H:
                    pe.wait_ge(max_ready, H * b + H)
                    for c in range(KC):
                        mm = pe.transpose(m.bank[6][0:H, c * P:(c + 1) * P], maxima[b % 2][:, c, :], m.ident)
                    mm.then_inc(max_turned, 1)

    return {"load": load, "moments": norm.moments, "head": head, "sync": sync, "gpsimd": gpsimd, "scalar": scalar, "vector": vector, "tensor": tensor}


def feed_forward(m, stage, name, chunks, experts):
    E, NS, K = 16, 2, 4
    GE = E + NS
    s = lambda x: m.sem(f"{name}_{x}")
    norm = Norm(m, stage)
    xt = Transposed(m, [[m.bank[4], m.bank[5]], [m.bank[6], m.bank[7]]], norm,
                    lambda g, c: m.xt_hi[:, c, G * g:G * g + G, :], lambda g, c: m.xt_lo[:, c, G * g:G * g + G, :])
    gate = m.tg[:, 5:6] if experts else m.tg[:, 6:7]
    IN = 3 * P if experts else 4 * P
    COLS = IN + D
    LOADED = COLS + 1 if experts else COLS
    hidden = m.work([P, NB, P])
    up = m.work([P, NB, P])
    gated = m.work([P, NB, P])
    h_hi = [m.work([P, NB, P], F32R) for _ in range(2)]
    h_lo = [m.work([P, NB, P], F32R) for _ in range(2)]
    summed = m.work([P, NB, D])
    w_in = [s("w_in_even"), s("w_in_odd")]
    cols_in, in_hi, in_lo, out_hi, out_lo = s("cols_in"), s("in_hi"), s("in_lo"), s("out_hi"), s("out_lo")
    h_raw, u_raw, h_ready, u_ready, gated_ready, h_hi_ready, h_lo_ready, used = s("h_raw"), s("u_raw"), s("h"), s("u"), s("gated"), s("h_hi"), s("h_lo"), s("used")
    if experts:
        cen = m.sb(f"{name}_cen", [P, KC, E])
        cen_hi = m.sb(f"{name}_cen_hi", [P, KC, E], F32R)
        cen_lo = m.sb(f"{name}_cen_lo", [P, KC, E], F32R)
        bias = m.sb(f"{name}_bias", [P, E])
        b2 = m.sb(f"{name}_b2", [2 * GE, D])
        b2_hi = m.sb(f"{name}_b2_hi", [2 * GE, D], F32R)
        b2_lo = m.sb(f"{name}_b2_lo", [2 * GE, D], F32R)
        gates_t = m.work([2 * GE, NB, P], F32R)
        th = m.work([P, NB, E])
        score = m.work([P, NB, E + 8])
        top = m.work([P, NB, 8])
        chosen = m.work([P, NB, 8])
        marked = m.work([P, NB, E + 8])
        mask = m.work([P, NB, E])
        kept = m.work([P, NB, E])
        total = m.work([P, NB])
        guarded = m.work([P, NB])
        inv = m.work([P, NB])
        gates = m.work([P, NB, GE])
        parts = m.work([P, NB, 2, GE], F32R)
        small_parts, pads = s("small_parts"), s("pads")
        routed, th_ready = s("routed"), s("th")
        gates_lo, turned, gates_t_ready = s("gates_lo"), s("turned"), s("gates_t")
    else:
        scales = m.sb(f"{name}_scales", [P, 2, chunks])
        factors = m.sb(f"{name}_factors", [P, 2, chunks])
        half = m.sb(f"{name}_half", [P, chunks])
        out_scale = m.sb(f"{name}_out_scale", [P, D])
        factors_ready = s("factors")

    acc = lambda b: m.bank[4 + b // 2][:, (b % 2) * D:(b % 2 + 1) * D]
    side = lambda t: slice(G * t, G * t + G)
    wide = lambda bank: bank[:, :].rearrange("p (j n) -> p j n", j=G)
    raw, hi, lo = m.ring_raw, m.ring_hi, m.ring_lo
    is_first = lambda c: isinstance(c, int) and c == 0
    is_last = lambda c: isinstance(c, int) and c == chunks - 1

    def load(sp):
        if experts:
            for tile, what in ((cen, "cen"), (b2, "b2")):
                src = m.dram[f"{name}_{what}"]
                sp.dma_start(tile[:, :, :] if what == "cen" else tile[:, :], src.rearrange("p (c n) -> p c n", c=KC) if what == "cen" else src).then_inc(cols_in, 16)
            sp.dma_start(bias[:, :], m.dram[f"{name}_bias"].broadcast_to((P, E))).then_inc(cols_in, 16)
        else:
            sp.dma_start(scales[:, :, :], m.dram[f"{name}_scales"].rearrange("p (k n) -> p k n", k=2)).then_inc(cols_in, 16)
            sp.dma_start(out_scale[:, :], m.dram[f"{name}_out_scale"].broadcast_to((P, D))).then_inc(cols_in, 16)

    def sync(sp):
        sp.wait_ge(m.x_done, m.x_at(stage - 1, 0))

        def chunk(c, even_odd):
            after(sp, out_lo, c - 1)
            sp.dma_start(raw[even_odd][:, 0:LOADED], m.dram[f"{name}_w"][c, :, :]).then_inc(w_in[even_odd], 16)

        over_chunks(sp, chunks, chunk)

    def gpsimd(pool):
        norm.gpsimd(pool, 0)
        if experts:
            pool.wait_ge(cols_in, 48)
            for tile, h, l in ((cen[:, :, :], cen_hi[:, :, :], cen_lo[:, :, :]), (b2[:, :], b2_hi[:, :], b2_lo[:, :])):
                pool.tensor_copy(h, tile).then_inc(small_parts, 1)
            pool.wait_ge(small_parts, 2)
            for tile, h, l in ((cen[:, :, :], cen_hi[:, :, :], cen_lo[:, :, :]), (b2[:, :], b2_hi[:, :], b2_lo[:, :])):
                pool.tensor_tensor(l, tile, f(h), ALU.subtract).then_inc(small_parts, 1)
            pool.wait_ge(norm.xn, norm.xn_at(G))
            pool.memset(score[:, :, E:E + 8], -BIG).then_inc(pads, 1)
            pool.memset(chosen[:, :, :], -BIG).then_inc(pads, 1)
            pool.memset(gates[:, :, E:GE], 1.0).then_inc(pads, 1)
        norm.gpsimd(pool, 1)

        def low_in(c, n):
            pool.wait_ge(in_hi, c + 1)
            pool.tensor_tensor(lo[n][:, 0:IN], raw[n][:, 0:IN], f(hi[n][:, 0:IN]), ALU.subtract).then_inc(in_lo, 1)

        def chunk(c, n):
            if not is_last(c):
                low_in(c + 1, 1 - n)
            pool.wait_ge(out_hi, c + 1)
            pool.tensor_tensor(lo[n][:, IN:COLS], raw[n][:, IN:COLS], f(hi[n][:, IN:COLS]), ALU.subtract).then_inc(out_lo, 1)

        low_in(0, 0)
        over_chunks(pool, chunks, chunk)

    def scalar(act):
        def high_in(c, n):
            act.wait_ge(w_in[n], 8 * (c - n) + 16)
            after(act, h_raw, 2 * (c - 1))
            act.activation(hi[n][:, 0:IN], raw[n][:, 0:IN], ACT.Copy).then_inc(in_hi, 1)

        act.wait_ge(norm.xn, norm.xn_at(G))
        high_in(0, 0)
        for g in range(NG):
            xt.scalar(act, g)
        if experts:
            for g in range(NG):
                act.wait_ge(routed, g + 1)
                act.activation(th[:, side(g), :], m.bank[2 + g][:, 0:G * E].rearrange("p (j e) -> p j e", j=G), ACT.Tanh, scale=0.5).then_inc(th_ready, 1)
            for g in range(NG):
                act.wait_ge(turned, g + 1)
                act.activation(gates_t[:, side(g), :], wide(m.bank[2 + g])[0:2 * GE, :, :], ACT.Copy).then_inc(gates_t_ready, 1)

        def chunk(c, n):
            for t in range(2):
                act.wait_ge(h_raw, 2 * c + t + 1)
                after(act, gated_ready, 2 * (c - 1) + t + 1)
                if experts:
                    act.activation(hidden[:, side(t), :], wide(m.bank[t]), ACT.Relu, bias=raw[n][:, COLS:LOADED]).then_inc(h_ready, 1)
                else:
                    act.wait_ge(factors_ready, 1)
                    act.activation(hidden[:, side(t), :], wide(m.bank[t]), ACT.Tanh, scale=half[:, c:c + 1]).then_inc(h_ready, 1)
                    act.wait_ge(u_raw, 2 * c + t + 1)
                    act.activation(up[:, side(t), :], wide(m.bank[2 + t]), ACT.Copy, scale=factors[:, 1, c:c + 1]).then_inc(u_ready, 1)
            if not is_last(c):
                high_in(c + 1, 1 - n)
            after(act, used, c - 1)
            act.activation(hi[n][:, IN:COLS], raw[n][:, IN:COLS], ACT.Copy).then_inc(out_hi, 1)
            for t in range(2):
                act.wait_ge(gated_ready, 2 * c + t + 1)
                act.activation(h_hi[n][:, side(t), :], gated[:, side(t), :], ACT.Copy).then_inc(h_hi_ready, 1)

        over_chunks(act, chunks, chunk)

    def head(dve):
        norm.scale(dve, 0, lambda j: m.xn_all[:, j, :])

    def vector(dve, next_moments, next_head):
        dve.wait_ge(cols_in, 48 if experts else 32)
        if experts:
            m.step(dve.tensor_scalar(bias[:, :], bias[:, :], 0.5, None, ALU.add))
        else:
            m.step(dve.tensor_scalar(half[:, :], scales[:, 0, :], 0.5, None, ALU.mult))
            m.wait_steps(dve)
            dve.tensor_tensor(factors[:, 1, :], half[:, :], scales[:, 1, :], ALU.mult).then_inc(factors_ready, 1)
        norm.moments(dve, 1)
        xt.vector(dve, 0)
        norm.scale(dve, 1, lambda j: m.xn_all[:, G + j, :])
        xt.vector(dve, 1)
        if experts:
            dve.wait_ge(norm.xn, norm.xn_at(NB))
            for q in range(NB // 2):
                two = slice(2 * q, 2 * q + 2)
                m.step(dve.scalar_tensor_tensor(m.X[:, two, :], m.xn_all[:, two, :], gate, m.X[:, two, :], ALU.mult, ALU.add))
            dve.wait_ge(th_ready, NG)
            m.wait_steps(dve)
            dve.wait_ge(pads, 3)
            m.step(dve.scalar_tensor_tensor(score[:, :, 0:E], th[:, :, :], 0.5, bias[:, :].unsqueeze(1).broadcast_to((P, NB, E)), ALU.mult, ALU.add))
            m.wait_steps(dve)
            for b in range(NB):
                m.step(dve.max(top[:, b, :], score[:, b, :]))
            m.wait_steps(dve)
            m.step(dve.tensor_copy(chosen[:, :, 0:K], top[:, :, 0:K]))
            m.wait_steps(dve)
            for b in range(NB):
                m.step(dve.match_replace(marked[:, b, :], chosen[:, b, :], score[:, b, :], BIG))
            m.wait_steps(dve)
            m.step(dve.tensor_tensor(mask[:, :, :], marked[:, :, 0:E], score[:, :, 0:E], ALU.not_equal))
            m.wait_steps(dve)
            m.step(dve.tensor_tensor(kept[:, :, :], score[:, :, 0:E], mask[:, :, :], ALU.mult))
            m.wait_steps(dve)
            m.step(dve.reduce_sum(total[:, :], kept[:, :, :], AX_X))
            m.wait_steps(dve)
            m.step(dve.tensor_scalar(guarded[:, :], total[:, :], 1e-8, None, ALU.max))
            m.wait_steps(dve)
            m.step(dve.reciprocal(inv[:, :], guarded[:, :]))
            m.wait_steps(dve)
            m.step(dve.tensor_tensor(gates[:, :, 0:E], kept[:, :, :], inv[:, :].unsqueeze(2).broadcast_to((P, NB, E)), ALU.mult))
            m.wait_steps(dve)
            m.step(dve.tensor_copy(parts[:, :, 0, :], gates[:, :, :]))
            m.wait_steps(dve)
            dve.tensor_tensor(parts[:, :, 1, :], gates[:, :, :], f(parts[:, :, 0, :]), ALU.subtract).then_inc(gates_lo, 1)

        def chunk(c, n):
            for t in range(2):
                dve.wait_ge(h_ready, 2 * c + t + 1)
                after(dve, h_lo_ready, 2 * (c - 1) + t + 1)
                if experts:
                    dve.wait_ge(u_raw, 2 * c + t + 1)
                    dve.tensor_tensor(gated[:, side(t), :], wide(m.bank[2 + t]), hidden[:, side(t), :], ALU.mult).then_inc(gated_ready, 1)
                else:
                    dve.wait_ge(u_ready, 2 * c + t + 1)
                    m.step(dve.scalar_tensor_tensor(up[:, side(t), :], hidden[:, side(t), :], 1.0, up[:, side(t), :], ALU.add, ALU.mult))
                    m.wait_steps(dve)
                    dve.tensor_tensor(gated[:, side(t), :], wide(m.bank[t]), up[:, side(t), :], ALU.mult).then_inc(gated_ready, 1)
            for t in range(2):
                dve.wait_ge(h_hi_ready, 2 * c + t + 1)
                dve.tensor_tensor(h_lo[n][:, side(t), :], gated[:, side(t), :], f(h_hi[n][:, side(t), :]), ALU.subtract).then_inc(h_lo_ready, 1)

        over_chunks(dve, chunks, chunk)
        for q in range(NB // 2):
            if q == NB // 4:
                next_moments(dve, 0)
            dve.wait_ge(used, chunks + q)
            two = m.bank[4 + q][:, :].rearrange("p (j n) -> p j n", j=2)
            if not experts:
                m.step(dve.tensor_tensor(summed[:, 2 * q:2 * q + 2, :], two, out_scale[:, :].unsqueeze(1).broadcast_to((P, 2, D)), ALU.mult))
                m.wait_steps(dve)
                two = summed[:, 2 * q:2 * q + 2, :]
            dve.scalar_tensor_tensor(m.X[:, 2 * q:2 * q + 2, :], two, gate, m.X[:, 2 * q:2 * q + 2, :], ALU.mult, ALU.add).then_inc(m.x_done, 2)
        next_head(dve)

    def tensor(pe):
        pe.wait_ge(m.x_done, m.x_at(stage, 0))
        if experts:
            pe.wait_ge(small_parts, 4)
        for g in range(NG):
            xt.tensor(pe, g, lambda j: m.xn_all[:, G * g + j, :])
            if experts:
                pe.wait_ge(xt.lo_ready, xt.lo_at(g + 1))
                for j in range(G):
                    for c in range(KC):
                        mm = split_matmul(pe, m.bank[2 + g][:, j * E:(j + 1) * E], (m.xt_hi[:, c, G * g + j, :], m.xt_lo[:, c, G * g + j, :]),
                                          (cen_hi[:, c, :], cen_lo[:, c, :]), c == 0, c == KC - 1)
                mm.then_inc(routed, 1)

        def gates_by_expert():
            pe.wait_ge(gates_lo, 1)
            for g in range(NG):
                for j in range(G):
                    mm = pe.transpose(m.bank[2 + g][0:2 * GE, j * P:(j + 1) * P], f(parts[:, G * g + j, :, :]).rearrange("p k e -> p (k e)"), m.ident)
                mm.then_inc(turned, 1)
            pe.wait_ge(gates_t_ready, NG)
            for b in range(NB):
                pe.matmul(acc(b), gates_t[:, b, :], b2_hi[:, :], start=b % 2 == 0, stop=False, skip_group_check=True)
                pe.matmul(acc(b), gates_t[:, b, :], b2_lo[:, :], start=False, stop=False, skip_group_check=True)

        def hidden_products(n, t, half):
            for k in range(KC):
                w = slice((KC * half + k) * P, (KC * half + k + 1) * P)
                mm = split_matmul(pe, m.bank[2 * half + t][:, :], (hi[n][:, w], lo[n][:, w]), (m.xt_hi[:, k, side(t), :], m.xt_lo[:, k, side(t), :]), k == 0, k == KC - 1)
            mm.then_inc(u_raw if half else h_raw, 1)

        def spread_gates(c, n, t):
            after(pe, gated_ready, 2 * (c - 1) + t + 1)
            pe.matmul(m.bank[2 + t][:, :], hi[n][0:2 * GE, KC * P:(KC + 1) * P], gates_t[:, side(t), :], start=True, stop=True).then_inc(u_raw, 1)

        def first_products(c, n):
            pe.wait_ge(in_lo, c + 1)
            for t in range(2):
                after(pe, h_ready if experts else gated_ready, 2 * (c - 1) + t + 1)
                hidden_products(n, t, 0)
                if not experts:
                    after(pe, u_ready, 2 * (c - 1) + t + 1)
                    hidden_products(n, t, 1)
                elif not is_first(c):
                    spread_gates(c, n, t)
            if experts and is_first(c):
                gates_by_expert()
                for t in range(2):
                    spread_gates(c, n, t)

        def second_products(c, n):
            pe.wait_ge(out_lo, c + 1)
            for b in range(NB):
                if b % G == 0:
                    pe.wait_ge(h_lo_ready, 2 * c + b // G + 1)
                for part, (x, w) in enumerate(((h_lo, hi), (h_hi, lo), (h_hi, hi))):
                    start = not experts and is_first(c) and part == 0 and b % 2 == 0
                    mm = pe.matmul(acc(b), x[n][:, b, :], w[n][:, IN:COLS], start=start, stop=is_last(c) and part == 2, skip_group_check=True)
                if is_last(c) and b % 2:
                    mm.then_inc(used, 1)
            if not is_last(c):
                mm.then_inc(used, 1)

        def chunk(c, n):
            first_products(c, n)
            if not is_first(c):
                second_products(c - 1, 1 - n)

        pe.wait_ge(xt.lo_ready, xt.lo_at(NG))
        over_chunks(pe, chunks, chunk)
        second_products(chunks - 1, (chunks - 1) % 2)

    return {"load": load, "moments": norm.moments, "head": head, "sync": sync, "gpsimd": gpsimd, "scalar": scalar, "vector": vector, "tensor": tensor}


def l2_attention(m, stage):
    NEG = -1e30
    s = lambda x: m.sem(f"l2a_{x}")
    norm = Norm(m, stage)
    mask_raw = m.sb("l2a_mask_raw", [P, NB, P], U8)
    mask = m.work([P, NB, P])
    below = m.work([P, NB, P])
    valid = m.sb("l2a_valid", [P, NB])
    valid_tg = m.sb("l2a_valid_tg", [P, NB])
    per_group = lambda shape: [m.work(shape) for _ in range(NG)]
    xn = [m.xn, m.work([P, G, D])]
    xt = per_group([P, KC, G, P])
    kept = per_group([P, G, P])
    masked = per_group([P, G, P])
    top = per_group([P, G])
    neg_top = per_group([P, G])
    expd = per_group([P, G, P])
    total = per_group([P, G])
    inv = per_group([P, G])
    weight = per_group([P, G])
    probs_t = per_group([P, G, P])
    mask_in, mask_ready = s("mask_in"), s("mask")
    xt_raw, xt_ready, scored, neg_ready = s("xt_raw"), s("xt"), s("scored"), s("neg")
    exp_ready, turned, probs_ready, out_ready = s("exp"), s("turned"), s("probs"), s("out")
    wide = lambda bank: bank[:, :].rearrange("p (j n) -> p j n", j=G)

    def load(sp):
        sp.dma_start(mask_raw[:, :, :], m.dram["l2a_mask"].rearrange("a (b n) -> a b n", b=NB).broadcast_to((P, NB, P))).then_inc(mask_in, 16)

    def gpsimd(pool):
        norm.gpsimd(pool, 0)
        norm.gpsimd(pool, 1)
        pool.wait_ge(mask_ready, 1)
        pool.tensor_scalar(below[:, :, :], mask[:, :, :], -1.0, -NEG, ALU.add, ALU.mult).then_inc(mask_ready, 1)

    def scalar(act):
        act.wait_ge(norm.xn, norm.xn_at(G))
        act.wait_ge(mask_in, 16)
        act.activation(mask[:, :, :], mask_raw[:, :, :], ACT.Copy).then_inc(mask_ready, 1)
        for g in range(NG):
            act.wait_ge(xt_raw, g + 1)
            for c in range(KC):
                act.activation(xt[g][:, c, :, :], wide(m.bank[c]), ACT.Copy).then_inc(xt_ready, 1)
        for g in range(NG):
            act.wait_ge(neg_ready, g + 1)
            for j in range(G):
                act.activation(expd[g][:, j, :], masked[g][:, j, :], ACT.Exp, bias=neg_top[g][:, j:j + 1], accum_out=total[g][:, j:j + 1]).then_inc(exp_ready, 1)
            act.wait_ge(turned, g + 1)
            act.activation(probs_t[g][:, :, :], wide(m.bank[3]), ACT.Copy).then_inc(probs_ready, 1)

    def head(dve):
        norm.scale(dve, 0, lambda j: xn[0][:, j, :])

    def vector(dve, next_moments, next_head):
        norm.vector(dve, 1, lambda j: xn[1][:, j, :])
        dve.wait_ge(mask_ready, 1)
        m.step(dve.reduce_max(valid[:, :], mask[:, :, :], AX_X))
        m.wait_steps(dve)
        m.step(dve.tensor_scalar(valid_tg[:, :], valid[:, :], m.tg[:, 2:3], None, ALU.mult))
        for g in range(NG):
            dve.wait_ge(scored, g + 1)
            dve.wait_ge(mask_ready, 2)
            m.step(dve.scalar_tensor_tensor(kept[g][:, :, :], wide(m.bank[2]), 1.0 / 16.0, mask[:, G * g:G * g + G, :], ALU.mult, ALU.mult))
            m.wait_steps(dve)
            m.step(dve.tensor_tensor(masked[g][:, :, :], kept[g][:, :, :], below[:, G * g:G * g + G, :], ALU.add))
            m.wait_steps(dve)
            m.step(dve.reduce_max(top[g][:, :], masked[g][:, :, :], AX_X))
            m.wait_steps(dve)
            dve.tensor_scalar(neg_top[g][:, :], top[g][:, :], -1.0, None, ALU.mult).then_inc(neg_ready, 1)
        for g in range(NG):
            if g == NG - 1:
                next_moments(dve, 0)
            dve.wait_ge(exp_ready, G * g + G)
            m.step(dve.reciprocal(inv[g][:, :], total[g][:, :]))
            m.wait_steps(dve)
            m.step(dve.tensor_tensor(weight[g][:, :], inv[g][:, :], valid_tg[:, G * g:G * g + G], ALU.mult))
            m.wait_steps(dve)
            if g == NG - 1:
                next_head(dve)
            for j in range(G):
                b = G * g + j
                dve.wait_ge(out_ready, b + 1)
                dve.scalar_tensor_tensor(m.X[:, b, :], m.bank[4 + j][:, 0:D], weight[g][:, j:j + 1], m.X[:, b, :], ALU.mult, ALU.add).then_inc(m.x_done, 1)

    def tensor(pe):
        pe.wait_ge(m.ctx_in, 16)
        pe.wait_ge(m.cn_in, 16)
        for g in range(NG):
            pe.wait_ge(norm.xn, norm.xn_at(G * g + G))
            after(pe, xt_ready, KC * g)
            for c in range(KC):
                for j in range(G):
                    mm = pe.transpose(m.bank[c][:, j * P:(j + 1) * P], xn[g][:, j, c * P:(c + 1) * P], m.ident)
            mm.then_inc(xt_raw, 1)
            pe.wait_ge(xt_ready, KC * g + KC)
            after(pe, neg_ready, g)
            for j in range(G):
                for c in range(KC):
                    mm = pe.matmul(m.bank[2][:, j * P:(j + 1) * P], xt[g][:, c, j, :], m.CT[:, c, G * g + j, :], start=c == 0, stop=c == KC - 1)
            mm.then_inc(scored, 1)
        for g in range(NG):
            after(pe, probs_ready, g)
            for j in range(G):
                pe.wait_ge(exp_ready, G * g + j + 1)
                mm = pe.transpose(m.bank[3][:, j * P:(j + 1) * P], expd[g][:, j, :], m.ident)
            mm.then_inc(turned, 1)
            pe.wait_ge(probs_ready, g + 1)
            for j in range(G):
                if g:
                    pe.wait_ge(m.x_done, m.x_at(stage, G * (g - 1) + j + 1))
                pe.matmul(m.bank[4 + j][:, 0:D], probs_t[g][:, j, :], m.CN[:, G * g + j, :], start=True, stop=True).then_inc(out_ready, 1)

    return {"load": load, "moments": norm.moments, "head": head, "gpsimd": gpsimd, "scalar": scalar, "vector": vector, "tensor": tensor}


def l3_attention(m, stage):
    T = P + 1
    NEG = -1e38
    s = lambda x: m.sem(f"l3a_{x}")
    norm = Norm(m, stage)
    wu = m.sb("l3a_wu", [P, KC, 2])
    full = lambda: [m.work([P, NB, T]) for _ in range(KC)]
    plain = lambda: [m.work([P, NB, P]) for _ in range(KC)]
    k, decay, o, fade, enter, entered = full(), full(), full(), full(), full(), full()
    p_sum, q_sum = k, decay
    lead, a, e = plain(), plain(), plain()
    wu_in, edges, decay_ready, xt_raw, k_ready = s("wu_in"), s("edges"), s("decay"), s("xt_raw"), s("k")
    diffs, pool_diffs, exps, entered_ready = s("diffs"), s("pool_diffs"), s("exps"), s("entered")
    p_ready, pool_terms, y_ready, turned = s("p"), s("pool_terms"), s("y"), s("turned")
    PIECES = NG * KC
    of = lambda t, n: t[n % KC][:, n // KC * G:n // KC * G + G, :]
    row = lambda t, n: of(t, n).rearrange("p b t -> p (b t)")
    past = lambda t, n: of(t, n)[:, :, 0:P]
    here = lambda t, n: of(t, n)[:, :, 1:T]

    def load(sp):
        sp.dma_start(wu[:, :, :], m.dram["l3a_wu"].rearrange("p (c k) -> p c k", c=KC)).then_inc(wu_in, 16)

    def in_turn(front, back):
        for n in range(PIECES + 1):
            if n < PIECES:
                front(n)
            if n:
                back(n - 1)

    def gpsimd(pool):
        norm.gpsimd(pool, 0)
        pool.wait_ge(m.x_done, m.x_at(stage, 0))
        for c in range(KC):
            pool.memset(k[c][:, :, 0:1], NEG).then_inc(edges, 1)
            pool.memset(decay[c][:, :, 0:1], NEG).then_inc(edges, 1)
            pool.memset(fade[c][:, :, 0:1], 0.0).then_inc(edges, 1)
            pool.memset(enter[c][:, :, 0:1], 0.0).then_inc(edges, 1)
            pool.memset(entered[c][:, :, 0:1], 0.0).then_inc(edges, 1)
            pool.memset(o[c][:, :, :], 0.0).then_inc(edges, 1)
        norm.gpsimd(pool, 1)

        def front(n):
            pool.wait_ge(diffs, 3 * n + 1)
            pool.tensor_tensor(here(enter, n), here(k, n), here(o, n), ALU.subtract).then_inc(pool_diffs, 1)
            pool.wait_ge(diffs, 3 * n + 2)
            pool.tensor_tensor(of(a, n), past(o, n), of(lead, n), ALU.subtract).then_inc(pool_diffs, 1)

        def weighted(n):
            v = m.CT[:, n % KC, n // KC * G:n // KC * G + G, :]
            pool.wait_ge(exps, 4 * n + 2)
            pool.tensor_tensor(here(entered, n), here(enter, n), v, ALU.mult).then_inc(entered_ready, 1)
            pool.wait_ge(exps, 4 * n + 4)
            pool.tensor_tensor(of(lead, n), of(e, n), v, ALU.mult).then_inc(pool_terms, 1)

        def back(n):
            pool.wait_ge(p_ready, n + 1)
            pool.tensor_tensor(here(fade, n), of(a, n), past(p_sum, n), ALU.mult).then_inc(pool_terms, 1)
            pool.wait_ge(pool_terms, 3 * n + 2)
            pool.tensor_tensor(here(fade, n), here(fade, n), of(lead, n), ALU.add).then_inc(pool_terms, 1)

        for n in range(PIECES + 1):
            if n < PIECES:
                front(n)
            if n:
                back(n - 1)
            if n < PIECES:
                weighted(n)

    def scalar(act):
        act.wait_ge(norm.xn, norm.xn_at(G))
        act.wait_ge(wu_in, 16)
        act.wait_ge(edges, 6 * KC)
        for c in range(KC):
            act.activation(decay[c][:, :, 1:T], o[c][:, :, 1:T], ACT.Identity, bias=wu[:, c, 0:1]).then_inc(decay_ready, 1)
        for g in range(NG):
            act.wait_ge(xt_raw, g + 1)
            for c in range(KC):
                act.activation(k[c][:, G * g:G * g + G, 1:T], m.bank[2 * g + c][:, :].rearrange("p (j n) -> p j n", j=G), ACT.Copy).then_inc(k_ready, 1)
        for n in range(PIECES):
            for ready, count, x in ((diffs, 3 * n + 1, here(fade, n)), (pool_diffs, 2 * n + 1, here(enter, n)),
                                    (pool_diffs, 2 * n + 2, of(a, n)), (diffs, 3 * n + 3, of(e, n))):
                act.wait_ge(ready, count)
                act.activation(x, x, ACT.Exp).then_inc(exps, 1)

    def head(dve):
        norm.scale(dve, 0, lambda j: m.xn_all[:, j, :])

    def vector(dve, next_moments, next_head):
        norm.vector(dve, 1, lambda j: m.xn_all[:, G + j, :])
        dve.wait_ge(decay_ready, KC)
        dve.wait_ge(wu_in, 16)

        def front(n):
            w, u = wu[:, n % KC, 0:1], wu[:, n % KC, 1:2]
            dve.wait_ge(k_ready, n + 1)
            m.step(dve.tensor_tensor_scan(row(o, n), row(decay, n), row(k, n), NEG, ALU.add, ALU.max))
            m.wait_steps(dve)
            dve.scalar_tensor_tensor(here(fade, n), past(o, n), w, here(o, n), ALU.add, ALU.subtract).then_inc(diffs, 1)
            dve.scalar_tensor_tensor(of(lead, n), here(k, n), u, past(o, n), ALU.add, ALU.max).then_inc(diffs, 1)
            dve.wait_ge(diffs, 3 * n + 2)
            dve.scalar_tensor_tensor(of(e, n), here(k, n), u, of(lead, n), ALU.add, ALU.subtract).then_inc(diffs, 1)

        def back(n):
            dve.wait_ge(exps, 4 * n + 2)
            m.step(dve.tensor_tensor_scan(row(q_sum, n), row(fade, n), row(enter, n), 0.0, ALU.mult, ALU.add))
            dve.wait_ge(entered_ready, n + 1)
            dve.wait_ge(exps, 4 * n + 4)
            dve.tensor_tensor_scan(row(p_sum, n), row(fade, n), row(entered, n), 0.0, ALU.mult, ALU.add).then_inc(p_ready, 1)
            den = here(enter, n)
            m.wait_steps(dve)
            m.step(dve.tensor_tensor(den, of(a, n), past(q_sum, n), ALU.mult))
            m.wait_steps(dve)
            m.step(dve.tensor_tensor(den, den, of(e, n), ALU.add))
            m.wait_steps(dve)
            if n == PIECES - 1:
                next_moments(dve, 0)
            m.step(dve.reciprocal(den, den))
            m.wait_steps(dve)
            dve.wait_ge(pool_terms, 3 * n + 3)
            dve.tensor_tensor(of(a, n), here(fade, n), den, ALU.mult).then_inc(y_ready, 1)
            if n % KC == 0 and n:
                add(n // KC - 1)

        def add(g):
            for q in range(G // 2 * g, G // 2 * (g + 1)):
                dve.wait_ge(turned, q + 1)
                dve.scalar_tensor_tensor(m.X[:, 2 * q:2 * q + 2, :], m.bank[4 + q][:, :].rearrange("p (j n) -> p j n", j=2), m.tg[:, 3:4],
                                         m.X[:, 2 * q:2 * q + 2, :], ALU.mult, ALU.add).then_inc(m.x_done, 2)

        in_turn(front, back)
        next_head(dve)
        add(NG - 1)

    def tensor(pe):
        for g in range(NG):
            pe.wait_ge(norm.xn, norm.xn_at(G * g + G))
            for c in range(KC):
                for j in range(G):
                    mm = pe.transpose(m.bank[2 * g + c][:, j * P:(j + 1) * P], m.xn_all[:, G * g + j, c * P:(c + 1) * P], m.ident)
            mm.then_inc(xt_raw, 1)
        for q in range(NB // 2):
            pe.wait_ge(y_ready, KC * (2 * q // G + 1))
            for j in range(2):
                for c in range(KC):
                    mm = pe.transpose(m.bank[4 + q][:, j * D + c * P:j * D + (c + 1) * P], a[c][:, 2 * q + j, :], m.ident)
            mm.then_inc(turned, 1)

    return {"load": load, "moments": norm.moments, "head": head, "gpsimd": gpsimd, "scalar": scalar, "vector": vector, "tensor": tensor}


def program(nc, dram, out):
    with ExitStack() as ctx:
        m = Machine(nc, ctx, dram)
        builders = [
            l0_attention,
            lambda m, n: adapters(m, n, "l0f", True),
            l1_attention,
            lambda m, n: feed_forward(m, n, "l1f", dram["l1f_w"].shape[0], True),
            l2_attention,
            lambda m, n: feed_forward(m, n, "l2f", dram["l2f_w"].shape[0], False),
            l3_attention,
            lambda m, n: adapters(m, n, "l3f", False),
        ]
        stages = []
        for n, build in enumerate(builders[:STAGES]):
            m.used = {"f": 0, "r": 0}
            stages.append(build(m, n))
        stored = m.sem("stored")
        block = ctx.enter_context(nc.Block())

        @block.sync
        def _(sp):
            for stage in stages:
                stage["load"](sp)
            for stage in stages:
                if "sync" in stage:
                    stage["sync"](sp)
            y = out.rearrange("b s d -> s b d")
            for g in range(NG):
                sp.wait_ge(m.x_done, m.x_at(len(stages) - 1, G * g + G))
                sp.dma_start(y[:, G * g:G * g + G, :], m.X[:, G * g:G * g + G, :]).then_inc(stored, 16)
            sp.wait_ge(stored, 16 * NG)

        @block.gpsimd
        def _(pool):
            for stage in stages:
                stage["gpsimd"](pool)

        @block.scalar
        def _(act):
            for stage in stages:
                stage["scalar"](act)

        @block.vector
        def _(dve):
            for n, stage in enumerate(stages):
                following = stages[n + 1] if n + 1 < len(stages) else {"moments": lambda dve, g: None, "head": lambda dve: None}
                stage["vector"](dve, following["moments"], following["head"])

        @block.tensor
        def _(pe):
            for stage in stages:
                stage["tensor"](pe)


def widths_on_partitions(w):
    w = np.asarray(w)
    return np.ascontiguousarray(w.reshape(-1, P, w.shape[1]).transpose(1, 0, 2).reshape(P, -1))


def by_rank(w):
    return np.asarray(w).transpose(1, 0, 2).reshape(D, -1)


def constants():
    rows = np.arange(P)
    c = np.zeros((P, CONST_COLS), np.float32)
    c[:, 0:P] = np.eye(P)
    c[:, P:2 * P] = rows[:, None] // 16 == rows[None, :] // 16
    c[:, 2 * P:2 * P + 8] = rows[:, None] // 16 == np.arange(8)[None, :]
    c[:, 2 * P + 8:2 * P + 16] = -0.5
    c[:, 2 * P + 16] = rows % 64 == 48
    return c


def stack_selectors():
    sel = np.zeros((P, 4, 4, P), np.float32)
    for kind, places in enumerate(((0, 2), (1,), (0, 1), (2,))):
        for pair in range(4):
            for a in range(2):
                for t in places:
                    for d in range(16):
                        sel[32 * pair + 16 * a + d, kind, pair, 64 * a + 16 * t + d] = 1
    return sel.reshape(P, -1)


def output_selectors():
    sel = np.zeros((P, 2, 2, P), np.float32)
    for h in range(8):
        for d in range(16):
            for kind in range(2):
                sel[32 * (h // 2) + 16 * kind + d, kind, h % 2, 16 * h + d] = 1
    return sel.reshape(P, -1)


def padded(w, n, axis):
    w = np.asarray(w)
    fill = list(w.shape)
    fill[axis] = n - w.shape[axis]
    return np.concatenate([w, np.zeros(fill, w.dtype)], axis=axis)


def expert_chunks(a):
    w1 = np.concatenate([np.asarray(a["L1_ffn_routed_w1"]), np.asarray(a["L1_ffn_shared_w1"])])
    w2 = np.concatenate([np.asarray(a["L1_ffn_routed_w2"]), np.asarray(a["L1_ffn_shared_w2"])])
    b1 = np.concatenate([np.asarray(a["L1_ffn_routed_b1"]), np.asarray(a["L1_ffn_shared_b1"])])
    b2 = np.concatenate([np.asarray(a["L1_ffn_routed_b2"]), np.asarray(a["L1_ffn_shared_b2"])])
    n, _, f = w1.shape
    chunks = -(-n * f // P)
    w1 = padded(w1.transpose(1, 0, 2).reshape(D, n * f), chunks * P, 1).reshape(KC, P, chunks, P)
    w2 = padded(w2.reshape(n * f, D), chunks * P, 0).reshape(chunks, P, D)
    expert = np.arange(chunks * P) // f
    sel = np.zeros((P, chunks * P), np.float32)
    for part in range(2):
        sel[part * n:(part + 1) * n] = expert[None, :] == np.arange(n)[:, None]
    b1 = padded(b1.reshape(-1), chunks * P, 0).reshape(chunks, P, 1)
    blob = np.concatenate([w1[0].transpose(1, 0, 2), w1[1].transpose(1, 0, 2), sel.reshape(P, chunks, P).transpose(1, 0, 2), w2, b1], axis=2)
    return blob, np.concatenate([b2, b2])


def swiglu_chunks(a):
    gate, up, down = (np.asarray(a[f"L2_ffn_{n}_w"]) for n in ("gate", "up", "down"))
    chunks = -(-gate.shape[0] // P)
    first = [padded(w, chunks * P, 0).reshape(chunks, P, KC, P).transpose(0, 3, 2, 1).reshape(chunks, P, KC * P) for w in (gate, up)]
    second = padded(down, chunks * P, 1).T.reshape(chunks, P, D)
    scales = np.stack([padded(a[f"L2_ffn_{n}_s"], chunks * P, 0).reshape(chunks, P).T for n in ("gate", "up")], axis=1)
    return np.concatenate(first + [second], axis=2), scales.reshape(P, -1)


def layouts(a):
    row = lambda v: np.asarray(v).reshape(1, -1)
    l1f_w, l1f_b2 = expert_chunks(a)
    l2f_w, l2f_scales = swiglu_chunks(a)
    return {
        "x": a["x"],
        "ctx": a["ctx_2048"],
        "ctx_t": np.ascontiguousarray(np.asarray(a["ctx_2048"]).transpose(2, 0, 1).reshape(KC, P, NB, P).transpose(1, 0, 2, 3).reshape(P, -1)),
        "const": constants(),
        "gates": row(np.concatenate([a["g_xattn"], a["g_ffn"]])),
        "l0a_w": widths_on_partitions(np.concatenate([np.asarray(a["L0_xattn_Wkv"]).T, np.asarray(a["L0_xattn_Wq"]).T,
                                                      np.asarray(a["L0_xattn_Wg"]).T, np.asarray(a["L0_xattn_Wo"]).T], axis=1)),
        "l0a_bg": row(a["L0_xattn_bg"]),
        "l0f_w": widths_on_partitions(np.concatenate([by_rank(a["L0_ffn_Wd"]), np.asarray(a["L0_ffn_Wr"])], axis=1)),
        "l0f_up": np.asarray(a["L0_ffn_Wu"]).reshape(P, D),
        "l0f_bias": row(np.concatenate([np.asarray(a["L0_ffn_bd"]).reshape(-1), np.asarray(a["L0_ffn_br"])])),
        "l0f_up_bias": a["L0_ffn_bu"],
        "l1a_sel": stack_selectors(),
        "l1a_out_sel": output_selectors(),
        "l1a_gamma": row(a["L1_xattn_gamma"]),
        "l1f_w": l1f_w,
        "l1f_b2": l1f_b2,
        "l1f_cen": widths_on_partitions(np.asarray(a["L1_ffn_centroids"]).T),
        "l1f_bias": row(a["L1_ffn_bias"]),
        "l2a_mask": row(a["mask_BxS2_bk0"]),
        "l2f_w": l2f_w,
        "l2f_scales": l2f_scales,
        "l2f_out_scale": row(a["L2_ffn_down_s"]),
        "l3a_wu": widths_on_partitions(np.stack([np.asarray(a["L3_xattn_w"]), np.asarray(a["L3_xattn_u"])], axis=1)),
        "l3f_w": widths_on_partitions(np.concatenate([by_rank(a["L3_ffn_experts_down"]), np.asarray(a["L3_ffn_router_w"]).T], axis=1)),
        "l3f_up": np.asarray(a["L3_ffn_experts_up"]).reshape(P, D),
    }


def kernel(**inputs):
    import concourse.bacc as bacc
    from concourse.bass_utils import run_bass_kernel_spmd

    arrays = {name: np.ascontiguousarray(v) for name, v in layouts(inputs).items()}
    nc = bacc.Bacc("TRN2", target_bir_lowering=False, num_devices=1)
    dram = {name: nc.dram_tensor(f"in_{name}", v.shape, mybir.dt.from_np(v.dtype), kind="ExternalInput").ap() for name, v in arrays.items()}
    out = nc.dram_tensor("out_x", (NB, P, D), F32, kind="ExternalOutput").ap()
    program(nc, dram, out)
    got = run_bass_kernel_spmd(nc, [{f"in_{name}": v for name, v in arrays.items()}], core_ids=[0])
    return got.results[0]["out_x"]
```
